# Optimizing a Trainium2 kernel written in Bass

```python
import numpy as np
import jax
import jax.numpy as jnp

def _softmax(x, axis=-1):
    return jax.nn.softmax(x, axis=axis)

def _gelu(x):
    return jax.nn.gelu(x, approximate=True)

def _silu(x):
    return jax.nn.silu(x)

def _sigmoid(x):
    return jax.nn.sigmoid(x)

def _layernorm(x, axis=-1, eps=1e-05):
    m = jnp.mean(x, axis=axis, keepdims=True)
    v = jnp.var(x, axis=axis, keepdims=True)
    return (x - m) / jnp.sqrt(v + eps)

def _scatter_add(tgt, idx, src, axis=0):
    return tgt.at[idx].add(src)

def _segment_sum(src, seg, n):
    return jax.ops.segment_sum(src, seg, n)
kernel_name = 'mk_gnn_resnorm_d4_gnn_r16_126f6d'

def setup_inputs(seed: int=0):
    np.random.seed(seed)
    _w = jnp.asarray

    def _rec_inputs():
        import jax
        import jax.numpy as jnp
        _gk = jax.random.key(seed)
        x = -0.0003713 + 1 * jax.random.normal(jax.random.fold_in(_gk, 1), (6250, 128), jnp.float32)
        src = jax.random.randint(jax.random.fold_in(_gk, 2), (100000,), 0, 6250, jnp.int32)
        dst = jnp.minimum((6250 * jax.random.uniform(jax.random.fold_in(_gk, 3), (100000,)) ** 2.0).astype(jnp.int32), 99999)
        _o = jnp.argsort(dst, stable=True)
        src = src[_o]
        dst = dst[_o]
        return (x, src, dst)
    x, src, dst = _rec_inputs()

    def _L0_gnn_setup():
        import jax, jax.numpy as jnp
        import numpy as np
        N_NODES = 6250
        N_EDGES = 100000
        D_MODEL = 128
        N_HEADS = 8
        D_HEAD = D_MODEL // N_HEADS

        def _batch_norm(x, w, b, eps=1e-05):
            m = x.mean(axis=0)
            v = x.var(axis=0)
            return (x - m) * jax.lax.rsqrt(v + eps) * w + b
        key = jax.random.key(seed)
        ks = jax.random.split(key, 12)
        s = 0.05
        inp = {'h': jax.random.normal(ks[0], (N_NODES, D_MODEL), dtype=jnp.float32), 'src': jax.random.randint(ks[1], (N_EDGES,), 0, N_NODES, dtype=jnp.int32), 'dst': jax.random.randint(ks[2], (N_EDGES,), 0, N_NODES, dtype=jnp.int32), 'Wq': jax.random.normal(ks[3], (D_MODEL, D_MODEL), dtype=jnp.float32) * s, 'Wk': jax.random.normal(ks[4], (D_MODEL, D_MODEL), dtype=jnp.float32) * s, 'Wv': jax.random.normal(ks[5], (D_MODEL, D_MODEL), dtype=jnp.float32) * s, 'Wo': jax.random.normal(ks[6], (D_MODEL, D_MODEL), dtype=jnp.float32) * s, 'bo': jnp.zeros((D_MODEL,), dtype=jnp.float32), 'W1': jax.random.normal(ks[7], (2 * D_MODEL, D_MODEL), dtype=jnp.float32) * s, 'b1': jnp.zeros((2 * D_MODEL,), dtype=jnp.float32), 'W2': jax.random.normal(ks[8], (D_MODEL, 2 * D_MODEL), dtype=jnp.float32) * s, 'b2': jnp.zeros((D_MODEL,), dtype=jnp.float32), 'bn1_w': jnp.ones((D_MODEL,), dtype=jnp.float32), 'bn1_b': jnp.zeros((D_MODEL,), dtype=jnp.float32), 'bn2_w': jnp.ones((D_MODEL,), dtype=jnp.float32), 'bn2_b': jnp.zeros((D_MODEL,), dtype=jnp.float32)}
        return inp
    _L0_gnn_all = _L0_gnn_setup()
    _L0_gnn_in = {k: v for k, v in _L0_gnn_all.items() if k in ('Wq', 'Wk', 'Wv', 'Wo', 'bo', 'W1', 'b1', 'W2', 'b2', 'bn1_w', 'bn1_b', 'bn2_w', 'bn2_b')}
    del _L0_gnn_all

    def _L1_gnn_setup():
        import jax, jax.numpy as jnp
        import numpy as np
        N = 3125
        E = 50000
        IN_DIM = 128
        HEADS = 4
        OUT_C = 32
        HC = HEADS * OUT_C
        key = jax.random.key(seed)
        ks = jax.random.split(key, 12)
        x = jax.random.normal(ks[0], (N, IN_DIM), dtype=jnp.float32)
        edge_index = jax.random.randint(ks[1], (2, E), 0, N, dtype=jnp.int64)
        s = 1.0 / np.sqrt(IN_DIM)
        Wq = jax.random.normal(ks[2], (IN_DIM, HC), dtype=jnp.float32) * s
        bq = jnp.zeros((HC,), dtype=jnp.float32)
        Wk = jax.random.normal(ks[3], (IN_DIM, HC), dtype=jnp.float32) * s
        bk = jnp.zeros((HC,), dtype=jnp.float32)
        Wv = jax.random.normal(ks[4], (IN_DIM, HC), dtype=jnp.float32) * s
        bv = jnp.zeros((HC,), dtype=jnp.float32)
        Wskip = jax.random.normal(ks[5], (IN_DIM, HC), dtype=jnp.float32) * s
        bskip = jnp.zeros((HC,), dtype=jnp.float32)
        Wbeta = jax.random.normal(ks[6], (3 * HC, 1), dtype=jnp.float32) * (1.0 / np.sqrt(3 * HC))
        return {'x': x, 'edge_index': edge_index, 'Wq': Wq, 'bq': bq, 'Wk': Wk, 'bk': bk, 'Wv': Wv, 'bv': bv, 'Wskip': Wskip, 'bskip': bskip, 'Wbeta': Wbeta}
    _L1_gnn_all = _L1_gnn_setup()
    _L1_gnn_in = {k: v for k, v in _L1_gnn_all.items() if k in ('Wq', 'bq', 'Wk', 'bk', 'Wv', 'bv', 'Wskip', 'bskip', 'Wbeta')}
    del _L1_gnn_all

    def _L2_gnn_setup():
        import jax, jax.numpy as jnp
        import numpy as np
        N_NODES = 3125
        N_EDGES = 50000
        IN_DIM = 128
        HID = 100

        def gcn_conv(x, edge_index, W, b, n):
            row, col = (edge_index[0], edge_index[1])
            loop = jnp.arange(n, dtype=row.dtype)
            row = jnp.concatenate([row, loop])
            col = jnp.concatenate([col, loop])
            deg = jax.ops.segment_sum(jnp.ones(row.shape, x.dtype), col, num_segments=n)
            dinv = jnp.where(deg > 0, jax.lax.rsqrt(deg), 0.0)
            norm = dinv[row] * dinv[col]
            h = x @ W
            msg = h[row] * norm[:, None]
            out = jax.ops.segment_sum(msg, col, num_segments=n)
            return out + b
        key = jax.random.key(seed)
        ks = jax.random.split(key, 10)
        x = jax.random.normal(ks[0], (N_NODES, IN_DIM), dtype=jnp.float32)
        edge_index = jax.random.randint(ks[1], (2, N_EDGES), 0, N_NODES, dtype=jnp.int32)

        def glorot(k, fan_in, fan_out):
            s = jnp.sqrt(6.0 / (fan_in + fan_out))
            return jax.random.uniform(k, (fan_in, fan_out), jnp.float32, -s, s)
        return {'x': x, 'edge_index': edge_index, 'W1': glorot(ks[2], IN_DIM, HID), 'b1': jnp.zeros((HID,), jnp.float32), 'W2': glorot(ks[3], HID, HID), 'b2': jnp.zeros((HID,), jnp.float32), 'W3': glorot(ks[4], HID, HID), 'b3': jnp.zeros((HID,), jnp.float32), 'W4': glorot(ks[5], HID, IN_DIM), 'b4': jnp.zeros((IN_DIM,), jnp.float32)}
    _L2_gnn_all = _L2_gnn_setup()
    _L2_gnn_in = {k: v for k, v in _L2_gnn_all.items() if k in ('W1', 'b1', 'W2', 'b2', 'W3', 'b3', 'W4', 'b4')}
    del _L2_gnn_all

    def _L3_gnn_setup():
        import jax, jax.numpy as jnp
        import numpy as np
        N_NODES = 6250
        N_EDGES = 100000
        D_IN = 128
        D_HID = 256

        def _glorot(key, shape):
            lim = 1.0 / np.sqrt(shape[0])
            return jax.random.uniform(key, shape, jnp.float32, -lim, lim)

        def _gin_conv(x, src, dst, Wa, ba, Wb, bb):
            agg = jax.ops.segment_sum(x[src], dst, num_segments=x.shape[0])
            h = x + agg
            h = jax.nn.relu(h @ Wa + ba)
            return h @ Wb + bb
        key = jax.random.key(seed)
        ks = jax.random.split(key, 10)
        x = jax.random.normal(ks[0], (N_NODES, D_IN), jnp.float32)
        edge_index = jax.random.randint(ks[1], (2, N_EDGES), 0, N_NODES, jnp.int32)
        W1a = _glorot(ks[2], (D_IN, D_HID))
        b1a = jnp.zeros((D_HID,), jnp.float32)
        W1b = _glorot(ks[3], (D_HID, D_HID))
        b1b = jnp.zeros((D_HID,), jnp.float32)
        W2a = _glorot(ks[4], (D_HID, D_HID))
        b2a = jnp.zeros((D_HID,), jnp.float32)
        W2b = _glorot(ks[5], (D_HID, D_IN))
        b2b = jnp.zeros((D_IN,), jnp.float32)
        return dict(x=x, edge_index=edge_index, W1a=W1a, b1a=b1a, W1b=W1b, b1b=b1b, W2a=W2a, b2a=b2a, W2b=W2b, b2b=b2b)
    _L3_gnn_all = _L3_gnn_setup()
    _L3_gnn_in = {k: v for k, v in _L3_gnn_all.items() if k in ('W1a', 'b1a', 'W1b', 'b1b', 'W2a', 'b2a', 'W2b', 'b2b')}
    del _L3_gnn_all
    return {'x': x, 'src': src, 'dst': dst, 'L0_gnn_Wq': _L0_gnn_in['Wq'], 'L0_gnn_Wk': _L0_gnn_in['Wk'], 'L0_gnn_Wv': _L0_gnn_in['Wv'], 'L0_gnn_Wo': _L0_gnn_in['Wo'], 'L0_gnn_bo': _L0_gnn_in['bo'], 'L0_gnn_W1': _L0_gnn_in['W1'], 'L0_gnn_b1': _L0_gnn_in['b1'], 'L0_gnn_W2': _L0_gnn_in['W2'], 'L0_gnn_b2': _L0_gnn_in['b2'], 'L0_gnn_bn1_w': _L0_gnn_in['bn1_w'], 'L0_gnn_bn1_b': _L0_gnn_in['bn1_b'], 'L0_gnn_bn2_w': _L0_gnn_in['bn2_w'], 'L0_gnn_bn2_b': _L0_gnn_in['bn2_b'], 'L1_gnn_Wq': _L1_gnn_in['Wq'], 'L1_gnn_bq': _L1_gnn_in['bq'], 'L1_gnn_Wk': _L1_gnn_in['Wk'], 'L1_gnn_bk': _L1_gnn_in['bk'], 'L1_gnn_Wv': _L1_gnn_in['Wv'], 'L1_gnn_bv': _L1_gnn_in['bv'], 'L1_gnn_Wskip': _L1_gnn_in['Wskip'], 'L1_gnn_bskip': _L1_gnn_in['bskip'], 'L1_gnn_Wbeta': _L1_gnn_in['Wbeta'], 'L2_gnn_W1': _L2_gnn_in['W1'], 'L2_gnn_b1': _L2_gnn_in['b1'], 'L2_gnn_W2': _L2_gnn_in['W2'], 'L2_gnn_b2': _L2_gnn_in['b2'], 'L2_gnn_W3': _L2_gnn_in['W3'], 'L2_gnn_b3': _L2_gnn_in['b3'], 'L2_gnn_W4': _L2_gnn_in['W4'], 'L2_gnn_b4': _L2_gnn_in['b4'], 'L3_gnn_W1a': _L3_gnn_in['W1a'], 'L3_gnn_b1a': _L3_gnn_in['b1a'], 'L3_gnn_W1b': _L3_gnn_in['W1b'], 'L3_gnn_b1b': _L3_gnn_in['b1b'], 'L3_gnn_W2a': _L3_gnn_in['W2a'], 'L3_gnn_b2a': _L3_gnn_in['b2a'], 'L3_gnn_W2b': _L3_gnn_in['W2b'], 'L3_gnn_b2b': _L3_gnn_in['b2b']}

def reference(x, src, dst, L0_gnn_Wq, L0_gnn_Wk, L0_gnn_Wv, L0_gnn_Wo, L0_gnn_bo, L0_gnn_W1, L0_gnn_b1, L0_gnn_W2, L0_gnn_b2, L0_gnn_bn1_w, L0_gnn_bn1_b, L0_gnn_bn2_w, L0_gnn_bn2_b, L1_gnn_Wq, L1_gnn_bq, L1_gnn_Wk, L1_gnn_bk, L1_gnn_Wv, L1_gnn_bv, L1_gnn_Wskip, L1_gnn_bskip, L1_gnn_Wbeta, L2_gnn_W1, L2_gnn_b1, L2_gnn_W2, L2_gnn_b2, L2_gnn_W3, L2_gnn_b3, L2_gnn_W4, L2_gnn_b4, L3_gnn_W1a, L3_gnn_b1a, L3_gnn_W1b, L3_gnn_b1b, L3_gnn_W2a, L3_gnn_b2a, L3_gnn_W2b, L3_gnn_b2b):
    import jax
    import jax.numpy as jnp

    def _L0_gnn_ref(h, src, dst, Wq, Wk, Wv, Wo, bo, W1, b1, W2, b2, bn1_w, bn1_b, bn2_w, bn2_b):
        import jax, jax.numpy as jnp
        import numpy as np
        N_NODES = 6250
        N_EDGES = 100000
        D_MODEL = 128
        N_HEADS = 8
        D_HEAD = D_MODEL // N_HEADS

        def _batch_norm(x, w, b, eps=1e-05):
            m = x.mean(axis=0)
            v = x.var(axis=0)
            return (x - m) * jax.lax.rsqrt(v + eps) * w + b
        N = h.shape[0]
        Q = (h @ Wq.T).reshape(N, N_HEADS, D_HEAD)
        K = (h @ Wk.T).reshape(N, N_HEADS, D_HEAD)
        V = (h @ Wv.T).reshape(N, N_HEADS, D_HEAD)
        score = jnp.einsum('ehd,ehd->eh', K[src], Q[dst]) / np.sqrt(D_HEAD).astype(np.float32)
        s = jnp.exp(jnp.clip(score, -5.0, 5.0))[:, :, None]
        wV = jax.ops.segment_sum(V[src] * s, dst, num_segments=N)
        z = jax.ops.segment_sum(s, dst, num_segments=N)
        h_attn = (wV / (z + 1e-06)).reshape(N, D_MODEL)
        x = h_attn @ Wo.T + bo
        x = h + x
        x = _batch_norm(x, bn1_w, bn1_b)
        y = jax.nn.relu(x @ W1.T + b1) @ W2.T + b2
        y = x + y
        y = _batch_norm(y, bn2_w, bn2_b)
        return y

    def _L1_gnn_ref(x, edge_index, Wq, bq, Wk, bk, Wv, bv, Wskip, bskip, Wbeta):
        import jax, jax.numpy as jnp
        import numpy as np
        N = 3125
        E = 50000
        IN_DIM = 128
        HEADS = 4
        OUT_C = 32
        HC = HEADS * OUT_C
        n = x.shape[0]
        src = edge_index[0]
        dst = edge_index[1]
        q = (x @ Wq + bq).reshape(n, HEADS, OUT_C)
        k = (x @ Wk + bk).reshape(n, HEADS, OUT_C)
        v = (x @ Wv + bv).reshape(n, HEADS, OUT_C)
        score = jnp.einsum('ehc,ehc->eh', q[dst], k[src]) / jnp.sqrt(jnp.asarray(OUT_C, dtype=x.dtype))
        m = jax.ops.segment_max(score, dst, num_segments=n)
        m = jnp.where(jnp.isfinite(m), m, 0.0)
        p = jnp.exp(score - m[dst])
        denom = jax.ops.segment_sum(p, dst, num_segments=n)
        alpha = p / jnp.maximum(denom[dst], 1e-16)
        msg = v[src] * alpha[:, :, None]
        out = jax.ops.segment_sum(msg, dst, num_segments=n)
        out = out.reshape(n, HC)
        x_r = x @ Wskip + bskip
        beta = jax.nn.sigmoid(jnp.concatenate([out, x_r, out - x_r], axis=-1) @ Wbeta)
        return beta * x_r + (1.0 - beta) * out

    def _L2_gnn_ref(x, edge_index, W1, b1, W2, b2, W3, b3, W4, b4):
        import jax, jax.numpy as jnp
        import numpy as np
        N_NODES = 3125
        N_EDGES = 50000
        IN_DIM = 128
        HID = 100

        def gcn_conv(x, edge_index, W, b, n):
            row, col = (edge_index[0], edge_index[1])
            loop = jnp.arange(n, dtype=row.dtype)
            row = jnp.concatenate([row, loop])
            col = jnp.concatenate([col, loop])
            deg = jax.ops.segment_sum(jnp.ones(row.shape, x.dtype), col, num_segments=n)
            dinv = jnp.where(deg > 0, jax.lax.rsqrt(deg), 0.0)
            norm = dinv[row] * dinv[col]
            h = x @ W
            msg = h[row] * norm[:, None]
            out = jax.ops.segment_sum(msg, col, num_segments=n)
            return out + b
        n = x.shape[0]
        h = x.astype(jnp.float32)
        h = jax.nn.relu(gcn_conv(h, edge_index, W1, b1, n))
        h = jax.nn.relu(gcn_conv(h, edge_index, W2, b2, n))
        h = jax.nn.relu(gcn_conv(h, edge_index, W3, b3, n))
        h = jax.nn.relu(gcn_conv(h, edge_index, W4, b4, n))
        return h

    def _L3_gnn_ref(x, edge_index, W1a, b1a, W1b, b1b, W2a, b2a, W2b, b2b):
        import jax, jax.numpy as jnp
        import numpy as np
        N_NODES = 6250
        N_EDGES = 100000
        D_IN = 128
        D_HID = 256

        def _glorot(key, shape):
            lim = 1.0 / np.sqrt(shape[0])
            return jax.random.uniform(key, shape, jnp.float32, -lim, lim)

        def _gin_conv(x, src, dst, Wa, ba, Wb, bb):
            agg = jax.ops.segment_sum(x[src], dst, num_segments=x.shape[0])
            h = x + agg
            h = jax.nn.relu(h @ Wa + ba)
            return h @ Wb + bb
        src, dst = (edge_index[0], edge_index[1])
        h = jax.nn.relu(_gin_conv(x, src, dst, W1a, b1a, W1b, b1b))
        h = jax.nn.relu(_gin_conv(h, src, dst, W2a, b2a, W2b, b2b))
        return h
    edge_index = jnp.stack([src, dst])
    x = _layernorm(x + _L0_gnn_ref(x, src, dst, L0_gnn_Wq, L0_gnn_Wk, L0_gnn_Wv, L0_gnn_Wo, L0_gnn_bo, L0_gnn_W1, L0_gnn_b1, L0_gnn_W2, L0_gnn_b2, L0_gnn_bn1_w, L0_gnn_bn1_b, L0_gnn_bn2_w, L0_gnn_bn2_b), axis=-1)
    x = _layernorm(x + _L1_gnn_ref(x, edge_index, L1_gnn_Wq, L1_gnn_bq, L1_gnn_Wk, L1_gnn_bk, L1_gnn_Wv, L1_gnn_bv, L1_gnn_Wskip, L1_gnn_bskip, L1_gnn_Wbeta), axis=-1)
    x = _layernorm(x + _L2_gnn_ref(x, edge_index, L2_gnn_W1, L2_gnn_b1, L2_gnn_W2, L2_gnn_b2, L2_gnn_W3, L2_gnn_b3, L2_gnn_W4, L2_gnn_b4), axis=-1)
    x = _layernorm(x + _L3_gnn_ref(x, edge_index, L3_gnn_W1a, L3_gnn_b1a, L3_gnn_W1b, L3_gnn_b1b, L3_gnn_W2a, L3_gnn_b2a, L3_gnn_W2b, L3_gnn_b2b), axis=-1)
    return x

_drawn_inputs = setup_inputs


def setup_inputs(seed=0):
    import zlib

    import numpy as np

    out = dict(_drawn_inputs(seed))
    spreads = {'L0_gnn_bo': (0.0, 0.8),
     'L0_gnn_b1': (0.0, 0.471),
     'L0_gnn_b2': (0.0, 0.8),
     'L0_gnn_bn1_w': (1.0, 0.2),
     'L0_gnn_bn1_b': (0.0, 0.8),
     'L0_gnn_bn2_w': (1.0, 0.2),
     'L0_gnn_bn2_b': (0.0, 0.1),
     'L1_gnn_bq': (0.0, 0.496),
     'L1_gnn_bk': (0.0, 0.8),
     'L1_gnn_bv': (0.0, 0.1),
     'L1_gnn_bskip': (0.0, 0.1),
     'L2_gnn_b1': (0.0, 0.1),
     'L2_gnn_b2': (0.0, 0.1),
     'L2_gnn_b3': (0.0, 0.1),
     'L2_gnn_b4': (0.0, 0.1),
     'L3_gnn_b1a': (0.0, 0.368),
     'L3_gnn_b1b': (0.0, 0.1),
     'L3_gnn_b2a': (0.0, 0.36),
     'L3_gnn_b2b': (0.0, 0.1)}
    factors = {'L0_gnn_Wq': 4.079, 'L0_gnn_Wk': 4.043}
    for name, (base, spread) in spreads.items():
        noise = np.random.default_rng([zlib.crc32(name.encode()), seed]).standard_normal(out[name].shape)
        drawn = base * np.exp(spread * noise) if base else spread * noise
        out[name] = jnp.asarray(drawn.astype(out[name].dtype))
    for name, factor in factors.items():
        out[name] = (out[name] * factor).astype(out[name].dtype)
    return out
```

```python
from contextlib import ExitStack

import concourse.bass as bass
from concourse import mybir

P = 128
NODES, EDGES, D = 6250, 100000, 128
BLOCKS = -(-NODES // P)
LAST = NODES - (BLOCKS - 1) * P
TILES = -(-EDGES // P)
GB = 7
GROUPS = BLOCKS // GB
GN = GB * P
HALF = 4
UNROLL = 2 * HALF
TURNS = -(-(TILES + BLOCKS - 1) // UNROLL)
STEPS = TURNS * UNROLL
ROWS = -(-TILES // P)
COLS = ROWS * P
assert BLOCKS == GROUPS * GB and STEPS + HALF <= COLS
NO_DST = 16384
BIG = 1e30
H0, C0 = 8, D // 8
H1, C1 = 4, D // 4
HID = 100
A0 = D + H0 + 1
A1 = D + H1
SC = COLS * H1

F32 = mybir.dt.float32
I32 = mybir.dt.int32
ALU = mybir.AluOpType
ACT = mybir.ActivationFunctionType
AX = mybir.AxisListType
ds = bass.ds

WEIGHTS = [("wqkv0", 1, 3 * D), ("wo", 1, D), ("w1", 1, 2 * D), ("w2", 2, D), ("wqkvs", 1, 4 * D),
           ("g1", 1, HID), ("g2", 1, HID), ("g3", 1, HID), ("g4", 1, D),
           ("w1a", 1, 2 * D), ("w1b", 2, 2 * D), ("w2a", 2, 2 * D), ("w2b", 2, D)]
COLUMNS = [("bo", 1), ("b1", 2), ("b2", 1), ("n1w", 1), ("n1b", 1), ("n2w", 1), ("n2b", 1),
           ("c1", 1), ("c2", 1), ("c3", 1), ("b1a", 2), ("b2a", 2)]
SPREAD = [("bqkvs", 4 * D), ("wbeta", 3 * D), ("c4", D), ("b1b", 2 * D), ("b2b", D)]


class Memory:

    def __init__(self, nc, ctx):
        def sb(name, n, dt=F32):
            return ctx.enter_context(nc.sbuf_tensor(name, [P, n], dt))

        def split(t, *shape):
            names = " ".join("abc"[:len(shape)])
            return t.rearrange(f"p ({names}) -> p {names}", **dict(zip("abc", shape)))

        self.x = sb("x", BLOCKS * D)
        big = sb("big", BLOCKS * A0 + BLOCKS * D)
        self.sums = big
        self.gin_sums = big[:, BLOCKS * A0:]
        self.q = big[:, BLOCKS * A0:]
        self.score = big[:, 0:SC]
        self.srow = split(big[:, SC:2 * SC], ROWS, H1, P)
        self.fwd = split(big[:, 2 * SC:3 * SC], ROWS, H1, P)
        self.bwd = split(big[:, 0:SC], ROWS, H1, P)
        self.weight = big[:, 9000:9000 + SC]
        self.feat = sb("feat", BLOCKS * P)
        rows = sb("rows", UNROLL * 2 * D)
        self.rows = split(rows[:, :], UNROLL, 2 * D)
        self.hit = split(sb("hit", UNROLL * P)[:, :], 2, HALF, P)
        self.hitT = split(sb("hitT", UNROLL * P)[:, :], 2, HALF, P)
        self.prod = sb("prod", HALF * D)
        self.msg = split(sb("msg", 2 * HALF * A0)[:, :], 2, HALF, A0)
        self.raw = sb("raw", 2 * HALF * H0)
        self.stage_a = sb("stage_a", GN)
        self.stage_b = sb("stage_b", GN)
        self.stage_c = sb("stage_c", 2 * GN)
        self.stage_d = rows[:, 0:2 * GN]
        self.local = sb("local", COLS)
        self.src = sb("src", COLS, I32)
        self.idx = sb("idx", UNROLL, I32)
        self.block = sb("block", COLS, I32)
        self.pick0 = sb("pick0", COLS)
        self.pick1 = sb("pick1", COLS)
        self.dst_rows = sb("dst_rows", COLS)
        self.w, at = {}, 0
        w = sb("w", sum(k * n for _, k, n in WEIGHTS))
        for name, k, n in WEIGHTS:
            self.w[name] = split(w[:, at:at + k * n], k, n)
            at += k * n
        self.column, at = {}, 0
        self.columns = col = sb("columns", sum(n for _, n in COLUMNS))
        for name, n in COLUMNS:
            self.column[name] = col[:, at:at + n]
            at += n
        self.spread, at = {}, 0
        self.spreads = spread = sb("spread", sum(n for _, n in SPREAD))
        for name, n in SPREAD:
            self.spread[name] = spread[:, at:at + n]
            at += n
        self.ident = sb("ident", P)
        self.ones = sb("ones", P)
        self.number = sb("number", P)
        self.tile_id = sb("tile_id", ROWS)
        self.small = sb("small", 512)
        self.eps = sb("eps", 1)
        self.mean_var, self.scale, self.shift = self.small[:, 360:362], self.small[:, 362:363], self.small[:, 363:364]
        self.norm = sb("norm", BLOCKS)
        self.x_scratch = split(self.q[:, 5000:5000 + ROWS * (P + 1)], ROWS, P + 1)
        self.gathered = [ctx.enter_context(nc.semaphore(f"gathered{k}")) for k in range(UNROLL)]
        self.gathered_before = 0
        self.stored_before = 0
        self.pool_stored = [ctx.enter_context(nc.semaphore("pool_stored"))]
        self.ps = ctx.enter_context(nc.psum_tensor("ps", [P, 8 * 512], F32))

    def bank(self, k, n=512):
        return self.ps[:, 512 * k:512 * k + n]


class Phase:

    def __init__(self, nc, tag, names, lasting=()):
        self.nc, self.names, self.lasting = nc, [f"{tag}_{n}" for n in names.split()], list(lasting)

    def __enter__(self):
        self.ctx = ExitStack()
        nc = self.nc
        sems = [self.ctx.enter_context(nc.semaphore(n)) for n in self.names]
        with nc.Block() as clear:
            @clear.sync
            def _(sp):
                for s in sems:
                    sp.sem_clear(s)
        self.block = self.ctx.enter_context(nc.Block())
        return (self.block, *sems, *self.lasting)

    def __exit__(self, *a):
        return self.ctx.__exit__(*a)


def copies(ap, axis, n):
    ap = ap.unsqueeze(axis)
    shape = list(ap.shape)
    shape[axis] = n
    return ap.broadcast_to(shape)


def group_rows(table, g):
    return table[ds(g * GN, GN), :].rearrange("(b p) f -> p b f", p=P)


def load_blocks(engine, regs, m, first):
    engine.load(regs, m.block[0:1, ds(first, HALF)])
    return [engine.snap(r, min_val=0, max_val=BLOCKS - 1) for r in regs]


def registers(nc, engine, name):
    return [engine.alloc_register(f"{name}{k}") for k in range(HALF)]


def plan(nc, m, t):
    with Phase(nc, "plan", "rows_in params_in made conv ranked compared counted stepped based "
               "picked drawn done") as (
            block, rows_in, params_in, made, conv, ranked, compared, counted, stepped, based,
            picked, drawn, done):
        dst_i = m.stage_a[:, :].bitcast(I32)
        src_i = m.stage_b[:, :].bitcast(I32)
        src_f = m.stage_c[:, 0:COLS]
        ramp = m.stage_c[:, COLS:2 * COLS]
        tile_of = m.feat[:, 0:COLS]
        block_of = m.feat[:, COLS:2 * COLS]
        reached = m.feat[:, 2 * COLS:4 * COLS]
        rank = m.small[:, 0:ROWS]
        blk_i = m.small[:, 8:8 + ROWS].bitcast(I32)
        blk_f = m.small[:, 16:16 + ROWS]
        ints = m.rows.rearrange("p a b -> p (a b)")[:, 0:COLS + P + 8].bitcast(I32)
        part = m.small[:, 24:25]

        @block.sync
        def _(sp):
            sp.dma_start(dst_i.rearrange("p (j e) -> p j e", e=P),
                         t["dst"].rearrange("(j p) e -> p j e", p=P)).then_inc(rows_in, 16)
            sp.dma_start(src_i.rearrange("p (j e) -> p j e", e=P),
                         t["src"].rearrange("(j p) e -> p j e", p=P)).then_inc(rows_in, 16)
            for name, k, n in WEIGHTS:
                r = min(P, t[name].shape[0])
                sp.dma_start(m.w[name][0:r, :, :], t[name].rearrange("(k p) n -> p k n", p=r)).then_inc(params_in, 16)
            sp.dma_start(m.columns[:, :], t["columns"]).then_inc(params_in, 16)
            sp.dma_start(m.spreads[:, :], t["spread"].broadcast_to([P, t["spread"].shape[1]])).then_inc(params_in, 16)
            sp.dma_start(m.x[:, :].rearrange("p (b f) -> p b f", f=D),
                         t["x"].rearrange("(b p) f -> p b f", p=P)).then_inc(params_in, 16)
            sp.wait_ge(params_in, 16 * (len(WEIGHTS) + 3))

        @block.gpsimd
        def _(pool):
            pool.iota(ints[:, 0:COLS], [[1, COLS]], base=0, channel_multiplier=0).then_inc(made, 1)
            pool.iota(ints[:, COLS:COLS + ROWS], [[P, ROWS]], base=0, channel_multiplier=1).then_inc(made, 1)
            pool.memset(m.ones[:, :], 1.0).then_inc(made, 1)

        @block.vector
        def _(dve):
            dve.wait_ge(made, 3)
            dve.tensor_copy(ramp, ints[:, 0:COLS]).then_inc(conv, 1)
            dve.tensor_copy(m.tile_id[:, :], ints[:, COLS:COLS + ROWS]).then_inc(conv, 1)
            dve.wait_ge(rows_in, 32)
            dve.tensor_copy(m.dst_rows[:, :], dst_i).then_inc(conv, 1)
            dve.tensor_copy(src_f, src_i).then_inc(conv, 1)
            dve.tensor_scalar(blk_i, dst_i[:, 0:COLS:P], 7, None, ALU.arith_shift_right).then_inc(conv, 1)
            dve.wait_ge(conv, 5)
            dve.tensor_copy(m.number[:, :], ramp[:, 0:P]).then_inc(ranked, 1)
            dve.tensor_copy(blk_f, blk_i).then_inc(ranked, 1)
            dve.tensor_scalar(m.ident[:, :], ramp[:, 0:P], m.tile_id[:, 0:1], None, ALU.is_equal).then_inc(ranked, 1)
            dve.wait_ge(ranked, 3)
            dve.tensor_tensor(rank, blk_f, m.tile_id[:, :], ALU.add).then_inc(ranked, 1)
            dve.wait_ge(ranked, 4)
            for j in range(ROWS):
                if j >= 2:
                    dve.wait_ge(counted, 2 * (j - 1))
                dve.tensor_scalar(reached[:, (j % 2) * COLS:(j % 2 + 1) * COLS], ramp, rank[:, j:j + 1],
                                  None, ALU.is_ge).then_inc(compared, 1)
            dve.wait_ge(counted, 2 * ROWS)
            for k in range(2):
                c = slice(k * COLS // 2, (k + 1) * COLS // 2)
                dve.tensor_scalar(tile_of[:, c], m.bank(k, COLS // 2), -1.0, 0.0, ALU.add, ALU.max).then_inc(stepped, 1)
            dve.wait_ge(stepped, 2)
            dve.tensor_tensor(block_of, ramp, tile_of, ALU.subtract).then_inc(based, 1)
            for j in range(ROWS):
                c = slice(j * P, (j + 1) * P)
                dve.tensor_scalar(m.pick0[:, c], tile_of[:, c], m.tile_id[:, j:j + 1], None, ALU.is_equal).then_inc(picked, 1)
                before = max(j - 1, 0)
                dve.tensor_scalar(m.pick1[:, c], tile_of[:, c], m.tile_id[:, before:before + 1],
                                  None, ALU.is_equal).then_inc(picked, 1)
            dve.wait_ge(based, 1)
            dve.tensor_scalar(block_of, block_of, -float(P), None, ALU.mult).then_inc(based, 1)
            dve.tensor_tensor(m.rows.rearrange("p a b -> p (a b)")[:, 0:COLS], ramp, tile_of, ALU.subtract).then_inc(based, 1)
            dve.wait_ge(based, 3)
            dve.tensor_scalar(m.block[:, :], m.rows.rearrange("p a b -> p (a b)")[:, 0:COLS], float(BLOCKS - 1),
                              None, ALU.min).then_inc(done, 1)
            dve.wait_ge(drawn, 2 * ROWS)
            for j in range(ROWS):
                c = slice(j * P, (j + 1) * P)
                dve.tensor_tensor(m.local[:, c], m.ps[:, 1024 + j * P:1024 + (j + 1) * P], block_of[:, c], ALU.add).then_inc(done, 1)
                dve.tensor_copy(m.src[:, c], m.ps[:, 2048 + j * P:2048 + (j + 1) * P]).then_inc(done, 1)

        @block.tensor
        def _(pe):
            for j in range(ROWS):
                pe.wait_ge(compared, j + 1)
                for k in range(2):
                    pe.matmul(m.bank(k, COLS // 2), m.ones[:, :],
                              reached[:, (j % 2) * COLS + k * COLS // 2:(j % 2) * COLS + (k + 1) * COLS // 2],
                              start=(j == 0), stop=(j == ROWS - 1)).then_inc(counted, 1)
            for j in range(ROWS):
                pe.wait_ge(picked, 2 * (j + 1))
                c = slice(j * P, (j + 1) * P)
                for at, rows in ((1024, m.dst_rows[:, :]), (2048, src_f)):
                    out = m.ps[:, at + j * P:at + (j + 1) * P]
                    mm = pe.matmul(out, rows[:, c], m.pick0[:, c], start=True, stop=(j == 0))
                    if j:
                        mm = pe.matmul(out, rows[:, (j - 1) * P:j * P], m.pick1[:, c], start=False, stop=True)
                    mm.then_inc(drawn, 1)


def gathers(pool, m, table, f, idx_copied, issued, free, gathered):
    with pool.Fori(0, TURNS) as i:
        for h in range(2):
            pool.wait_ge(free, 2 * i + h + 1)
            pool.tensor_copy(m.idx[:, h * HALF:(h + 1) * HALF],
                             m.src[:, ds(i * UNROLL + h * HALF, HALF)]).then_inc(idx_copied, 1)
            pool.wait_ge(idx_copied, 2 * i + h + 1)
            pool.sem_inc(issued, 1)
            for k in range(h * HALF, (h + 1) * HALF):
                pool.indirect_dma_start(m.rows[:, k, 0:f], None, table,
                                        bass.IndirectOffsetOnAxis(m.idx[:, k:k + 1], 0)).then_inc(gathered[k], 16)


def hits(dve, m, h, first):
    return dve.tensor_tensor(m.hit[:, h], copies(m.number[:, :], 1, HALF),
                             copies(m.local[:, ds(first, HALF)], 2, P), ALU.is_equal)


def sum_rows(nc, m, tag, table, f, sums, width):
    with Phase(nc, tag, "idx_copied issued free used added hit_ready", m.gathered) as (
            block, idx_copied, issued, free, used, added, hit_ready, *gathered):
        before = m.gathered_before
        m.gathered_before += 16 * TURNS

        @block.gpsimd
        def _(pool):
            gathers(pool, m, table, f, idx_copied, issued, free, gathered)

        @block.tensor
        def _(pe):
            pe.sem_inc(free, 2)
            with pe.Fori(0, TURNS) as i:
                for h in range(2):
                    pe.wait_ge(hit_ready, 2 * i + h + 1)
                    for k in range(HALF):
                        slot = h * HALF + k
                        pe.wait_ge(gathered[slot], before + 16 * i + 16)
                        pe.wait_ge(added, i * UNROLL + slot + 1)
                        pe.matmul(m.bank(slot, f), m.hit[:, h, k, :], m.rows[:, slot, 0:f],
                                  start=True, stop=True).then_inc(used, 1)
                    pe.wait_ge(used, i * UNROLL + (h + 1) * HALF)
                    pe.sem_inc(free, 1)

        @block.vector
        def _(dve):
            regs = registers(nc, dve, tag)
            dve.sem_inc(added, UNROLL)
            with dve.Fori(0, TURNS) as i:
                for h in range(2):
                    hits(dve, m, h, i * UNROLL + h * HALF).then_inc(hit_ready, 1)
                for h in range(2):
                    at = load_blocks(dve, regs, m, i * UNROLL + h * HALF)
                    for k in range(HALF):
                        slot = h * HALF + k
                        to = sums[:, ds(at[k] * width, f)]
                        dve.wait_ge(used, i * UNROLL + slot + 1)
                        dve.wait_ge(added, UNROLL + i * UNROLL + slot)
                        dve.tensor_tensor(to, to, m.bank(slot, f), ALU.add).then_inc(added, 1)


def attend(nc, m, table):
    with Phase(nc, "at0", "idx_copied issued free used added hit_ready turned copied q_ready multiplied "
               "reduced clipped weights_ready weighted ones_in", m.gathered) as (
            block, idx_copied, issued, free, used, added, hit_ready, turned, copied, q_ready, multiplied,
            reduced, clipped, weights_ready, weighted, ones_in, *gathered):
        before = m.gathered_before
        m.gathered_before += 16 * TURNS
        raw = m.raw[:, :].rearrange("p (a n) -> p a n", a=2)

        @block.gpsimd
        def _(pool):
            gathers(pool, m, table, 2 * D, idx_copied, issued, free, gathered)

        @block.tensor
        def _(pe):
            regs = registers(nc, pe, "at0pe")
            pe.sem_inc(free, 2)

            def products(j, h):
                pe.wait_ge(weighted, j + 1)
                for k in range(HALF):
                    pe.wait_ge(added, j * HALF + k + 1)
                    mm = pe.matmul(m.bank(k, A0), m.hit[:, h, k, :], m.msg[:, h, k, :], start=True, stop=True)
                    mm.then_inc(used, 1)
                pe.wait_ge(used, (j + 2) * HALF)
                pe.sem_inc(free, 1)

            def queries(j, h, first=False):
                pe.wait_ge(hit_ready, j + 1)
                if not first:
                    pe.wait_ge(copied, j - 1)
                for k in range(HALF):
                    mm = pe.transpose(m.bank(4 + h)[:, k * P:(k + 1) * P], m.hit[:, h, k, :], m.ident[:, :])
                mm.then_inc(turned, 1)
                at = load_blocks(pe, regs, m, j * HALF)
                pe.wait_ge(copied, j + 1)
                if not first:
                    pe.wait_ge(multiplied, j - 1)
                for k in range(HALF):
                    mm = pe.matmul(m.bank(6 + h)[:, k * P:(k + 1) * P], m.hitT[:, h, k, :],
                                   m.q[:, ds(at[k] * D, D)], start=True, stop=True)
                mm.then_inc(q_ready, 1)

            pe.sem_inc(used, HALF)
            queries(0, 0, True)
            queries(1, 1, True)
            products(0, 0)
            queries(2, 0)
            with pe.Fori(1, TURNS) as i:
                products(2 * i - 1, 1)
                queries(2 * i + 1, 1)
                products(2 * i, 0)
                queries(2 * i + 2, 0)
            products(2 * TURNS - 1, 1)

        @block.scalar
        def _(act):
            def copy(j, h, first=False):
                act.wait_ge(turned, j + 1)
                if not first:
                    act.wait_ge(q_ready, j - 1)
                act.activation(m.hitT[:, h], m.bank(4 + h).rearrange("p (k n) -> p k n", k=HALF), ACT.Copy).then_inc(copied, 1)

            def exps(j, h):
                act.wait_ge(clipped, j + 1)
                act.wait_ge(used, j * HALF)
                act.activation(m.msg[:, h, :, D:D + H0], raw[:, h].rearrange("p (k n) -> p k n", k=HALF),
                               ACT.Exp, scale=float(C0) ** -0.5).then_inc(weights_ready, 1)

            copy(0, 0, True)
            copy(1, 1, True)
            act.wait_ge(clipped, 1)
            act.activation(m.msg[:, 0, :, D:D + H0], raw[:, 0].rearrange("p (k n) -> p k n", k=HALF),
                           ACT.Exp, scale=float(C0) ** -0.5).then_inc(weights_ready, 1)
            copy(2, 0)
            with act.Fori(1, TURNS) as i:
                exps(2 * i - 1, 1)
                copy(2 * i + 1, 1)
                exps(2 * i, 0)
                copy(2 * i + 2, 0)
            exps(2 * TURNS - 1, 1)

        @block.vector
        def _(dve):
            regs = registers(nc, dve, "at0dve")
            dve.memset(m.msg[:, :, :, D + H0:A0], 1.0).then_inc(ones_in, 1)
            dve.wait_ge(ones_in, 1)
            dve.sem_inc(added, HALF)

            def scores(i, j, h):
                dve.wait_ge(q_ready, j + 1)
                for k in range(HALF):
                    dve.wait_ge(gathered[h * HALF + k], before + 16 * i + 16)
                prod = m.prod[:, :].rearrange("p (k n) -> p k n", k=HALF)
                dve.tensor_tensor(prod, m.rows[:, h * HALF:(h + 1) * HALF, 0:D],
                                  m.bank(6 + h).rearrange("p (k n) -> p k n", k=HALF), ALU.mult).then_inc(multiplied, 1)
                dve.wait_ge(multiplied, j + 1)
                dve.tensor_reduce(raw[:, h], m.prod[:, :].rearrange("p (n c) -> p n c", c=C0), AX.X, ALU.add).then_inc(reduced, 1)
                dve.wait_ge(reduced, j + 1)
                lim = 5.0 * float(C0) ** 0.5
                dve.tensor_scalar(raw[:, h], raw[:, h], lim, -lim, ALU.min, ALU.max).then_inc(clipped, 1)

            def adds(j):
                at = load_blocks(dve, regs, m, j * HALF)
                for k in range(HALF):
                    to = m.sums[:, ds(at[k] * A0, A0)]
                    dve.wait_ge(used, j * HALF + HALF + k + 1)
                    dve.wait_ge(added, j * HALF + HALF + k)
                    dve.tensor_tensor(to, to, m.bank(k, A0), ALU.add).then_inc(added, 1)

            def weigh(j, h):
                dve.wait_ge(weights_ready, j + 1)
                dve.tensor_tensor(m.msg[:, h, :, 0:D].rearrange("p k (n c) -> p k n c", c=C0),
                                  m.rows[:, h * HALF:(h + 1) * HALF, D:2 * D].rearrange("p k (n c) -> p k n c", c=C0),
                                  copies(m.msg[:, h, :, D:D + H0], 3, C0), ALU.mult).then_inc(weighted, 1)

            def next_hits(j, h):
                dve.wait_ge(used, (j + 1) * HALF)
                hits(dve, m, 1 - h, (j + 1) * HALF).then_inc(hit_ready, 1)

            hits(dve, m, 0, 0).then_inc(hit_ready, 1)
            hits(dve, m, 1, HALF).then_inc(hit_ready, 1)
            scores(0, 0, 0)
            weigh(0, 0)
            scores(0, 1, 1)
            next_hits(1, 1)
            adds(0)
            weigh(1, 1)
            with dve.Fori(1, TURNS) as i:
                scores(i, 2 * i, 0)
                next_hits(2 * i, 0)
                adds(2 * i - 1)
                weigh(2 * i, 0)
                scores(i, 2 * i + 1, 1)
                next_hits(2 * i + 1, 1)
                adds(2 * i)
                weigh(2 * i + 1, 1)
            adds(2 * TURNS - 1)


def score(nc, m, table):
    with Phase(nc, "sc1", "idx_copied issued free hit_ready turned copied q_ready multiplied reduced", m.gathered) as (
            block, idx_copied, issued, free, hit_ready, turned, copied, q_ready, multiplied, reduced, *gathered):
        before = m.gathered_before
        m.gathered_before += 16 * TURNS

        @block.gpsimd
        def _(pool):
            gathers(pool, m, table, D, idx_copied, issued, free, gathered)

        @block.tensor
        def _(pe):
            regs = registers(nc, pe, "sc1pe")
            pe.sem_inc(free, 2)

            def queries(j, h, first=False):
                pe.wait_ge(hit_ready, j + 1)
                if not first:
                    pe.wait_ge(copied, j - 1)
                for k in range(HALF):
                    mm = pe.transpose(m.bank(4 + h)[:, k * P:(k + 1) * P], m.hit[:, h, k, :], m.ident[:, :])
                mm.then_inc(turned, 1)
                at = load_blocks(pe, regs, m, j * HALF)
                pe.wait_ge(copied, j + 1)
                if not first:
                    pe.wait_ge(multiplied, j - 1)
                for k in range(HALF):
                    mm = pe.matmul(m.bank(6 + h)[:, k * P:(k + 1) * P], m.hitT[:, h, k, :],
                                   m.q[:, ds(at[k] * D, D)], start=True, stop=True)
                mm.then_inc(q_ready, 1)

            queries(0, 0, True)
            queries(1, 1, True)
            with pe.Fori(1, TURNS) as i:
                queries(2 * i, 0)
                queries(2 * i + 1, 1)

        @block.scalar
        def _(act):
            def copy(j, h, first=False):
                act.wait_ge(turned, j + 1)
                if not first:
                    act.wait_ge(q_ready, j - 1)
                act.activation(m.hitT[:, h], m.bank(4 + h).rearrange("p (k n) -> p k n", k=HALF), ACT.Copy).then_inc(copied, 1)

            copy(0, 0, True)
            copy(1, 1, True)
            with act.Fori(1, TURNS) as i:
                copy(2 * i, 0)
                copy(2 * i + 1, 1)

        @block.vector
        def _(dve):
            prod = m.prod[:, :].rearrange("p (k n) -> p k n", k=HALF)

            def scores(i, j, h):
                dve.wait_ge(q_ready, j + 1)
                for k in range(HALF):
                    dve.wait_ge(gathered[h * HALF + k], before + 16 * i + 16)
                dve.tensor_tensor(prod, m.rows[:, h * HALF:(h + 1) * HALF, 0:D],
                                  m.bank(6 + h).rearrange("p (k n) -> p k n", k=HALF), ALU.mult).then_inc(multiplied, 1)
                dve.wait_ge(multiplied, j + 1)
                dve.sem_inc(free, 1)
                dve.tensor_reduce(m.score[:, ds(j * HALF * H1, HALF * H1)],
                                  m.prod[:, :].rearrange("p (n c) -> p n c", c=C1), AX.X, ALU.add).then_inc(reduced, 1)
                dve.wait_ge(reduced, j + 1)

            def next_hits(j, h):
                dve.wait_ge(turned, j)
                hits(dve, m, h, j * HALF).then_inc(hit_ready, 1)

            hits(dve, m, 0, 0).then_inc(hit_ready, 1)
            with dve.Fori(0, TURNS) as i:
                next_hits(2 * i + 1, 1)
                scores(i, 2 * i, 0)
                next_hits(2 * i + 2, 0)
                scores(i, 2 * i + 1, 1)
            dve.memset(m.score[:, STEPS * H1:SC], 0.0).then_inc(reduced, 1)


def sum_values(nc, m, table):
    with Phase(nc, "va1", "idx_copied issued free used added hit_ready weights_ready weighted", m.gathered) as (
            block, idx_copied, issued, free, used, added, hit_ready, weights_ready, weighted, *gathered):
        before = m.gathered_before
        m.gathered_before += 16 * TURNS

        @block.gpsimd
        def _(pool):
            gathers(pool, m, table, D, idx_copied, issued, free, gathered)

        @block.tensor
        def _(pe):
            pe.sem_inc(free, 2)
            with pe.Fori(0, TURNS) as i:
                for h in range(2):
                    j = 2 * i + h
                    pe.wait_ge(hit_ready, j + 1)
                    pe.wait_ge(weighted, j + 1)
                    pe.wait_ge(weights_ready, j + 1)
                    for k in range(HALF):
                        slot = h * HALF + k
                        pe.wait_ge(added, i * UNROLL + slot + 1)
                        pe.matmul(m.bank(slot, A1), m.hit[:, h, k, :], m.msg[:, h, k, 0:A1],
                                  start=True, stop=True).then_inc(used, 1)

        @block.scalar
        def _(act):
            with act.Fori(0, TURNS) as i:
                for h in range(2):
                    act.wait_ge(added, i * UNROLL + (h + 1) * HALF)
                    act.activation(m.msg[:, h, :, D:A1],
                                   m.weight[:, ds((i * UNROLL + h * HALF) * H1, HALF * H1)].rearrange("p (k n) -> p k n", n=H1),
                                   ACT.Copy).then_inc(weights_ready, 1)

        @block.vector
        def _(dve):
            regs = registers(nc, dve, "va1")
            dve.sem_inc(added, UNROLL)

            def weigh(i, j, h):
                hits(dve, m, h, j * HALF).then_inc(hit_ready, 1)
                for k in range(HALF):
                    dve.wait_ge(gathered[h * HALF + k], before + 16 * i + 16)
                dve.tensor_tensor(m.msg[:, h, :, 0:D].rearrange("p k (n c) -> p k n c", c=C1),
                                  m.rows[:, h * HALF:(h + 1) * HALF, 0:D].rearrange("p k (n c) -> p k n c", c=C1),
                                  copies(m.weight[:, ds(j * HALF * H1, HALF * H1)].rearrange("p (k n) -> p k n", n=H1), 3, C1),
                                  ALU.mult).then_inc(weighted, 1)
                dve.wait_ge(weighted, j + 1)
                dve.sem_inc(free, 1)

            def adds(j, h):
                at = load_blocks(dve, regs, m, j * HALF)
                for k in range(HALF):
                    to = m.sums[:, ds(at[k] * A1, A1)]
                    dve.wait_ge(used, j * HALF + k + 1)
                    dve.wait_ge(added, UNROLL + j * HALF + k)
                    dve.tensor_tensor(to, to, m.bank(h * HALF + k, A1), ALU.add).then_inc(added, 1)

            weigh(0, 0, 0)
            weigh(0, 1, 1)
            adds(0, 0)
            with dve.Fori(1, TURNS) as i:
                weigh(i, 2 * i, 0)
                adds(2 * i - 1, 1)
                weigh(i, 2 * i + 1, 1)
                adds(2 * i, 0)
            adds(2 * TURNS - 1, 1)


def softmax_rows(nc, m):
    with Phase(nc, "sr1", "turned copied placed taken") as (block, turned, copied, placed, taken):
        by_step = m.score.rearrange("p (s h) -> p h s", h=H1)
        turned_scores = m.stage_c[:, 0:H1 * P]
        turned_picks = m.stage_a[:, 0:2 * P]

        @block.tensor
        def _(pe):
            for j in range(ROWS):
                c = slice(j * P, (j + 1) * P)
                if j:
                    pe.wait_ge(copied, 2 * j)
                for h in range(H1):
                    pe.transpose(m.bank(0)[:, h * P:(h + 1) * P], by_step[:, h, c], m.ident[:, :])
                pe.transpose(m.bank(1)[:, 0:P], m.pick0[:, c], m.ident[:, :])
                pe.transpose(m.bank(1)[:, P:2 * P], m.pick1[:, c], m.ident[:, :]).then_inc(turned, 1)
                pe.wait_ge(copied, 2 * (j + 1))
                if j >= 2:
                    pe.wait_ge(taken, j - 1)
                pe.matmul(m.bank(2 + j % 2), turned_picks[:, 0:P], turned_scores, start=True,
                          stop=(j == ROWS - 1)).then_inc(placed, 1)
                if j:
                    pe.matmul(m.bank(2 + (j - 1) % 2), turned_picks[:, P:2 * P], turned_scores,
                              start=False, stop=True).then_inc(placed, 1)

        @block.scalar
        def _(act):
            for j in range(ROWS):
                act.wait_ge(turned, j + 1)
                if j:
                    act.wait_ge(placed, 2 * j - 1)
                act.activation(turned_scores, m.bank(0), ACT.Copy).then_inc(copied, 1)
                act.activation(turned_picks, m.bank(1, 2 * P), ACT.Copy).then_inc(copied, 1)

        @block.vector
        def _(dve):
            for j in range(ROWS):
                dve.wait_ge(placed, min(2 * (j + 2) - 1, 2 * ROWS - 1))
                dve.tensor_copy(m.srow[:, j], m.bank(2 + j % 2).rearrange("p (h e) -> p h e", h=H1)).then_inc(taken, 1)


def softmax_weights(nc, m):
    with Phase(nc, "sw1", "linked first ends turned rowed seven chained back backed second maxed exped drawn stored") as (
            block, linked, first, ends, turned, rowed, seven, chained, back, backed, second, maxed, exped, drawn, stored):
        links = m.x_scratch
        dst = m.dst_rows[:, :].rearrange("p (j e) -> p j e", e=P)
        ends_of = m.small[:, 0:ROWS * 4 * H1].rearrange("p (j q h) -> p j q h", q=4, h=H1)
        carried = m.small[:, 128:128 + ROWS * 2 * H1].rearrange("p (j q h) -> p j q h", q=2, h=H1)
        row = lambda t, a=0: t[0:H1, a:a + COLS]
        last_max, first_max = row(m.stage_a), row(m.stage_b)
        first_dst, last_dst = row(m.stage_c), row(m.stage_c, COLS)
        flat = m.hit.rearrange("p a k n -> p (a k n)")
        flat_t = m.hitT.rearrange("p a k n -> p (a k n)")
        flat_m = m.msg.rearrange("p a k n -> p (a k n)")
        cont, single = row(m.stage_d), row(m.stage_d, COLS)
        onward, backward, penalty = row(flat), row(flat_t), row(flat_m)

        def run(dve, starts, sem):
            for j in range(ROWS):
                for h in range(H1):
                    for to, q in ((m.fwd, 0), (m.bwd, 1)):
                        start = -BIG if starts is None else starts[:, j, q, h:h + 1]
                        if q == 0:
                            dve.tensor_tensor_scan(to[:, j, h, :], links[:, j, 0:P], m.srow[:, j, h, :], start,
                                                   ALU.add, ALU.max).then_inc(sem, 1)
                        else:
                            dve.tensor_tensor_scan(to[:, j, h, ::-1], links[:, j, P:0:-1], m.srow[:, j, h, ::-1], start,
                                                   ALU.add, ALU.max).then_inc(sem, 1)

        @block.vector
        def _(dve):
            dve.memset(links[:, :, 0:1], 0.0).then_inc(linked, 1)
            dve.memset(links[:, :, P:P + 1], 0.0).then_inc(linked, 1)
            dve.tensor_tensor(links[:, :, 1:P], dst[:, :, 1:P], dst[:, :, 0:P - 1], ALU.is_equal).then_inc(linked, 1)
            dve.wait_ge(linked, 3)
            dve.tensor_scalar(links[:, :, 1:P], links[:, :, 1:P], -1.0, BIG, ALU.add, ALU.mult).then_inc(linked, 1)
            dve.wait_ge(linked, 4)
            run(dve, None, first)
            dve.wait_ge(first, 2 * ROWS * H1)
            dve.tensor_copy(ends_of[:, :, 0, :], m.fwd[:, :, :, P - 1]).then_inc(ends, 1)
            dve.tensor_copy(ends_of[:, :, 1, :], m.bwd[:, :, :, 0]).then_inc(ends, 1)
            dve.tensor_copy(ends_of[:, :, 2, :], copies(dst[:, :, 0], 2, H1)).then_inc(ends, 1)
            dve.tensor_copy(ends_of[:, :, 3, :], copies(dst[:, :, P - 1], 2, H1)).then_inc(ends, 1)
            for q, to in enumerate((last_max, first_max, first_dst, last_dst)):
                dve.wait_ge(turned, q + 1)
                dve.tensor_copy(to, m.ps[0:H1, 1024 * q:1024 * q + COLS]).then_inc(rowed, 1)
            dve.wait_ge(rowed, 4)
            dve.memset(cont[:, 0:1], 0.0).then_inc(seven, 1)
            dve.tensor_tensor(cont[:, 1:COLS], first_dst[:, 1:COLS], last_dst[:, 0:COLS - 1], ALU.is_equal).then_inc(seven, 1)
            dve.tensor_tensor(single, first_dst, last_dst, ALU.is_equal).then_inc(seven, 1)
            dve.memset(backward[:, COLS - 1:COLS], 0.0).then_inc(seven, 1)
            dve.wait_ge(seven, 4)
            dve.tensor_tensor(onward, cont, single, ALU.mult).then_inc(seven, 1)
            dve.tensor_tensor(backward[:, 0:COLS - 1], cont[:, 1:COLS], single[:, 0:COLS - 1], ALU.mult).then_inc(seven, 1)
            dve.wait_ge(seven, 6)
            for t_, f_ in ((onward, onward), (backward, backward), (penalty, cont)):
                dve.tensor_scalar(t_, f_, -1.0, BIG, ALU.add, ALU.mult).then_inc(seven, 1)
            dve.wait_ge(seven, 9)
            dve.tensor_tensor_scan(onward, onward, last_max, -BIG, ALU.add, ALU.max).then_inc(chained, 1)
            dve.tensor_tensor_scan(backward[:, ::-1], backward[:, ::-1], first_max[:, ::-1], -BIG, ALU.add, ALU.max).then_inc(chained, 1)
            dve.wait_ge(chained, 2)
            dve.memset(last_max[:, 0:1], -BIG).then_inc(chained, 1)
            dve.memset(first_max[:, COLS - 1:COLS], -BIG).then_inc(chained, 1)
            dve.tensor_tensor(last_max[:, 1:COLS], onward[:, 0:COLS - 1], penalty[:, 1:COLS], ALU.add).then_inc(chained, 1)
            dve.tensor_tensor(first_max[:, 0:COLS - 1], backward[:, 1:COLS], penalty[:, 1:COLS], ALU.add).then_inc(chained, 1)
            dve.wait_ge(back, 1)
            dve.tensor_copy(m.small[:, 128:128 + ROWS * 2 * H1], m.ps[:, 0:ROWS * 2 * H1]).then_inc(backed, 1)
            dve.wait_ge(backed, 1)
            run(dve, carried, second)
            dve.wait_ge(second, 2 * ROWS * H1)
            for j in range(ROWS):
                dve.tensor_tensor(m.fwd[:, j], m.fwd[:, j], m.bwd[:, j], ALU.max).then_inc(maxed, 1)
            for j in range(ROWS):
                dve.wait_ge(maxed, j + 1)
                dve.tensor_tensor(m.srow[:, j], m.srow[:, j], m.fwd[:, j], ALU.subtract).then_inc(maxed, 1)
            for j in range(ROWS):
                dve.wait_ge(drawn, j + 1)
                dve.wait_ge(maxed, 2 * ROWS)
                dve.tensor_copy(m.weight[:, j * P * H1:(j + 1) * P * H1].rearrange("p (s h) -> p h s", h=H1),
                                m.bank(1 + j % 2).rearrange("p (h s) -> p h s", h=H1)).then_inc(stored, 1)

        @block.scalar
        def _(act):
            for j in range(ROWS):
                act.wait_ge(maxed, ROWS + j + 1)
                act.activation(m.srow[:, j], m.srow[:, j], ACT.Exp, scale=float(C1) ** -0.5).then_inc(exped, 1)

        @block.tensor
        def _(pe):
            pe.wait_ge(ends, 4)
            for q in range(4):
                for j in range(ROWS):
                    mm = pe.transpose(m.ps[0:H1, 1024 * q + j * P:1024 * q + (j + 1) * P], ends_of[:, j, q, :], m.ident[:, :])
                mm.then_inc(turned, 1)
            pe.wait_ge(chained, 6)
            pe.wait_ge(rowed, 4)
            for j in range(ROWS):
                for q, of in enumerate((last_max, first_max)):
                    mm = pe.transpose(m.ps[:, (2 * j + q) * H1:(2 * j + q + 1) * H1], of[:, j * P:(j + 1) * P], m.ident[0:H1, 0:H1])
            mm.then_inc(back, 1)
            for j in range(ROWS):
                pe.wait_ge(exped, j + 1)
                if j >= 2:
                    pe.wait_ge(stored, j - 1)
                for h in range(H1):
                    out = m.bank(1 + j % 2)[:, h * P:(h + 1) * P]
                    mm = pe.matmul(out, m.srow[:, j, h, :], m.pick0[:, j * P:(j + 1) * P], start=True, stop=(j == 0))
                    if j:
                        mm = pe.matmul(out, m.srow[:, j - 1, h, :], m.pick1[:, j * P:(j + 1) * P], start=False, stop=True)
                mm.then_inc(drawn, 1)


CHUNKS = ((0, 512), (512, GN))


def blocks(ap, n=P):
    return ap.rearrange("p (b n) -> p b n", n=n)


def turn_blocks(pe, m, bank, of, rows=P):
    for b in range(GB):
        out = m.ps[0:rows, 512 * bank + b * P:512 * bank + (b + 1) * P]
        mm = pe.transpose(out, of[:, b * P:b * P + rows], m.ident[:, :])
    return mm


def feature_product(pe, m, bank, pairs):
    for a, b in CHUNKS:
        for n, (w, x) in enumerate(pairs):
            mm = pe.matmul(m.ps[:, 512 * bank + a:512 * bank + b], w, x[:, a:b], start=(n == 0), stop=(n == len(pairs) - 1))
    return mm


def normalize(dve, m, at, to, stats, summing, root, rooted, inverted, step, g):
    six = m.small[:, 256:256 + 6 * GB].rearrange("p (b n) -> p b n", n=6)
    two = m.small[:, 304:304 + 2 * GB].rearrange("p (b n) -> p b n", n=2)
    std = m.small[:, 320:320 + GB]
    base = g * (2 * GB)
    for b in range(GB):
        dve.bn_stats(six[:, b, :], at[:, b * P:(b + 1) * P]).then_inc(stats, 1)
    dve.wait_ge(stats, base + GB)
    dve.sem_inc(summing, 1)
    for b in range(GB):
        dve.bn_aggr(two[:, b, :], six[:, b, :]).then_inc(stats, 1)
    dve.wait_ge(rooted, g + 1)
    dve.reciprocal(std, root).then_inc(inverted, 1)
    dve.wait_ge(inverted, g + 1)
    for b in range(GB):
        dve.tensor_scalar(to[:, b * P:(b + 1) * P], at[:, b * P:(b + 1) * P], two[:, b, 0:1], std[:, b:b + 1],
                          ALU.subtract, ALU.mult).then_inc(step, 1)


def take_roots(act, m, root, stats, rooted, g):
    two = m.small[:, 304:304 + 2 * GB].rearrange("p (b n) -> p b n", n=2)
    act.wait_ge(stats, g * (2 * GB) + 2 * GB)
    act.activation(root, two[:, :, 1], ACT.Sqrt, bias=m.eps[:, 0:1]).then_inc(rooted, 1)


def project0(nc, m, t, table):
    with Phase(nc, "pr0", "loaded projected dve_out act_out stage_free zeroed", m.pool_stored) as (
            block, loaded, projected, dve_out, act_out, stage_free, zeroed, stored):
        before = m.stored_before
        m.stored_before += 16 * GROUPS
        share = {0: (GB + 1) // 2, 1: GB // 2}

        @block.sync
        def _(sp):
            with sp.Fori(0, GROUPS) as g:
                sp.wait_ge(projected, g * GB + GB)
                sp.dma_start(m.stage_a[:, :], t["xT"][:, ds(g * GN, GN)]).then_inc(loaded, 16)

        @block.tensor
        def _(pe):
            pe.sem_inc(projected, GB)
            with pe.Fori(0, GROUPS) as g:
                pe.wait_ge(loaded, g * 16 + 16)
                for b in range(GB):
                    pe.wait_ge((dve_out, act_out)[b % 2], g * share[b % 2] + b // 2 + 1)
                    pe.matmul(m.bank(b, 3 * D), m.stage_a[:, b * P:(b + 1) * P], m.w["wqkv0"][:, 0, :],
                              start=True, stop=True).then_inc(projected, 1)

        @block.vector
        def _(dve):
            dve.sem_inc(dve_out, share[0])
            dve.memset(m.sums[:, 0:BLOCKS * A0], 0.0).then_inc(zeroed, 1)
            dve.memset(m.eps[:, :], 1e-5).then_inc(zeroed, 1)
            with dve.Fori(0, GROUPS) as g:
                dve.wait_ge(stage_free, g + 1)
                for b in range(0, GB, 2):
                    dve.wait_ge(projected, g * GB + GB + b + 1)
                    dve.tensor_copy(m.q[:, ds((g * GB + b) * D, D)], m.bank(b)[:, 0:D])
                    dve.tensor_copy(m.stage_c[:, b * 2 * D:(b + 1) * 2 * D], m.bank(b)[:, D:3 * D]).then_inc(dve_out, 1)

        @block.scalar
        def _(act):
            act.sem_inc(act_out, share[1])
            with act.Fori(0, GROUPS) as g:
                act.wait_ge(stage_free, g + 1)
                for b in range(1, GB, 2):
                    act.wait_ge(projected, g * GB + GB + b + 1)
                    act.activation(m.q[:, ds((g * GB + b) * D, D)], m.bank(b)[:, 0:D], ACT.Copy)
                    act.activation(m.stage_c[:, b * 2 * D:(b + 1) * 2 * D], m.bank(b)[:, D:3 * D], ACT.Copy).then_inc(act_out, 1)

        @block.gpsimd
        def _(pool):
            pool.sem_inc(stage_free, 1)
            with pool.Fori(0, GROUPS) as g:
                pool.wait_ge(dve_out, (g + 2) * share[0])
                pool.wait_ge(act_out, (g + 2) * share[1])
                pool.dma_start(group_rows(table, g), blocks(m.stage_c[:, :], 2 * D)).then_inc(stored, 16)
                pool.wait_ge(stored, before + g * 16 + 16)
                pool.sem_inc(stage_free, 1)


def batch_stats(dve, m, stats, weight, bias, rooted, scaled):
    n, parts = 250, NODES // 250
    six = m.small[:, 0:6 * parts].rearrange("p (b n) -> p b n", n=6)
    for b in range(parts):
        dve.bn_stats(six[:, b, :], m.feat[:, b * n:(b + 1) * n]).then_inc(stats, 1)
    dve.wait_ge(stats, parts)
    dve.bn_aggr(m.mean_var, m.small[:, 0:6 * parts]).then_inc(stats, 1)
    dve.wait_ge(rooted, 1)
    dve.reciprocal(m.scale, m.scale).then_inc(scaled, 1)
    dve.wait_ge(scaled, 1)
    dve.tensor_tensor(m.scale, m.scale, weight, ALU.mult).then_inc(scaled, 1)
    dve.wait_ge(scaled, 2)
    dve.tensor_tensor(m.shift, m.mean_var[:, 0:1], m.scale, ALU.mult).then_inc(scaled, 1)
    dve.wait_ge(scaled, 3)
    dve.tensor_tensor(m.shift, bias, m.shift, ALU.subtract).then_inc(scaled, 1)


def batch_root(act, m, stats, rooted):
    act.wait_ge(stats, NODES // 250 + 1)
    act.activation(m.scale, m.mean_var[:, 1:2], ACT.Sqrt, bias=m.eps[:, 0:1]).then_inc(rooted, 1)


def attend_out(nc, m, t):
    with Phase(nc, "ao0", "loaded inv scaled_in turned copied out done degs rooted2 stats rooted scaled") as (
            block, loaded, inv, scaled_in, turned, copied, out, done, degs, rooted2, stats, rooted, scaled):
        z = blocks(m.small[:, 200:200 + GB * H0], H0)
        deg = m.small[:, 400:400 + BLOCKS]

        @block.sync
        def _(sp):
            with sp.Fori(0, GROUPS) as g:
                sp.wait_ge(done, g + 1)
                sp.dma_start(m.stage_c[:, 0:GN], t["xT"][:, ds(g * GN, GN)]).then_inc(loaded, 16)

        @block.vector
        def _(dve):
            dve.sem_inc(done, 1)
            with dve.Fori(0, GROUPS) as g:
                s = blocks(m.sums[:, ds(g * (GB * A0), GB * A0)], A0)
                dve.tensor_scalar(z, s[:, :, D:D + H0], 1e-6, None, ALU.add).then_inc(inv, 1)
                dve.wait_ge(inv, g * 2 + 1)
                dve.reciprocal(z, z).then_inc(inv, 1)
                dve.wait_ge(inv, g * 2 + 2)
                dve.tensor_tensor(blocks(m.stage_a[:, :]).rearrange("p b (n c) -> p b n c", c=C0),
                                  s[:, :, 0:D].rearrange("p b (n c) -> p b n c", c=C0), copies(z, 3, C0),
                                  ALU.mult).then_inc(scaled_in, 1)
                dve.wait_ge(out, g + 1)
                dve.wait_ge(loaded, g * 16 + 16)
                dve.scalar_tensor_tensor(m.feat[:, ds(g * GN, GN)], m.ps[:, 1024:1024 + GN], m.column["bo"],
                                         m.stage_c[:, 0:GN], ALU.add, ALU.add).then_inc(done, 1)
            dve.tensor_scalar(deg, blocks(m.sums[:, 0:BLOCKS * A0], A0)[:, :, A0 - 1], 1.0, None, ALU.add).then_inc(degs, 1)
            dve.wait_ge(rooted2, 1)
            dve.reciprocal(m.norm[:, :], m.norm[:, :]).then_inc(degs, 1)
            dve.wait_ge(done, GROUPS + 1)
            batch_stats(dve, m, stats, m.column["n1w"], m.column["n1b"], rooted, scaled)

        @block.tensor
        def _(pe):
            with pe.Fori(0, GROUPS) as g:
                pe.wait_ge(scaled_in, g + 1)
                turn_blocks(pe, m, 0, m.stage_a).then_inc(turned, 1)
                pe.wait_ge(copied, g + 1)
                feature_product(pe, m, 2, [(m.w["wo"][:, 0, :], m.stage_b)]).then_inc(out, 1)

        @block.scalar
        def _(act):
            with act.Fori(0, GROUPS) as g:
                act.wait_ge(turned, g + 1)
                act.activation(m.stage_b[:, :], m.ps[:, 0:GN], ACT.Copy).then_inc(copied, 1)
            act.wait_ge(degs, 1)
            act.activation(m.norm[:, :], deg, ACT.Sqrt).then_inc(rooted2, 1)
            batch_root(act, m, stats, rooted)


def feed_forward(nc, m):
    with Phase(nc, "ff0", "normed hidden relu0 relu1 out done stats rooted scaled") as (
            block, normed, hidden, relu0, relu1, out, done, stats, rooted, scaled):
        act0, act1 = m.stage_c[:, 0:GN], m.stage_c[:, GN:2 * GN]

        @block.scalar
        def _(act):
            act.sem_inc(done, 1)
            with act.Fori(0, GROUPS) as g:
                act.wait_ge(done, g + 1)
                act.activation(m.stage_a[:, :], m.feat[:, ds(g * GN, GN)], ACT.Identity,
                               bias=m.shift, scale=m.scale).then_inc(normed, 1)
                act.wait_ge(hidden, g * 2 + 1)
                act.activation(act0, m.ps[:, 0:GN], ACT.Relu, bias=m.column["b1"][:, 0:1]).then_inc(relu0, 1)
            batch_root(act, m, stats, rooted)

        @block.tensor
        def _(pe):
            with pe.Fori(0, GROUPS) as g:
                pe.wait_ge(normed, g + 1)
                for o in range(2):
                    feature_product(pe, m, 2 * o, [(m.w["w1"][:, 0, o * P:(o + 1) * P], m.stage_a)]).then_inc(hidden, 1)
                pe.wait_ge(relu0, g + 1)
                pe.wait_ge(relu1, g + 1)
                feature_product(pe, m, 4, [(m.w["w2"][:, 0, :], act0), (m.w["w2"][:, 1, :], act1)]).then_inc(out, 1)

        @block.vector
        def _(dve):
            with dve.Fori(0, GROUPS) as g:
                dve.wait_ge(hidden, g * 2 + 2)
                dve.tensor_scalar(act1, m.ps[:, 1024:1024 + GN], m.column["b1"][:, 1:2], 0.0, ALU.add, ALU.max).then_inc(relu1, 1)
                dve.wait_ge(out, g + 1)
                dve.scalar_tensor_tensor(m.feat[:, ds(g * GN, GN)], m.ps[:, 2048:2048 + GN], m.column["b2"],
                                         m.stage_a[:, :], ALU.add, ALU.add).then_inc(done, 1)
            dve.wait_ge(done, GROUPS + 1)
            batch_stats(dve, m, stats, m.column["n2w"], m.column["n2b"], rooted, scaled)


def project1(nc, m, t, keys, values):
    with Phase(nc, "pr1", "normed turned added stats summing rooted inverted lned turned2 copied2 xed projected "
               "evened evac stage_free done kept", m.pool_stored) as (
            block, normed, turned, added, stats, summing, rooted, inverted, lned, turned2, copied2, xed, projected,
            evened, evac, stage_free, done, kept, stored):
        before = m.stored_before
        m.stored_before += 32 * GROUPS
        root = m.small[:, 330:330 + GB]

        @block.scalar
        def _(act):
            act.sem_inc(done, 1)
            with act.Fori(0, GROUPS) as g:
                act.wait_ge(done, g + 1)
                act.activation(m.stage_a[:, :], m.feat[:, ds(g * GN, GN)], ACT.Identity,
                               bias=m.shift, scale=m.scale).then_inc(normed, 1)
                take_roots(act, m, root, stats, rooted, g)
                act.wait_ge(lned, g * GB + GB)
                act.activation(m.x[:, ds(g * GN, GN)], m.stage_b[:, :], ACT.Copy).then_inc(xed, 1)
                act.wait_ge(turned2, g + 1)
                act.activation(m.stage_a[:, :], m.ps[:, 1024:1024 + GN], ACT.Copy).then_inc(copied2, 1)
                act.wait_ge(xed, g + 1)
                act.wait_ge(evac, g * 3 * GB + 3 * GB)
                act.wait_ge(stage_free, g + 1)
                act.sem_inc(done, 1)

        @block.tensor
        def _(pe):
            pe.sem_inc(evened, 4)
            with pe.Fori(0, GROUPS) as g:
                pe.wait_ge(normed, g + 1)
                turn_blocks(pe, m, 0, m.stage_a).then_inc(turned, 1)
                pe.wait_ge(lned, g * GB + GB)
                turn_blocks(pe, m, 2, m.stage_b).then_inc(turned2, 1)
                pe.wait_ge(copied2, g + 1)
                for b in range(GB):
                    if b >= 4:
                        pe.wait_ge(evac, g * 3 * GB + 3 * (b - 3))
                    pe.matmul(m.bank(4 + b % 4), m.stage_a[:, b * P:(b + 1) * P], m.w["wqkvs"][:, 0, :],
                              start=True, stop=True).then_inc(projected, 1)

        @block.vector
        def _(dve):
            with dve.Fori(0, GROUPS) as g:
                dve.wait_ge(turned, g + 1)
                dve.tensor_tensor(m.stage_b[:, :], m.ps[:, 0:GN], m.x[:, ds(g * GN, GN)], ALU.add).then_inc(added, 1)
                dve.wait_ge(added, g + 1)
                normalize(dve, m, m.stage_b, m.stage_b, stats, summing, root, rooted, inverted, lned, g)
                bias = m.spread["bqkvs"]
                for b in range(GB):
                    dve.wait_ge(projected, g * GB + b + 1)
                    ps = m.bank(4 + b % 4)
                    at = (g * GB + b) * D
                    dve.tensor_tensor(m.q[:, ds(at, D)], ps[:, 0:D], bias[:, 0:D], ALU.add).then_inc(evac, 1)
                    dve.tensor_tensor(m.stage_c[:, b * 2 * D:(b + 1) * 2 * D], ps[:, D:3 * D], bias[:, D:3 * D],
                                      ALU.add).then_inc(evac, 1)
                    dve.tensor_tensor(m.feat[:, ds(at, D)], ps[:, 3 * D:4 * D], bias[:, 3 * D:4 * D], ALU.add).then_inc(evac, 1)

        @block.gpsimd
        def _(pool):
            kv = blocks(m.stage_c[:, :], 2 * D)
            with pool.Fori(0, GROUPS) as g:
                pool.wait_ge(evac, g * 3 * GB + 3 * GB)
                pool.dma_start(group_rows(keys, g), kv[:, :, 0:D]).then_inc(stored, 16)
                pool.dma_start(group_rows(values, g), kv[:, :, D:2 * D]).then_inc(stored, 16)
                pool.wait_ge(stored, before + g * 32 + 32)
                pool.sem_inc(stage_free, 1)


def skip_gate(nc, m, table):
    with Phase(nc, "sg1", "vec gate stats summing rooted inverted lned turned copied xed projected placed stored done") as (
            block, vec, gate, stats, summing, rooted, inverted, lned, turned, copied, xed, projected, placed, stored, done):
        root = m.small[:, 330:330 + GB]
        z = blocks(m.small[:, 200:200 + GB * H1], H1)
        logit, beta = m.small[:, 340:340 + GB], m.small[:, 350:350 + GB]
        wbeta = m.spread["wbeta"]
        steps = 11

        @block.vector
        def _(dve):
            dve.tensor_tensor(m.prod[:, 0:D], wbeta[:, 0:D], wbeta[:, 2 * D:3 * D], ALU.add).then_inc(vec, 1)
            dve.tensor_tensor(m.prod[:, D:2 * D], wbeta[:, D:2 * D], wbeta[:, 2 * D:3 * D], ALU.subtract).then_inc(vec, 1)
            dve.sem_inc(done, 1)
            with dve.Fori(0, GROUPS) as g:
                s = blocks(m.sums[:, ds(g * (GB * A1), GB * A1)], A1)
                skip = m.feat[:, ds(g * GN, GN)]
                a, b, c = m.stage_a[:, :], m.stage_b[:, :], m.stage_c[:, 0:GN]
                after = lambda n: dve.wait_ge(vec, g * steps + 2 + n)
                after(0)
                dve.wait_ge(done, g + 1)
                dve.tensor_scalar(z, s[:, :, D:A1], 1e-16, None, ALU.max).then_inc(vec, 1)
                after(1)
                dve.reciprocal(z, z).then_inc(vec, 1)
                after(2)
                dve.tensor_tensor(blocks(a).rearrange("p b (n c) -> p b n c", c=C1),
                                  s[:, :, 0:D].rearrange("p b (n c) -> p b n c", c=C1), copies(z, 3, C1), ALU.mult).then_inc(vec, 1)
                dve.tensor_tensor(blocks(b), blocks(skip), copies(m.prod[:, D:2 * D], 1, GB), ALU.mult).then_inc(vec, 1)
                after(4)
                dve.tensor_tensor(blocks(c), blocks(a), copies(m.prod[:, 0:D], 1, GB), ALU.mult).then_inc(vec, 1)
                after(5)
                dve.tensor_tensor(b, b, c, ALU.add).then_inc(vec, 1)
                after(6)
                dve.tensor_reduce(logit, blocks(b), AX.X, ALU.add).then_inc(vec, 1)
                dve.tensor_tensor(c, skip, a, ALU.subtract).then_inc(vec, 1)
                after(8)
                dve.tensor_tensor(a, a, m.x[:, ds(g * GN, GN)], ALU.add).then_inc(vec, 1)
                dve.wait_ge(gate, g + 1)
                dve.tensor_tensor(blocks(c), blocks(c), copies(beta, 2, P), ALU.mult).then_inc(vec, 1)
                after(10)
                dve.tensor_tensor(b, c, a, ALU.add).then_inc(vec, 1)
                after(11)
                normalize(dve, m, m.stage_b, m.stage_b, stats, summing, root, rooted, inverted, lned, g)
                dve.wait_ge(projected, g + 1)
                dve.tensor_tensor(blocks(m.sums[:, ds(g * GN, GN)])[:, :, 0:HID], blocks(m.ps[:, 1024:1024 + GN])[:, :, 0:HID],
                                  copies(m.norm[:, ds(g * GB, GB)], 2, HID), ALU.mult).then_inc(placed, 1)

        @block.scalar
        def _(act):
            with act.Fori(0, GROUPS) as g:
                act.wait_ge(vec, g * steps + 2 + 7)
                act.activation(beta, logit, ACT.Sigmoid).then_inc(gate, 1)
                take_roots(act, m, root, stats, rooted, g)
                act.wait_ge(lned, g * GB + GB)
                act.activation(m.x[:, ds(g * GN, GN)], m.stage_b[:, :], ACT.Copy).then_inc(xed, 1)
                act.wait_ge(turned, g + 1)
                act.activation(m.stage_d[:, 0:GN], m.ps[:, 0:GN], ACT.Copy).then_inc(copied, 1)

        @block.tensor
        def _(pe):
            with pe.Fori(0, GROUPS) as g:
                pe.wait_ge(lned, g * GB + GB)
                turn_blocks(pe, m, 0, m.stage_b).then_inc(turned, 1)
                pe.wait_ge(copied, g + 1)
                for b in range(GB):
                    mm = pe.matmul(m.ps[:, 1024 + b * P:1024 + b * P + HID], m.stage_d[:, b * P:(b + 1) * P],
                                   m.w["g1"][:, 0, :], start=True, stop=True)
                mm.then_inc(projected, 1)

        store_sums(block, m, table, HID, placed, xed, stored, done)


def store_sums(block, m, table, f, placed, xed, stored, done):
    @block.sync
    def _(sp):
        with sp.Fori(0, GROUPS) as g:
            sp.wait_ge(placed, g + 1)
            if xed is not None:
                sp.wait_ge(xed, g + 1)
            sp.sem_inc(done, 1)
            sp.dma_start(group_rows(table, g), blocks(m.sums[:, ds(g * GN, GN)])[:, :, 0:f]).then_inc(stored, 16)
        sp.wait_ge(stored, 16 * GROUPS)


def gcn_step(nc, m, tag, weight, bias, f, table):
    with Phase(nc, tag, "scaled turned relued projected placed stored done") as (
            block, scaled, turned, relued, projected, placed, stored, done):

        @block.vector
        def _(dve):
            dve.sem_inc(done, 1)
            with dve.Fori(0, GROUPS) as g:
                s = blocks(m.sums[:, ds(g * GN, GN)])
                norm = m.norm[:, ds(g * GB, GB)]
                dve.wait_ge(done, g + 1)
                dve.tensor_tensor(blocks(m.stage_a[:, :])[:, :, 0:HID], s[:, :, 0:HID], copies(norm, 2, HID),
                                  ALU.mult).then_inc(scaled, 1)
                dve.wait_ge(projected, g + 1)
                dve.tensor_tensor(s[:, :, 0:f], blocks(m.ps[:, 1024:1024 + GN])[:, :, 0:f], copies(norm, 2, f),
                                  ALU.mult).then_inc(placed, 1)

        @block.tensor
        def _(pe):
            with pe.Fori(0, GROUPS) as g:
                pe.wait_ge(scaled, g + 1)
                turn_blocks(pe, m, 0, m.stage_a, HID).then_inc(turned, 1)
                pe.wait_ge(relued, g + 1)
                for b in range(GB):
                    mm = pe.matmul(m.ps[:, 1024 + b * P:1024 + b * P + f], m.stage_b[0:HID, b * P:(b + 1) * P],
                                   weight[0:HID, 0, :], start=True, stop=True)
                mm.then_inc(projected, 1)

        @block.scalar
        def _(act):
            with act.Fori(0, GROUPS) as g:
                act.wait_ge(turned, g + 1)
                act.activation(m.stage_b[0:HID, :], m.ps[0:HID, 0:GN], ACT.Relu, bias=bias[0:HID, :]).then_inc(relued, 1)

        store_sums(block, m, table, f, placed, None, stored, done)


def gcn_end(nc, m, table):
    with Phase(nc, "ge2", "vec stats summing rooted inverted lned xed placed stored done") as (
            block, vec, stats, summing, rooted, inverted, lned, xed, placed, stored, done):
        root = m.small[:, 330:330 + GB]
        steps = 3

        @block.vector
        def _(dve):
            dve.sem_inc(done, 1)
            with dve.Fori(0, GROUPS) as g:
                a, b = m.stage_a[:, :], m.stage_b[:, :]
                after = lambda n: dve.wait_ge(vec, g * steps + n)
                dve.wait_ge(done, g + 1)
                dve.tensor_tensor(blocks(a), blocks(m.sums[:, ds(g * GN, GN)]),
                                  copies(m.norm[:, ds(g * GB, GB)], 2, P), ALU.mult).then_inc(vec, 1)
                after(1)
                dve.tensor_tensor(blocks(a), blocks(a), copies(m.spread["c4"], 1, GB), ALU.add).then_inc(vec, 1)
                after(2)
                dve.scalar_tensor_tensor(b, a, 0.0, m.x[:, ds(g * GN, GN)], ALU.max, ALU.add).then_inc(vec, 1)
                after(3)
                normalize(dve, m, m.stage_b, m.stage_b, stats, summing, root, rooted, inverted, lned, g)
                dve.wait_ge(lned, g * GB + GB)
                dve.tensor_copy(m.gin_sums[:, ds(g * GN, GN)], b).then_inc(placed, 1)

        @block.scalar
        def _(act):
            with act.Fori(0, GROUPS) as g:
                take_roots(act, m, root, stats, rooted, g)
                act.wait_ge(lned, g * GB + GB)
                act.activation(m.x[:, ds(g * GN, GN)], m.stage_b[:, :], ACT.Copy).then_inc(xed, 1)

        @block.sync
        def _(sp):
            with sp.Fori(0, GROUPS) as g:
                sp.wait_ge(placed, g + 1)
                sp.wait_ge(xed, g + 1)
                sp.sem_inc(done, 1)
                sp.dma_start(group_rows(table, g), blocks(m.gin_sums[:, ds(g * GN, GN)])).then_inc(stored, 16)
            sp.wait_ge(stored, 16 * GROUPS)


def gin_step(nc, m, table):
    with Phase(nc, "gs3", "staged turned copied hidden relu0 relu1 projected biased placed stored done") as (
            block, staged, turned, copied, hidden, relu0, relu1, projected, biased, placed, stored, done):
        act0, act1 = m.stage_c[:, 0:GN], m.stage_c[:, GN:2 * GN]

        @block.scalar
        def _(act):
            act.sem_inc(done, 1)
            with act.Fori(0, GROUPS) as g:
                act.wait_ge(done, g + 1)
                act.activation(m.stage_a[:, :], m.gin_sums[:, ds(g * GN, GN)], ACT.Copy).then_inc(staged, 1)
                act.wait_ge(turned, g + 1)
                act.activation(m.stage_b[:, :], m.ps[:, 0:GN], ACT.Copy).then_inc(copied, 1)
                act.wait_ge(hidden, g * 2 + 1)
                act.activation(act0, m.ps[:, 1024:1024 + GN], ACT.Relu, bias=m.column["b1a"][:, 0:1]).then_inc(relu0, 1)

        @block.tensor
        def _(pe):
            pe.sem_inc(biased, 2)
            with pe.Fori(0, GROUPS) as g:
                pe.wait_ge(staged, g + 1)
                turn_blocks(pe, m, 0, m.stage_a).then_inc(turned, 1)
                pe.wait_ge(copied, g + 1)
                for o in range(2):
                    feature_product(pe, m, 2 + 2 * o, [(m.w["w1a"][:, 0, o * P:(o + 1) * P], m.stage_b)]).then_inc(hidden, 1)
                pe.wait_ge(relu0, g + 1)
                pe.wait_ge(relu1, g + 1)
                for b in range(GB):
                    out = gin_bank(m, b, 2 * D)
                    pe.wait_ge(biased, g * GB + b + 1)
                    pe.matmul(out, act0[:, b * P:(b + 1) * P], m.w["w1b"][:, 0, :], start=True, stop=False)
                    pe.matmul(out, act1[:, b * P:(b + 1) * P], m.w["w1b"][:, 1, :], start=False, stop=True).then_inc(projected, 1)

        @block.vector
        def _(dve):
            with dve.Fori(0, GROUPS) as g:
                s = m.sums[:, ds(g * 2 * GN, 2 * GN)]
                dve.wait_ge(hidden, g * 2 + 2)
                dve.tensor_scalar(act1, m.ps[:, 2048:2048 + GN], m.column["b1a"][:, 1:2], 0.0, ALU.add, ALU.max).then_inc(relu1, 1)
                for b in range(GB):
                    dve.wait_ge(projected, g * GB + b + 1)
                    dve.tensor_tensor(m.stage_d[:, b * 2 * D:(b + 1) * 2 * D], gin_bank(m, b, 2 * D), m.spread["b1b"],
                                      ALU.add).then_inc(biased, 1)
                dve.wait_ge(biased, g * GB + GB + 2)
                dve.tensor_scalar(s, m.stage_d, 0.0, None, ALU.max).then_inc(placed, 1)

        @block.sync
        def _(sp):
            with sp.Fori(0, GROUPS) as g:
                sp.wait_ge(placed, g + 1)
                sp.sem_inc(done, 1)
                sp.dma_start(group_rows(table, g), blocks(m.sums[:, ds(g * 2 * GN, 2 * GN)], 2 * D)).then_inc(stored, 16)
            sp.wait_ge(stored, 16 * GROUPS)


def gin_bank(m, b, n):
    return m.bank(6 + b % 2, n)


def gin_end(nc, m, out):
    with Phase(nc, "gf3", "staged turned copied0 copied1 hidden relu0 relu1 projected vec stats summing rooted inverted lned stored done") as (
            block, staged, turned, copied0, copied1, hidden, relu0, relu1, projected, vec, stats, summing, rooted, inverted,
            lned, stored, done):
        root = m.small[:, 330:330 + GB]
        steps = 2

        @block.scalar
        def _(act):
            act.sem_inc(done, 1)
            with act.Fori(0, GROUPS) as g:
                act.wait_ge(done, g + 1)
                act.activation(m.stage_c[:, :], m.sums[:, ds(g * 2 * GN, 2 * GN)], ACT.Copy).then_inc(staged, 1)
                act.wait_ge(turned, g * 2 + 1)
                act.activation(m.stage_d[:, 0:GN], m.ps[:, 0:GN], ACT.Copy).then_inc(copied0, 1)
                act.wait_ge(hidden, g * 2 + 1)
                act.activation(m.stage_a[:, :], m.ps[:, 2048:2048 + GN], ACT.Relu, bias=m.column["b2a"][:, 0:1]).then_inc(relu0, 1)
                take_roots(act, m, root, stats, rooted, g)

        @block.tensor
        def _(pe):
            with pe.Fori(0, GROUPS) as g:
                pe.wait_ge(staged, g + 1)
                for k in range(2):
                    for b in range(GB):
                        mm = pe.transpose(m.ps[:, 1024 * k + b * P:1024 * k + (b + 1) * P],
                                          m.stage_c[:, (2 * b + k) * P:(2 * b + k + 1) * P], m.ident[:, :])
                    mm.then_inc(turned, 1)
                pe.wait_ge(copied0, g + 1)
                pe.wait_ge(copied1, g + 1)
                for o in range(2):
                    feature_product(pe, m, 4 + 2 * o, [(m.w["w2a"][:, k, o * P:(o + 1) * P], m.stage_d[:, k * GN:(k + 1) * GN])
                                                       for k in range(2)]).then_inc(hidden, 1)
                pe.wait_ge(relu0, g + 1)
                pe.wait_ge(relu1, g + 1)
                for b in range(GB):
                    o = m.ps[:, b * P:(b + 1) * P]
                    pe.matmul(o, m.stage_a[:, b * P:(b + 1) * P], m.w["w2b"][:, 0, :], start=True, stop=False)
                    mm = pe.matmul(o, m.stage_b[:, b * P:(b + 1) * P], m.w["w2b"][:, 1, :], start=False, stop=True)
                mm.then_inc(projected, 1)

        @block.vector
        def _(dve):
            a, b = m.stage_a[:, :], m.stage_b[:, :]
            with dve.Fori(0, GROUPS) as g:
                dve.wait_ge(turned, g * 2 + 2)
                dve.tensor_copy(m.stage_d[:, GN:2 * GN], m.ps[:, 1024:1024 + GN]).then_inc(copied1, 1)
                dve.wait_ge(hidden, g * 2 + 2)
                dve.tensor_scalar(b, m.ps[:, 3072:3072 + GN], m.column["b2a"][:, 1:2], 0.0, ALU.add, ALU.max).then_inc(relu1, 1)
                dve.wait_ge(projected, g + 1)
                dve.tensor_tensor(blocks(a), blocks(m.ps[:, 0:GN]), copies(m.spread["b2b"], 1, GB), ALU.add).then_inc(vec, 1)
                dve.wait_ge(vec, g * steps + 1)
                dve.scalar_tensor_tensor(b, a, 0.0, m.x[:, ds(g * GN, GN)], ALU.max, ALU.add).then_inc(vec, 1)
                dve.wait_ge(vec, g * steps + 2)
                normalize(dve, m, m.stage_b, m.stage_c, stats, summing, root, rooted, inverted, lned, g)

        @block.sync
        def _(sp):
            with sp.Fori(0, GROUPS - 1) as g:
                sp.wait_ge(lned, g * GB + GB)
                sp.dma_start(group_rows(out, g), blocks(m.stage_c[:, 0:GN])).then_inc(stored, 16)
                sp.wait_ge(stored, g * 16 + 16)
                sp.sem_inc(done, 1)
            sp.wait_ge(lned, GROUPS * GB)
            first = (GROUPS - 1) * GN
            whole = (GB - 1) * P
            sp.dma_start(out[first:first + whole, :].rearrange("(b p) f -> p b f", p=P),
                         blocks(m.stage_c[:, 0:whole])).then_inc(stored, 16)
            sp.dma_start(out[first + whole:NODES, :], m.stage_c[0:LAST, whole:whole + P]).then_inc(stored, 16)
            sp.wait_ge(stored, 16 * (GROUPS + 1))


def clear_sums(nc, m, n):
    with Phase(nc, "cs", "zeroed") as (block, zeroed):
        @block.vector
        def _(dve):
            dve.memset(m.sums[:, 0:n], 0.0).then_inc(zeroed, 1)


def program(nc, t, out):
    tables = {n: nc.dram_tensor(f"table_{n}", (BLOCKS * P, f), F32, kind="Internal").ap() for n, f in
              (("kv", 2 * D), ("k", D), ("v", D), ("h1", HID), ("h2", HID), ("h3", HID), ("h4", D), ("x", D), ("g", 2 * D))}
    with ExitStack() as ctx:
        m = Memory(nc, ctx)
        plan(nc, m, t)
        project0(nc, m, t, tables["kv"])
        attend(nc, m, tables["kv"])
        attend_out(nc, m, t)
        feed_forward(nc, m)
        project1(nc, m, t, tables["k"], tables["v"])
        score(nc, m, tables["k"])
        softmax_rows(nc, m)
        softmax_weights(nc, m)
        clear_sums(nc, m, BLOCKS * A1)
        sum_values(nc, m, tables["v"])
        skip_gate(nc, m, tables["h1"])
        sum_rows(nc, m, "s1", tables["h1"], HID, m.sums, D)
        gcn_step(nc, m, "n1", m.w["g2"], m.column["c1"], HID, tables["h2"])
        sum_rows(nc, m, "s2", tables["h2"], HID, m.sums, D)
        gcn_step(nc, m, "n2", m.w["g3"], m.column["c2"], HID, tables["h3"])
        sum_rows(nc, m, "s3", tables["h3"], HID, m.sums, D)
        gcn_step(nc, m, "n3", m.w["g4"], m.column["c3"], D, tables["h4"])
        sum_rows(nc, m, "s4", tables["h4"], D, m.sums, D)
        gcn_end(nc, m, tables["x"])
        sum_rows(nc, m, "s5", tables["x"], D, m.gin_sums, D)
        gin_step(nc, m, tables["g"])
        sum_rows(nc, m, "s6", tables["g"], 2 * D, m.sums, 2 * D)
        gin_end(nc, m, out)


def kernel(**inputs):
    import numpy as np
    from concourse import bacc
    from concourse.bass_utils import run_bass_kernel_spmd

    i = {k: np.asarray(v) for k, v in inputs.items()}

    def padded(a, rows, fill):
        out = np.full((rows, *a.shape[1:]), fill, a.dtype)
        out[:a.shape[0]] = a
        return out

    x = padded(i["x"], BLOCKS * P, 0)
    g0, g1, g2, g3 = ({k[7:]: v for k, v in i.items() if k.startswith(f"L{n}_gnn_")} for n in range(4))
    columns = {"bo": g0["bo"], "b1": g0["b1"], "b2": g0["b2"], "n1w": g0["bn1_w"], "n1b": g0["bn1_b"],
               "n2w": g0["bn2_w"], "n2b": g0["bn2_b"], "c1": g2["b1"], "c2": g2["b2"], "c3": g2["b3"],
               "b1a": g3["b1a"], "b2a": g3["b2a"]}
    spread = {"bqkvs": np.concatenate([g1["bq"], g1["bk"], g1["bv"], g1["bskip"]]),
              "wbeta": g1["Wbeta"].reshape(-1), "c4": g2["b4"], "b1b": g3["b1b"], "b2b": g3["b2b"]}
    arrays = {
        "x": x, "xT": x.T,
        "src": padded(i["src"], COLS * P, 0).reshape(COLS, P),
        "dst": padded(i["dst"], COLS * P, NO_DST).reshape(COLS, P),
        "wqkv0": np.concatenate([g0["Wq"].T, g0["Wk"].T, g0["Wv"].T], axis=1),
        "wo": g0["Wo"].T, "w1": g0["W1"].T, "w2": g0["W2"].T,
        "wqkvs": np.concatenate([g1["Wq"], g1["Wk"], g1["Wv"], g1["Wskip"]], axis=1),
        "g1": g2["W1"], "g2": g2["W2"], "g3": g2["W3"], "g4": g2["W4"],
        "w1a": g3["W1a"], "w1b": g3["W1b"], "w2a": g3["W2a"], "w2b": g3["W2b"],
        "columns": np.concatenate([padded(columns[n], k * P, 0).reshape(k, P) for n, k in COLUMNS]).T,
        "spread": np.concatenate([spread[n] for n, _ in SPREAD]).reshape(1, -1),
    }
    arrays = {k: np.ascontiguousarray(v) for k, v in arrays.items()}
    nc = bacc.Bacc("TRN2", target_bir_lowering=False, num_devices=1)
    tensors = {k: nc.dram_tensor(f"in_{k}", v.shape, mybir.dt.from_np(v.dtype), kind="ExternalInput").ap()
               for k, v in arrays.items()}
    out = nc.dram_tensor("out", (NODES, D), F32, kind="ExternalOutput").ap()
    program(nc, tensors, out)
    result = run_bass_kernel_spmd(nc, [{f"in_{k}": v for k, v in arrays.items()}], core_ids=[0])
    return result.results[0]["out"]
```

```python
from contextlib import ExitStack

import concourse.bass as bass
from concourse import mybir

P = 128
NODES, EDGES, D = 6250, 100000, 128
BLOCKS = -(-NODES // P)
LAST = NODES - (BLOCKS - 1) * P
TILES = -(-EDGES // P)
GB = 7
GROUPS = BLOCKS // GB
GN = GB * P
HALF = 4
UNROLL = 2 * HALF
TURNS = -(-(TILES + BLOCKS - 1) // UNROLL)
STEPS = TURNS * UNROLL
ROWS = -(-TILES // P)
COLS = ROWS * P
assert BLOCKS == GROUPS * GB and STEPS + HALF <= COLS
NO_DST = 16384
BIG = 1e30
H0, C0 = 8, D // 8
H1, C1 = 4, D // 4
HID = 100
A0 = D + H0 + 1
A1 = D + H1
SC = COLS * H1

F32 = mybir.dt.float32
I32 = mybir.dt.int32
BF16 = mybir.dt.bfloat16
F16 = mybir.dt.float16
ALU = mybir.AluOpType
ACT = mybir.ActivationFunctionType
AX = mybir.AxisListType
ds = bass.ds

WIN = 8
WINDOWS = BLOCKS * P // WIN
SLOTS = P // WIN
WIDE = BLOCKS * WIN
WTURNS = -(-(TILES + WINDOWS - 1) // UNROLL)
WSTEPS = WTURNS * UNROLL
assert WTURNS % 2 == 0
WCOLS = 1664
assert WSTEPS < WCOLS and WCOLS % 4 == 0 and WCOLS // 4 <= 512 and SLOTS == 2 * UNROLL
SPARE = BLOCKS + 1
ADJ_BLOCKS = SPARE + -(-WSTEPS // SLOTS)
EXACT = 256
ARENA = 40200

WEIGHTS = [("wqkv0", 1, 3 * D), ("wo", 1, D), ("w1", 1, 2 * D), ("w2", 2, D), ("wqkvs", 1, 4 * D),
           ("g1", 1, HID), ("g2", 1, HID), ("g3", 1, HID), ("g4", 1, D),
           ("w1a", 1, 2 * D), ("w1b", 2, 2 * D), ("w2a", 2, 2 * D), ("w2b", 2, D)]
COLUMNS = [("bo", 1), ("b1", 2), ("b2", 1), ("n1w", 1), ("n1b", 1), ("n2w", 1), ("n2b", 1),
           ("c1", 1), ("c2", 1), ("c3", 1), ("b1a", 2), ("b2a", 2)]
SPREAD = [("bqkvs", 4 * D), ("wbeta", 3 * D), ("c4", D), ("b1b", 2 * D), ("b2b", D)]


class Memory:

    def __init__(self, nc, ctx):
        def sb(name, n, dt=F32):
            return ctx.enter_context(nc.sbuf_tensor(name, [P, n], dt))

        def split(t, *shape):
            names = " ".join("abc"[:len(shape)])
            return t.rearrange(f"p ({names}) -> p {names}", **dict(zip("abc", shape)))

        self.x = sb("x", BLOCKS * D)
        arena = sb("arena", ARENA)
        self.used = 0

        def take(n, dt=F32):
            size = n if dt in (F32, I32) else -(-n // 2)
            part = arena[:, self.used:self.used + size]
            self.used += size
            assert self.used <= ARENA, self.used
            return part if dt == F32 else part.bitcast(dt)

        big = take(BLOCKS * A0 + BLOCKS * D)
        self.sums = big
        self.gin_sums = big[:, BLOCKS * A0:]
        self.q = big[:, BLOCKS * A0:]
        self.score = big[:, 0:SC]
        self.srow = split(big[:, SC:2 * SC], ROWS, H1, P)
        self.fwd = split(big[:, 2 * SC:3 * SC], ROWS, H1, P)
        self.bwd = split(big[:, 0:SC], ROWS, H1, P)
        self.weight = big[:, 9000:9000 + SC]
        self.x_scratch = split(self.q[:, 5000:5000 + ROWS * (P + 1)], ROWS, P + 1)
        self.feat = take(BLOCKS * P)
        rows = take(UNROLL * 2 * D)
        self.rows = split(rows, UNROLL, 2 * D)
        self.hit = split(take(UNROLL * P), 2, HALF, P)
        self.hitT = split(take(UNROLL * P), 2, HALF, P)
        self.prod = take(HALF * D)
        self.msg = split(take(2 * HALF * A0), 2, HALF, A0)
        self.raw = take(2 * HALF * H0)
        self.stage_a = take(GN)
        self.stage_b = take(GN)
        self.stage_c = take(2 * GN)
        self.stage_d = rows[:, 0:2 * GN]
        self.local = take(COLS)
        self.src = take(COLS, I32)
        self.idx = take(UNROLL, I32)
        self.block = take(COLS, I32)
        self.pick0 = take(COLS)
        self.pick1 = take(COLS)
        self.dst_rows = take(COLS)
        self.ring4 = split(take(4 * HALF * 2 * D), 4 * HALF, 2 * D)
        self.idx4 = take(4 * HALF, I32)
        self.hit4 = split(take(4 * HALF * P), 4, HALF, P)

        self.used = 0
        self.rows_i = take(2 * COLS, I32)
        self.rows_f = take(2 * COLS)
        self.wramp = take(WCOLS)
        self.wtile = take(WCOLS)
        self.window = take(WCOLS)
        self.wwork = [take(WCOLS) for _ in range(3)]
        self.wint = take(WCOLS, I32)
        self.lo = take(WCOLS)
        self.place = take(WCOLS)
        self.ring = take(WCOLS, I32)
        self.clean = take(WCOLS, I32)
        self.stores = take(3 * WCOLS, I32)
        self.out_slot, self.out_block, self.out_part = (self.stores[:, k:3 * WCOLS:3] for k in range(3))
        self.count_to = take(WIDE, F16)
        self.by_lo = split(take(2 * HALF * P, BF16), 2, HALF, P)
        self.by_place = split(take(2 * HALF * WIDE, BF16), 2, HALF, WIDE)
        self.counted = split(take(2 * HALF * WIDE, BF16), 2, HALF, WIDE)
        self.slots = take((SLOTS + 1) * WIDE, BF16)
        self.slots_as_f32 = self.slots.bitcast(F32)
        self.zeros = take(WIDE // 2)

        self.used = 0
        self.adj = [take(SLOTS * WIDE, BF16) for _ in range(3)]
        parts0 = take(BLOCKS * 3 * D, BF16)
        parts1 = take(BLOCKS * 6 * D, BF16)
        self.parts = [parts0, parts1]
        self.most = parts0[:, 0:SLOTS * WIDE]
        self.y = take(2 * D)
        self.yT = take(2 * D)
        self.hid = take(2 * D)
        self.h = take(2 * D)
        self.rest = take(2 * D)
        self.stats = take(6)
        self.root, self.inverse = take(1), take(1)
        self.w, at = {}, 0
        w = sb("w", sum(k * n for _, k, n in WEIGHTS))
        for name, k, n in WEIGHTS:
            self.w[name] = split(w[:, at:at + k * n], k, n)
            at += k * n
        self.column, at = {}, 0
        self.columns = col = sb("columns", sum(n for _, n in COLUMNS))
        for name, n in COLUMNS:
            self.column[name] = col[:, at:at + n]
            at += n
        self.spread, at = {}, 0
        self.spreads = spread = sb("spread", sum(n for _, n in SPREAD))
        for name, n in SPREAD:
            self.spread[name] = spread[:, at:at + n]
            at += n
        self.ident = sb("ident", P)
        self.identb = sb("identb", P, BF16)
        self.flag = sb("flag", 1, I32)
        self.ones = sb("ones", P)
        self.number = sb("number", P)
        self.tile_id = sb("tile_id", ROWS)
        self.small = sb("small", 512)
        self.eps = sb("eps", 1)
        self.mean_var, self.scale, self.shift = self.small[:, 360:362], self.small[:, 362:363], self.small[:, 363:364]
        self.norm = sb("norm", BLOCKS)
        self.x_scratch = split(self.q[:, 5000:5000 + ROWS * (P + 1)], ROWS, P + 1)
        self.gathered = [ctx.enter_context(nc.semaphore(f"gathered{k}")) for k in range(UNROLL)]
        self.gathered_before = 0
        self.stored_before = 0
        self.gathered4 = [ctx.enter_context(nc.semaphore(f"gathered4_{r}")) for r in range(4)]
        self.gathered4_before = 0
        self.pool_stored = [ctx.enter_context(nc.semaphore("pool_stored"))]
        self.ps = ctx.enter_context(nc.psum_tensor("ps", [P, 8 * 512], F32))

    def bank(self, k, n=512):
        return self.ps[:, 512 * k:512 * k + n]


class Where:

    def __init__(self, block, flag):
        self.block, self.flag = block, flag

    def guarded(self, program):
        def run(engine):
            flag = engine.value_load(self.flag[0:1, 0:1], min_val=0, max_val=1)
            with engine.If(flag > 0):
                program(engine)
        return run

    def vector(self, program):
        self.block.vector(self.guarded(program))

    def scalar(self, program):
        self.block.scalar(self.guarded(program))

    def tensor(self, program):
        self.block.tensor(self.guarded(program))

    def gpsimd(self, program):
        self.block.gpsimd(self.guarded(program))

    def sync(self, program):
        self.block.sync(self.guarded(program))


class Phase:
    flag = None

    def __init__(self, nc, tag, names, lasting=()):
        self.nc, self.names, self.lasting = nc, [f"{tag}_{n}" for n in names.split()], list(lasting)

    def __enter__(self):
        self.ctx = ExitStack()
        nc = self.nc
        sems = [self.ctx.enter_context(nc.semaphore(n)) for n in self.names]
        with nc.Block() as clear:
            @clear.sync
            def _(sp):
                for s in sems:
                    sp.sem_clear(s)
        self.block = self.ctx.enter_context(nc.Block())
        if Phase.flag is not None:
            self.block = Where(self.block, Phase.flag)
        return (self.block, *sems, *self.lasting)

    def __exit__(self, *a):
        return self.ctx.__exit__(*a)


def copies(ap, axis, n):
    ap = ap.unsqueeze(axis)
    shape = list(ap.shape)
    shape[axis] = n
    return ap.broadcast_to(shape)


def group_rows(table, g):
    return table[ds(g * GN, GN), :].rearrange("(b p) f -> p b f", p=P)


def load_blocks(engine, regs, m, first):
    engine.load(regs, m.block[0:1, ds(first, HALF)])
    return [engine.snap(r, min_val=0, max_val=BLOCKS - 1) for r in regs]


def wait(engine, sem, n):
    if not (isinstance(n, int) and n <= 0):
        engine.wait_ge(sem, n)


def registers(nc, engine, name, n=HALF):
    return [engine.alloc_register(f"{name}{k}") for k in range(n)]


def plan(nc, m, t, again=False):
    with Phase(nc, "plan2" if again else "plan", "rows_in params_in made conv ranked compared counted stepped based "
               "picked drawn done") as (
            block, rows_in, params_in, made, conv, ranked, compared, counted, stepped, based,
            picked, drawn, done):
        dst_i = m.stage_a[:, :].bitcast(I32)
        src_i = m.stage_b[:, :].bitcast(I32)
        src_f = m.stage_c[:, 0:COLS]
        ramp = m.stage_c[:, COLS:2 * COLS]
        tile_of = m.feat[:, 0:COLS]
        block_of = m.feat[:, COLS:2 * COLS]
        reached = m.feat[:, 2 * COLS:4 * COLS]
        rank = m.small[:, 0:ROWS]
        blk_i = m.small[:, 8:8 + ROWS].bitcast(I32)
        blk_f = m.small[:, 16:16 + ROWS]
        ints = m.rows.rearrange("p a b -> p (a b)")[:, 0:COLS + P + 8].bitcast(I32)
        part = m.small[:, 24:25]

        @block.sync
        def _(sp):
            sp.dma_start(dst_i.rearrange("p (j e) -> p j e", e=P),
                         t["dst"].rearrange("(j p) e -> p j e", p=P)).then_inc(rows_in, 16)
            sp.dma_start(src_i.rearrange("p (j e) -> p j e", e=P),
                         t["src"].rearrange("(j p) e -> p j e", p=P)).then_inc(rows_in, 16)
            if again:
                sp.wait_ge(rows_in, 32)
                return
            for name, k, n in WEIGHTS:
                r = min(P, t[name].shape[0])
                sp.dma_start(m.w[name][0:r, :, :], t[name].rearrange("(k p) n -> p k n", p=r)).then_inc(params_in, 16)
            sp.dma_start(m.columns[:, :], t["columns"]).then_inc(params_in, 16)
            sp.dma_start(m.spreads[:, :], t["spread"].broadcast_to([P, t["spread"].shape[1]])).then_inc(params_in, 16)
            sp.dma_start(m.x[:, :].rearrange("p (b f) -> p b f", f=D),
                         t["x"].rearrange("(b p) f -> p b f", p=P)).then_inc(params_in, 16)
            sp.wait_ge(params_in, 16 * (len(WEIGHTS) + 3))

        @block.gpsimd
        def _(pool):
            pool.iota(ints[:, 0:COLS], [[1, COLS]], base=0, channel_multiplier=0).then_inc(made, 1)
            pool.iota(ints[:, COLS:COLS + ROWS], [[P, ROWS]], base=0, channel_multiplier=1).then_inc(made, 1)
            pool.memset(m.ones[:, :], 1.0).then_inc(made, 1)

        @block.vector
        def _(dve):
            dve.wait_ge(made, 3)
            dve.tensor_copy(ramp, ints[:, 0:COLS]).then_inc(conv, 1)
            dve.tensor_copy(m.tile_id[:, :], ints[:, COLS:COLS + ROWS]).then_inc(conv, 1)
            dve.wait_ge(rows_in, 32)
            dve.tensor_copy(m.dst_rows[:, :], dst_i).then_inc(conv, 1)
            dve.tensor_copy(src_f, src_i).then_inc(conv, 1)
            dve.tensor_scalar(blk_i, dst_i[:, 0:COLS:P], 7, None, ALU.arith_shift_right).then_inc(conv, 1)
            dve.wait_ge(conv, 5)
            dve.tensor_copy(m.number[:, :], ramp[:, 0:P]).then_inc(ranked, 1)
            dve.tensor_copy(blk_f, blk_i).then_inc(ranked, 1)
            dve.tensor_scalar(m.ident[:, :], ramp[:, 0:P], m.tile_id[:, 0:1], None, ALU.is_equal).then_inc(ranked, 1)
            dve.wait_ge(ranked, 3)
            dve.tensor_tensor(rank, blk_f, m.tile_id[:, :], ALU.add).then_inc(ranked, 1)
            dve.wait_ge(ranked, 4)
            for j in range(ROWS):
                if j >= 2:
                    dve.wait_ge(counted, 2 * (j - 1))
                dve.tensor_scalar(reached[:, (j % 2) * COLS:(j % 2 + 1) * COLS], ramp, rank[:, j:j + 1],
                                  None, ALU.is_ge).then_inc(compared, 1)
            dve.wait_ge(counted, 2 * ROWS)
            for k in range(2):
                c = slice(k * COLS // 2, (k + 1) * COLS // 2)
                dve.tensor_scalar(tile_of[:, c], m.bank(k, COLS // 2), -1.0, 0.0, ALU.add, ALU.max).then_inc(stepped, 1)
            dve.wait_ge(stepped, 2)
            dve.tensor_tensor(block_of, ramp, tile_of, ALU.subtract).then_inc(based, 1)
            for j in range(ROWS):
                c = slice(j * P, (j + 1) * P)
                dve.tensor_scalar(m.pick0[:, c], tile_of[:, c], m.tile_id[:, j:j + 1], None, ALU.is_equal).then_inc(picked, 1)
                before = max(j - 1, 0)
                dve.tensor_scalar(m.pick1[:, c], tile_of[:, c], m.tile_id[:, before:before + 1],
                                  None, ALU.is_equal).then_inc(picked, 1)
            dve.wait_ge(based, 1)
            dve.tensor_scalar(block_of, block_of, -float(P), None, ALU.mult).then_inc(based, 1)
            dve.tensor_tensor(m.rows.rearrange("p a b -> p (a b)")[:, 0:COLS], ramp, tile_of, ALU.subtract).then_inc(based, 1)
            dve.wait_ge(based, 3)
            dve.tensor_scalar(m.block[:, :], m.rows.rearrange("p a b -> p (a b)")[:, 0:COLS], float(BLOCKS - 1),
                              None, ALU.min).then_inc(done, 1)
            dve.wait_ge(drawn, 2 * ROWS)
            for j in range(ROWS):
                c = slice(j * P, (j + 1) * P)
                dve.tensor_tensor(m.local[:, c], m.ps[:, 1024 + j * P:1024 + (j + 1) * P], block_of[:, c], ALU.add).then_inc(done, 1)
                dve.tensor_copy(m.src[:, c], m.ps[:, 2048 + j * P:2048 + (j + 1) * P]).then_inc(done, 1)

        @block.tensor
        def _(pe):
            for j in range(ROWS):
                pe.wait_ge(compared, j + 1)
                for k in range(2):
                    pe.matmul(m.bank(k, COLS // 2), m.ones[:, :],
                              reached[:, (j % 2) * COLS + k * COLS // 2:(j % 2) * COLS + (k + 1) * COLS // 2],
                              start=(j == 0), stop=(j == ROWS - 1)).then_inc(counted, 1)
            for j in range(ROWS):
                pe.wait_ge(picked, 2 * (j + 1))
                c = slice(j * P, (j + 1) * P)
                for at, rows in ((1024, m.dst_rows[:, :]), (2048, src_f)):
                    out = m.ps[:, at + j * P:at + (j + 1) * P]
                    mm = pe.matmul(out, rows[:, c], m.pick0[:, c], start=True, stop=(j == 0))
                    if j:
                        mm = pe.matmul(out, rows[:, (j - 1) * P:j * P], m.pick1[:, c], start=False, stop=True)
                    mm.then_inc(drawn, 1)


def gathers(pool, m, table, f, idx_copied, issued, free, gathered):
    with pool.Fori(0, TURNS) as i:
        for h in range(2):
            pool.wait_ge(free, 2 * i + h + 1)
            pool.tensor_copy(m.idx[:, h * HALF:(h + 1) * HALF],
                             m.src[:, ds(i * UNROLL + h * HALF, HALF)]).then_inc(idx_copied, 1)
            pool.wait_ge(idx_copied, 2 * i + h + 1)
            pool.sem_inc(issued, 1)
            for k in range(h * HALF, (h + 1) * HALF):
                pool.indirect_dma_start(m.rows[:, k, 0:f], None, table,
                                        bass.IndirectOffsetOnAxis(m.idx[:, k:k + 1], 0)).then_inc(gathered[k], 16)


def gathers4(pool, m, table, f, idx_copied, issued, free, gathered):
    with pool.Fori(0, TURNS // 2) as i:
        for r in range(4):
            pool.wait_ge(free, 4 * i + r + 1)
            pool.tensor_copy(m.idx4[:, r * HALF:(r + 1) * HALF],
                             m.src[:, ds(i * (4 * HALF) + r * HALF, HALF)]).then_inc(idx_copied, 1)
            pool.wait_ge(idx_copied, 4 * i + r + 1)
            pool.sem_inc(issued, 1)
            for k in range(HALF):
                pool.indirect_dma_start(m.ring4[:, r * HALF + k, 0:f], None, table,
                                        bass.IndirectOffsetOnAxis(m.idx4[:, r * HALF + k:r * HALF + k + 1], 0)).then_inc(gathered[r], 16)


def hits4(dve, m, r, first):
    return dve.tensor_tensor(m.hit4[:, r], copies(m.number[:, :], 1, HALF),
                             copies(m.local[:, ds(first, HALF)], 2, P), ALU.is_equal)


def hits(dve, m, h, first):
    return dve.tensor_tensor(m.hit[:, h], copies(m.number[:, :], 1, HALF),
                             copies(m.local[:, ds(first, HALF)], 2, P), ALU.is_equal)


def sum_rows(nc, m, tag, table, f, sums, width):
    with Phase(nc, tag, "idx_copied issued free used added hit_ready", m.gathered) as (
            block, idx_copied, issued, free, used, added, hit_ready, *gathered):
        before = m.gathered_before
        m.gathered_before += 16 * TURNS

        @block.gpsimd
        def _(pool):
            gathers(pool, m, table, f, idx_copied, issued, free, gathered)

        @block.tensor
        def _(pe):
            pe.sem_inc(free, 2)
            with pe.Fori(0, TURNS) as i:
                for h in range(2):
                    pe.wait_ge(hit_ready, 2 * i + h + 1)
                    for k in range(HALF):
                        slot = h * HALF + k
                        pe.wait_ge(gathered[slot], before + 16 * i + 16)
                        pe.wait_ge(added, i * UNROLL + slot + 1)
                        pe.matmul(m.bank(slot, f), m.hit[:, h, k, :], m.rows[:, slot, 0:f],
                                  start=True, stop=True).then_inc(used, 1)
                    pe.wait_ge(used, i * UNROLL + (h + 1) * HALF)
                    pe.sem_inc(free, 1)

        @block.vector
        def _(dve):
            regs = registers(nc, dve, tag)
            dve.sem_inc(added, UNROLL)
            with dve.Fori(0, TURNS) as i:
                for h in range(2):
                    hits(dve, m, h, i * UNROLL + h * HALF).then_inc(hit_ready, 1)
                for h in range(2):
                    at = load_blocks(dve, regs, m, i * UNROLL + h * HALF)
                    for k in range(HALF):
                        slot = h * HALF + k
                        to = sums[:, ds(at[k] * width, f)]
                        dve.wait_ge(used, i * UNROLL + slot + 1)
                        dve.wait_ge(added, UNROLL + i * UNROLL + slot)
                        dve.tensor_tensor(to, to, m.bank(slot, f), ALU.add).then_inc(added, 1)


def attend(nc, m, table):
    with Phase(nc, "at0", "idx_copied issued free used added hit_ready turned copied q_ready multiplied "
               "reduced clipped weights_ready weighted ones_in", m.gathered4) as (
            block, idx_copied, issued, free, used, added, hit_ready, turned, copied, q_ready, multiplied,
            reduced, clipped, weights_ready, weighted, ones_in, *gathered):
        before = m.gathered4_before
        m.gathered4_before += 64 * (TURNS // 2)
        raw = m.raw[:, :].rearrange("p (a n) -> p a n", a=2)

        @block.gpsimd
        def _(pool):
            gathers4(pool, m, table, 2 * D, idx_copied, issued, free, gathered)

        @block.tensor
        def _(pe):
            regs = registers(nc, pe, "at0pe")
            pe.sem_inc(free, 4)

            def products(j, r):
                pe.wait_ge(weighted, j + 1)
                for k in range(HALF):
                    pe.wait_ge(added, j * HALF + k + 1)
                    mm = pe.matmul(m.bank(k, A0), m.hit4[:, r, k, :], m.msg[:, r % 2, k, :], start=True, stop=True)
                    mm.then_inc(used, 1)
                pe.wait_ge(used, (j + 2) * HALF)
                pe.sem_inc(free, 1)

            def turn(j, r):
                pe.wait_ge(hit_ready, j + 1)
                wait(pe, copied, j - 1)
                for k in range(HALF):
                    mm = pe.transpose(m.bank(4 + r % 2)[:, k * P:(k + 1) * P], m.hit4[:, r, k, :], m.ident[:, :])
                mm.then_inc(turned, 1)

            def queries(j, h):
                at = load_blocks(pe, regs, m, j * HALF)
                pe.wait_ge(copied, j + 1)
                wait(pe, multiplied, j - 1)
                for k in range(HALF):
                    mm = pe.matmul(m.bank(6 + h)[:, k * P:(k + 1) * P], m.hitT[:, h, k, :],
                                   m.q[:, ds(at[k] * D, D)], start=True, stop=True)
                mm.then_inc(q_ready, 1)

            def half(j, r):
                turn(j + 2, (r + 2) % 4)
                products(j, r)
                queries(j + 2, r % 2)

            pe.sem_inc(used, HALF)
            turn(0, 0)
            turn(1, 1)
            queries(0, 0)
            queries(1, 1)
            for j in range(4):
                half(j, j)
            with pe.Fori(1, TURNS // 2) as i:
                for r in range(4):
                    half(4 * i + r, r)

        @block.scalar
        def _(act):
            def copy(j, h):
                act.wait_ge(turned, j + 1)
                wait(act, q_ready, j - 1)
                act.activation(m.hitT[:, h], m.bank(4 + h).rearrange("p (k n) -> p k n", k=HALF), ACT.Copy).then_inc(copied, 1)

            def exps(j, h):
                act.wait_ge(clipped, j + 1)
                wait(act, used, j * HALF)
                act.activation(m.msg[:, h, :, D:D + H0], raw[:, h].rearrange("p (k n) -> p k n", k=HALF),
                               ACT.Exp, scale=float(C0) ** -0.5).then_inc(weights_ready, 1)

            copy(0, 0)
            copy(1, 1)
            for j in range(2):
                exps(j, j)
                copy(j + 2, j)
            with act.Fori(1, TURNS) as i:
                for h in range(2):
                    exps(2 * i + h, h)
                    copy(2 * i + h + 2, h)

        @block.vector
        def _(dve):
            regs = registers(nc, dve, "at0dve")
            dve.memset(m.msg[:, :, :, D + H0:A0], 1.0).then_inc(ones_in, 1)
            dve.wait_ge(ones_in, 1)
            dve.sem_inc(added, HALF)

            def half(i, j, h, r, first=False):
                if not first:
                    at = load_blocks(dve, regs, m, (j - 1) * HALF)

                def add(k):
                    if first:
                        return
                    to = m.sums[:, ds(at[k] * A0, A0)]
                    dve.wait_ge(used, j * HALF + k + 1)
                    dve.wait_ge(added, j * HALF + k)
                    dve.tensor_tensor(to, to, m.bank(k, A0), ALU.add).then_inc(added, 1)

                rows = m.ring4[:, r * HALF:(r + 1) * HALF, :]
                dve.wait_ge(q_ready, j + 1)
                dve.wait_ge(gathered[r], before + 64 * i + 64)
                prod = m.prod[:, :].rearrange("p (k n) -> p k n", k=HALF)
                dve.tensor_tensor(prod, rows[:, :, 0:D],
                                  m.bank(6 + h).rearrange("p (k n) -> p k n", k=HALF), ALU.mult).then_inc(multiplied, 1)
                add(0)
                dve.wait_ge(multiplied, j + 1)
                dve.tensor_reduce(raw[:, h], m.prod[:, :].rearrange("p (n c) -> p n c", c=C0), AX.X, ALU.add).then_inc(reduced, 1)
                add(1)
                dve.wait_ge(reduced, j + 1)
                lim = 5.0 * float(C0) ** 0.5
                dve.tensor_scalar(raw[:, h], raw[:, h], lim, -lim, ALU.min, ALU.max).then_inc(clipped, 1)
                add(2)
                wait(dve, used, j * HALF)
                hits4(dve, m, (r + 2) % 4, (j + 2) * HALF).then_inc(hit_ready, 1)
                add(3)
                dve.wait_ge(weights_ready, j + 1)
                dve.tensor_tensor(m.msg[:, h, :, 0:D].rearrange("p k (n c) -> p k n c", c=C0),
                                  rows[:, :, D:2 * D].rearrange("p k (n c) -> p k n c", c=C0),
                                  copies(m.msg[:, h, :, D:D + H0], 3, C0), ALU.mult).then_inc(weighted, 1)

            hits4(dve, m, 0, 0).then_inc(hit_ready, 1)
            hits4(dve, m, 1, HALF).then_inc(hit_ready, 1)
            half(0, 0, 0, 0, True)
            for j in range(1, 4):
                half(0, j, j % 2, j)
            with dve.Fori(1, TURNS // 2) as i:
                for r in range(4):
                    half(i, 4 * i + r, r % 2, r)
            at = load_blocks(dve, regs, m, (2 * TURNS - 1) * HALF)
            for k in range(HALF):
                to = m.sums[:, ds(at[k] * A0, A0)]
                dve.wait_ge(used, 2 * TURNS * HALF + k + 1)
                dve.wait_ge(added, 2 * TURNS * HALF + k)
                dve.tensor_tensor(to, to, m.bank(k, A0), ALU.add).then_inc(added, 1)


def score(nc, m, table):
    with Phase(nc, "sc1", "idx_copied issued free hit_ready turned copied q_ready multiplied reduced", m.gathered) as (
            block, idx_copied, issued, free, hit_ready, turned, copied, q_ready, multiplied, reduced, *gathered):
        before = m.gathered_before
        m.gathered_before += 16 * TURNS

        @block.gpsimd
        def _(pool):
            gathers(pool, m, table, D, idx_copied, issued, free, gathered)

        @block.tensor
        def _(pe):
            regs = registers(nc, pe, "sc1pe")
            pe.sem_inc(free, 2)

            def queries(j, h, first=False):
                pe.wait_ge(hit_ready, j + 1)
                if not first:
                    pe.wait_ge(copied, j - 1)
                for k in range(HALF):
                    mm = pe.transpose(m.bank(4 + h)[:, k * P:(k + 1) * P], m.hit[:, h, k, :], m.ident[:, :])
                mm.then_inc(turned, 1)
                at = load_blocks(pe, regs, m, j * HALF)
                pe.wait_ge(copied, j + 1)
                if not first:
                    pe.wait_ge(multiplied, j - 1)
                for k in range(HALF):
                    mm = pe.matmul(m.bank(6 + h)[:, k * P:(k + 1) * P], m.hitT[:, h, k, :],
                                   m.q[:, ds(at[k] * D, D)], start=True, stop=True)
                mm.then_inc(q_ready, 1)

            queries(0, 0, True)
            queries(1, 1, True)
            with pe.Fori(1, TURNS) as i:
                queries(2 * i, 0)
                queries(2 * i + 1, 1)

        @block.scalar
        def _(act):
            def copy(j, h, first=False):
                act.wait_ge(turned, j + 1)
                if not first:
                    act.wait_ge(q_ready, j - 1)
                act.activation(m.hitT[:, h], m.bank(4 + h).rearrange("p (k n) -> p k n", k=HALF), ACT.Copy).then_inc(copied, 1)

            copy(0, 0, True)
            copy(1, 1, True)
            with act.Fori(1, TURNS) as i:
                copy(2 * i, 0)
                copy(2 * i + 1, 1)

        @block.vector
        def _(dve):
            prod = m.prod[:, :].rearrange("p (k n) -> p k n", k=HALF)

            def scores(i, j, h):
                dve.wait_ge(q_ready, j + 1)
                for k in range(HALF):
                    dve.wait_ge(gathered[h * HALF + k], before + 16 * i + 16)
                dve.tensor_tensor(prod, m.rows[:, h * HALF:(h + 1) * HALF, 0:D],
                                  m.bank(6 + h).rearrange("p (k n) -> p k n", k=HALF), ALU.mult).then_inc(multiplied, 1)
                dve.wait_ge(multiplied, j + 1)
                dve.sem_inc(free, 1)
                dve.tensor_reduce(m.score[:, ds(j * HALF * H1, HALF * H1)],
                                  m.prod[:, :].rearrange("p (n c) -> p n c", c=C1), AX.X, ALU.add).then_inc(reduced, 1)
                dve.wait_ge(reduced, j + 1)

            def next_hits(j, h):
                dve.wait_ge(turned, j)
                hits(dve, m, h, j * HALF).then_inc(hit_ready, 1)

            hits(dve, m, 0, 0).then_inc(hit_ready, 1)
            with dve.Fori(0, TURNS) as i:
                next_hits(2 * i + 1, 1)
                scores(i, 2 * i, 0)
                next_hits(2 * i + 2, 0)
                scores(i, 2 * i + 1, 1)
            dve.memset(m.score[:, STEPS * H1:SC], 0.0).then_inc(reduced, 1)


def sum_values(nc, m, table):
    with Phase(nc, "va1", "idx_copied issued free used added hit_ready weights_ready weighted", m.gathered) as (
            block, idx_copied, issued, free, used, added, hit_ready, weights_ready, weighted, *gathered):
        before = m.gathered_before
        m.gathered_before += 16 * TURNS

        @block.gpsimd
        def _(pool):
            gathers(pool, m, table, D, idx_copied, issued, free, gathered)

        @block.tensor
        def _(pe):
            pe.sem_inc(free, 2)
            with pe.Fori(0, TURNS) as i:
                for h in range(2):
                    j = 2 * i + h
                    pe.wait_ge(hit_ready, j + 1)
                    pe.wait_ge(weighted, j + 1)
                    pe.wait_ge(weights_ready, j + 1)
                    for k in range(HALF):
                        slot = h * HALF + k
                        pe.wait_ge(added, i * UNROLL + slot + 1)
                        pe.matmul(m.bank(slot, A1), m.hit[:, h, k, :], m.msg[:, h, k, 0:A1],
                                  start=True, stop=True).then_inc(used, 1)

        @block.scalar
        def _(act):
            with act.Fori(0, TURNS) as i:
                for h in range(2):
                    act.wait_ge(added, i * UNROLL + (h + 1) * HALF)
                    act.activation(m.msg[:, h, :, D:A1],
                                   m.weight[:, ds((i * UNROLL + h * HALF) * H1, HALF * H1)].rearrange("p (k n) -> p k n", n=H1),
                                   ACT.Copy).then_inc(weights_ready, 1)

        @block.vector
        def _(dve):
            regs = registers(nc, dve, "va1")
            dve.sem_inc(added, UNROLL)

            def weigh(i, j, h):
                hits(dve, m, h, j * HALF).then_inc(hit_ready, 1)
                for k in range(HALF):
                    dve.wait_ge(gathered[h * HALF + k], before + 16 * i + 16)
                dve.tensor_tensor(m.msg[:, h, :, 0:D].rearrange("p k (n c) -> p k n c", c=C1),
                                  m.rows[:, h * HALF:(h + 1) * HALF, 0:D].rearrange("p k (n c) -> p k n c", c=C1),
                                  copies(m.weight[:, ds(j * HALF * H1, HALF * H1)].rearrange("p (k n) -> p k n", n=H1), 3, C1),
                                  ALU.mult).then_inc(weighted, 1)
                dve.wait_ge(weighted, j + 1)
                dve.sem_inc(free, 1)

            def adds(j, h):
                at = load_blocks(dve, regs, m, j * HALF)
                for k in range(HALF):
                    to = m.sums[:, ds(at[k] * A1, A1)]
                    dve.wait_ge(used, j * HALF + k + 1)
                    dve.wait_ge(added, UNROLL + j * HALF + k)
                    dve.tensor_tensor(to, to, m.bank(h * HALF + k, A1), ALU.add).then_inc(added, 1)

            weigh(0, 0, 0)
            weigh(0, 1, 1)
            adds(0, 0)
            with dve.Fori(1, TURNS) as i:
                weigh(i, 2 * i, 0)
                adds(2 * i - 1, 1)
                weigh(i, 2 * i + 1, 1)
                adds(2 * i, 0)
            adds(2 * TURNS - 1, 1)


def softmax_rows(nc, m):
    with Phase(nc, "sr1", "turned copied placed taken") as (block, turned, copied, placed, taken):
        by_step = m.score.rearrange("p (s h) -> p h s", h=H1)
        turned_scores = m.stage_c[:, 0:H1 * P]
        turned_picks = m.stage_a[:, 0:2 * P]

        @block.tensor
        def _(pe):
            for j in range(ROWS):
                c = slice(j * P, (j + 1) * P)
                if j:
                    pe.wait_ge(copied, 2 * j)
                for h in range(H1):
                    pe.transpose(m.bank(0)[:, h * P:(h + 1) * P], by_step[:, h, c], m.ident[:, :])
                pe.transpose(m.bank(1)[:, 0:P], m.pick0[:, c], m.ident[:, :])
                pe.transpose(m.bank(1)[:, P:2 * P], m.pick1[:, c], m.ident[:, :]).then_inc(turned, 1)
                pe.wait_ge(copied, 2 * (j + 1))
                if j >= 2:
                    pe.wait_ge(taken, j - 1)
                pe.matmul(m.bank(2 + j % 2), turned_picks[:, 0:P], turned_scores, start=True,
                          stop=(j == ROWS - 1)).then_inc(placed, 1)
                if j:
                    pe.matmul(m.bank(2 + (j - 1) % 2), turned_picks[:, P:2 * P], turned_scores,
                              start=False, stop=True).then_inc(placed, 1)

        @block.scalar
        def _(act):
            for j in range(ROWS):
                act.wait_ge(turned, j + 1)
                if j:
                    act.wait_ge(placed, 2 * j - 1)
                act.activation(turned_scores, m.bank(0), ACT.Copy).then_inc(copied, 1)
                act.activation(turned_picks, m.bank(1, 2 * P), ACT.Copy).then_inc(copied, 1)

        @block.vector
        def _(dve):
            for j in range(ROWS):
                dve.wait_ge(placed, min(2 * (j + 2) - 1, 2 * ROWS - 1))
                dve.tensor_copy(m.srow[:, j], m.bank(2 + j % 2).rearrange("p (h e) -> p h e", h=H1)).then_inc(taken, 1)


def softmax_weights(nc, m):
    with Phase(nc, "sw1", "linked first ends turned rowed seven chained back backed second maxed exped drawn stored") as (
            block, linked, first, ends, turned, rowed, seven, chained, back, backed, second, maxed, exped, drawn, stored):
        links = m.x_scratch
        dst = m.dst_rows[:, :].rearrange("p (j e) -> p j e", e=P)
        ends_of = m.small[:, 0:ROWS * 4 * H1].rearrange("p (j q h) -> p j q h", q=4, h=H1)
        carried = m.small[:, 128:128 + ROWS * 2 * H1].rearrange("p (j q h) -> p j q h", q=2, h=H1)
        row = lambda t, a=0: t[0:H1, a:a + COLS]
        last_max, first_max = row(m.stage_a), row(m.stage_b)
        first_dst, last_dst = row(m.stage_c), row(m.stage_c, COLS)
        flat = m.hit.rearrange("p a k n -> p (a k n)")
        flat_t = m.hitT.rearrange("p a k n -> p (a k n)")
        flat_m = m.msg.rearrange("p a k n -> p (a k n)")
        cont, single = row(m.stage_d), row(m.stage_d, COLS)
        onward, backward, penalty = row(flat), row(flat_t), row(flat_m)

        def run(dve, starts, sem):
            for j in range(ROWS):
                for h in range(H1):
                    for to, q in ((m.fwd, 0), (m.bwd, 1)):
                        start = -BIG if starts is None else starts[:, j, q, h:h + 1]
                        if q == 0:
                            dve.tensor_tensor_scan(to[:, j, h, :], links[:, j, 0:P], m.srow[:, j, h, :], start,
                                                   ALU.add, ALU.max).then_inc(sem, 1)
                        else:
                            dve.tensor_tensor_scan(to[:, j, h, ::-1], links[:, j, P:0:-1], m.srow[:, j, h, ::-1], start,
                                                   ALU.add, ALU.max).then_inc(sem, 1)

        @block.vector
        def _(dve):
            dve.memset(links[:, :, 0:1], 0.0).then_inc(linked, 1)
            dve.memset(links[:, :, P:P + 1], 0.0).then_inc(linked, 1)
            dve.tensor_tensor(links[:, :, 1:P], dst[:, :, 1:P], dst[:, :, 0:P - 1], ALU.is_equal).then_inc(linked, 1)
            dve.wait_ge(linked, 3)
            dve.tensor_scalar(links[:, :, 1:P], links[:, :, 1:P], -1.0, BIG, ALU.add, ALU.mult).then_inc(linked, 1)
            dve.wait_ge(linked, 4)
            run(dve, None, first)
            dve.wait_ge(first, 2 * ROWS * H1)
            dve.tensor_copy(ends_of[:, :, 0, :], m.fwd[:, :, :, P - 1]).then_inc(ends, 1)
            dve.tensor_copy(ends_of[:, :, 1, :], m.bwd[:, :, :, 0]).then_inc(ends, 1)
            dve.tensor_copy(ends_of[:, :, 2, :], copies(dst[:, :, 0], 2, H1)).then_inc(ends, 1)
            dve.tensor_copy(ends_of[:, :, 3, :], copies(dst[:, :, P - 1], 2, H1)).then_inc(ends, 1)
            for q, to in enumerate((last_max, first_max, first_dst, last_dst)):
                dve.wait_ge(turned, q + 1)
                dve.tensor_copy(to, m.ps[0:H1, 1024 * q:1024 * q + COLS]).then_inc(rowed, 1)
            dve.wait_ge(rowed, 4)
            dve.memset(cont[:, 0:1], 0.0).then_inc(seven, 1)
            dve.tensor_tensor(cont[:, 1:COLS], first_dst[:, 1:COLS], last_dst[:, 0:COLS - 1], ALU.is_equal).then_inc(seven, 1)
            dve.tensor_tensor(single, first_dst, last_dst, ALU.is_equal).then_inc(seven, 1)
            dve.memset(backward[:, COLS - 1:COLS], 0.0).then_inc(seven, 1)
            dve.wait_ge(seven, 4)
            dve.tensor_tensor(onward, cont, single, ALU.mult).then_inc(seven, 1)
            dve.tensor_tensor(backward[:, 0:COLS - 1], cont[:, 1:COLS], single[:, 0:COLS - 1], ALU.mult).then_inc(seven, 1)
            dve.wait_ge(seven, 6)
            for t_, f_ in ((onward, onward), (backward, backward), (penalty, cont)):
                dve.tensor_scalar(t_, f_, -1.0, BIG, ALU.add, ALU.mult).then_inc(seven, 1)
            dve.wait_ge(seven, 9)
            dve.tensor_tensor_scan(onward, onward, last_max, -BIG, ALU.add, ALU.max).then_inc(chained, 1)
            dve.tensor_tensor_scan(backward[:, ::-1], backward[:, ::-1], first_max[:, ::-1], -BIG, ALU.add, ALU.max).then_inc(chained, 1)
            dve.wait_ge(chained, 2)
            dve.memset(last_max[:, 0:1], -BIG).then_inc(chained, 1)
            dve.memset(first_max[:, COLS - 1:COLS], -BIG).then_inc(chained, 1)
            dve.tensor_tensor(last_max[:, 1:COLS], onward[:, 0:COLS - 1], penalty[:, 1:COLS], ALU.add).then_inc(chained, 1)
            dve.tensor_tensor(first_max[:, 0:COLS - 1], backward[:, 1:COLS], penalty[:, 1:COLS], ALU.add).then_inc(chained, 1)
            dve.wait_ge(back, 1)
            dve.tensor_copy(m.small[:, 128:128 + ROWS * 2 * H1], m.ps[:, 0:ROWS * 2 * H1]).then_inc(backed, 1)
            dve.wait_ge(backed, 1)
            run(dve, carried, second)
            dve.wait_ge(second, 2 * ROWS * H1)
            for j in range(ROWS):
                dve.tensor_tensor(m.fwd[:, j], m.fwd[:, j], m.bwd[:, j], ALU.max).then_inc(maxed, 1)
            for j in range(ROWS):
                dve.wait_ge(maxed, j + 1)
                dve.tensor_tensor(m.srow[:, j], m.srow[:, j], m.fwd[:, j], ALU.subtract).then_inc(maxed, 1)
            for j in range(ROWS):
                dve.wait_ge(drawn, j + 1)
                dve.wait_ge(maxed, 2 * ROWS)
                dve.tensor_copy(m.weight[:, j * P * H1:(j + 1) * P * H1].rearrange("p (s h) -> p h s", h=H1),
                                m.bank(1 + j % 2).rearrange("p (h s) -> p h s", h=H1)).then_inc(stored, 1)

        @block.scalar
        def _(act):
            for j in range(ROWS):
                act.wait_ge(maxed, ROWS + j + 1)
                act.activation(m.srow[:, j], m.srow[:, j], ACT.Exp, scale=float(C1) ** -0.5).then_inc(exped, 1)

        @block.tensor
        def _(pe):
            pe.wait_ge(ends, 4)
            for q in range(4):
                for j in range(ROWS):
                    mm = pe.transpose(m.ps[0:H1, 1024 * q + j * P:1024 * q + (j + 1) * P], ends_of[:, j, q, :], m.ident[:, :])
                mm.then_inc(turned, 1)
            pe.wait_ge(chained, 6)
            pe.wait_ge(rowed, 4)
            for j in range(ROWS):
                for q, of in enumerate((last_max, first_max)):
                    mm = pe.transpose(m.ps[:, (2 * j + q) * H1:(2 * j + q + 1) * H1], of[:, j * P:(j + 1) * P], m.ident[0:H1, 0:H1])
            mm.then_inc(back, 1)
            for j in range(ROWS):
                pe.wait_ge(exped, j + 1)
                if j >= 2:
                    pe.wait_ge(stored, j - 1)
                for h in range(H1):
                    out = m.bank(1 + j % 2)[:, h * P:(h + 1) * P]
                    mm = pe.matmul(out, m.srow[:, j, h, :], m.pick0[:, j * P:(j + 1) * P], start=True, stop=(j == 0))
                    if j:
                        mm = pe.matmul(out, m.srow[:, j - 1, h, :], m.pick1[:, j * P:(j + 1) * P], start=False, stop=True)
                mm.then_inc(drawn, 1)


CHUNKS = ((0, 512), (512, GN))


def blocks(ap, n=P):
    return ap.rearrange("p (b n) -> p b n", n=n)


def turn_blocks(pe, m, bank, of, rows=P):
    for b in range(GB):
        out = m.ps[0:rows, 512 * bank + b * P:512 * bank + (b + 1) * P]
        mm = pe.transpose(out, of[:, b * P:b * P + rows], m.ident[:, :])
    return mm


def feature_product(pe, m, bank, pairs):
    for a, b in CHUNKS:
        for n, (w, x) in enumerate(pairs):
            mm = pe.matmul(m.ps[:, 512 * bank + a:512 * bank + b], w, x[:, a:b], start=(n == 0), stop=(n == len(pairs) - 1))
    return mm


def normalize(dve, m, at, to, stats, summing, root, rooted, inverted, step, g):
    six = m.small[:, 256:256 + 6 * GB].rearrange("p (b n) -> p b n", n=6)
    two = m.small[:, 304:304 + 2 * GB].rearrange("p (b n) -> p b n", n=2)
    std = m.small[:, 320:320 + GB]
    base = g * (2 * GB)
    for b in range(GB):
        dve.bn_stats(six[:, b, :], at[:, b * P:(b + 1) * P]).then_inc(stats, 1)
    dve.wait_ge(stats, base + GB)
    dve.sem_inc(summing, 1)
    for b in range(GB):
        dve.bn_aggr(two[:, b, :], six[:, b, :]).then_inc(stats, 1)
    dve.wait_ge(rooted, g + 1)
    dve.reciprocal(std, root).then_inc(inverted, 1)
    dve.wait_ge(inverted, g + 1)
    for b in range(GB):
        dve.tensor_scalar(to[:, b * P:(b + 1) * P], at[:, b * P:(b + 1) * P], two[:, b, 0:1], std[:, b:b + 1],
                          ALU.subtract, ALU.mult).then_inc(step, 1)


def take_roots(act, m, root, stats, rooted, g):
    two = m.small[:, 304:304 + 2 * GB].rearrange("p (b n) -> p b n", n=2)
    act.wait_ge(stats, g * (2 * GB) + 2 * GB)
    act.activation(root, two[:, :, 1], ACT.Sqrt, bias=m.eps[:, 0:1]).then_inc(rooted, 1)


def project0(nc, m, t, table):
    with Phase(nc, "pr0", "loaded projected dve_out act_out stage_free zeroed", m.pool_stored) as (
            block, loaded, projected, dve_out, act_out, stage_free, zeroed, stored):
        before = m.stored_before
        m.stored_before += 16 * GROUPS
        share = {0: (GB + 1) // 2, 1: GB // 2}

        @block.sync
        def _(sp):
            with sp.Fori(0, GROUPS) as g:
                sp.wait_ge(projected, g * GB + GB)
                sp.dma_start(m.stage_a[:, :], t["xT"][:, ds(g * GN, GN)]).then_inc(loaded, 16)

        @block.tensor
        def _(pe):
            pe.sem_inc(projected, GB)
            with pe.Fori(0, GROUPS) as g:
                pe.wait_ge(loaded, g * 16 + 16)
                for b in range(GB):
                    pe.wait_ge((dve_out, act_out)[b % 2], g * share[b % 2] + b // 2 + 1)
                    pe.matmul(m.bank(b, 3 * D), m.stage_a[:, b * P:(b + 1) * P], m.w["wqkv0"][:, 0, :],
                              start=True, stop=True).then_inc(projected, 1)

        @block.vector
        def _(dve):
            dve.sem_inc(dve_out, share[0])
            dve.memset(m.sums[:, 0:BLOCKS * A0], 0.0).then_inc(zeroed, 1)
            dve.memset(m.eps[:, :], 1e-5).then_inc(zeroed, 1)
            with dve.Fori(0, GROUPS) as g:
                dve.wait_ge(stage_free, g + 1)
                for b in range(0, GB, 2):
                    dve.wait_ge(projected, g * GB + GB + b + 1)
                    dve.tensor_copy(m.q[:, ds((g * GB + b) * D, D)], m.bank(b)[:, 0:D])
                    dve.tensor_copy(m.stage_c[:, b * 2 * D:(b + 1) * 2 * D], m.bank(b)[:, D:3 * D]).then_inc(dve_out, 1)

        @block.scalar
        def _(act):
            act.sem_inc(act_out, share[1])
            with act.Fori(0, GROUPS) as g:
                act.wait_ge(stage_free, g + 1)
                for b in range(1, GB, 2):
                    act.wait_ge(projected, g * GB + GB + b + 1)
                    act.activation(m.q[:, ds((g * GB + b) * D, D)], m.bank(b)[:, 0:D], ACT.Copy)
                    act.activation(m.stage_c[:, b * 2 * D:(b + 1) * 2 * D], m.bank(b)[:, D:3 * D], ACT.Copy).then_inc(act_out, 1)

        @block.gpsimd
        def _(pool):
            pool.sem_inc(stage_free, 1)
            with pool.Fori(0, GROUPS) as g:
                pool.wait_ge(dve_out, (g + 2) * share[0])
                pool.wait_ge(act_out, (g + 2) * share[1])
                pool.dma_start(group_rows(table, g), blocks(m.stage_c[:, :], 2 * D)).then_inc(stored, 16)
                pool.wait_ge(stored, before + g * 16 + 16)
                pool.sem_inc(stage_free, 1)


def batch_stats(dve, m, stats, weight, bias, rooted, scaled):
    n, parts = 250, NODES // 250
    six = m.small[:, 0:6 * parts].rearrange("p (b n) -> p b n", n=6)
    for b in range(parts):
        dve.bn_stats(six[:, b, :], m.feat[:, b * n:(b + 1) * n]).then_inc(stats, 1)
    dve.wait_ge(stats, parts)
    dve.bn_aggr(m.mean_var, m.small[:, 0:6 * parts]).then_inc(stats, 1)
    dve.wait_ge(rooted, 1)
    dve.reciprocal(m.scale, m.scale).then_inc(scaled, 1)
    dve.wait_ge(scaled, 1)
    dve.tensor_tensor(m.scale, m.scale, weight, ALU.mult).then_inc(scaled, 1)
    dve.wait_ge(scaled, 2)
    dve.tensor_tensor(m.shift, m.mean_var[:, 0:1], m.scale, ALU.mult).then_inc(scaled, 1)
    dve.wait_ge(scaled, 3)
    dve.tensor_tensor(m.shift, bias, m.shift, ALU.subtract).then_inc(scaled, 1)


def batch_root(act, m, stats, rooted):
    act.wait_ge(stats, NODES // 250 + 1)
    act.activation(m.scale, m.mean_var[:, 1:2], ACT.Sqrt, bias=m.eps[:, 0:1]).then_inc(rooted, 1)


def attend_out(nc, m, t):
    with Phase(nc, "ao0", "loaded inv scaled_in turned copied out done degs rooted2 stats rooted scaled") as (
            block, loaded, inv, scaled_in, turned, copied, out, done, degs, rooted2, stats, rooted, scaled):
        z = blocks(m.small[:, 200:200 + GB * H0], H0)
        deg = m.small[:, 400:400 + BLOCKS]

        @block.sync
        def _(sp):
            with sp.Fori(0, GROUPS) as g:
                sp.wait_ge(done, g + 1)
                sp.dma_start(m.stage_c[:, 0:GN], t["xT"][:, ds(g * GN, GN)]).then_inc(loaded, 16)

        @block.vector
        def _(dve):
            dve.sem_inc(done, 1)
            with dve.Fori(0, GROUPS) as g:
                s = blocks(m.sums[:, ds(g * (GB * A0), GB * A0)], A0)
                dve.tensor_scalar(z, s[:, :, D:D + H0], 1e-6, None, ALU.add).then_inc(inv, 1)
                dve.wait_ge(inv, g * 2 + 1)
                dve.reciprocal(z, z).then_inc(inv, 1)
                dve.wait_ge(inv, g * 2 + 2)
                dve.tensor_tensor(blocks(m.stage_a[:, :]).rearrange("p b (n c) -> p b n c", c=C0),
                                  s[:, :, 0:D].rearrange("p b (n c) -> p b n c", c=C0), copies(z, 3, C0),
                                  ALU.mult).then_inc(scaled_in, 1)
                dve.wait_ge(out, g + 1)
                dve.wait_ge(loaded, g * 16 + 16)
                dve.scalar_tensor_tensor(m.feat[:, ds(g * GN, GN)], m.ps[:, 1024:1024 + GN], m.column["bo"],
                                         m.stage_c[:, 0:GN], ALU.add, ALU.add).then_inc(done, 1)
            dve.tensor_scalar(deg, blocks(m.sums[:, 0:BLOCKS * A0], A0)[:, :, A0 - 1], 1.0, None, ALU.add).then_inc(degs, 1)
            dve.wait_ge(rooted2, 1)
            dve.reciprocal(m.norm[:, :], m.norm[:, :]).then_inc(degs, 1)
            dve.wait_ge(done, GROUPS + 1)
            batch_stats(dve, m, stats, m.column["n1w"], m.column["n1b"], rooted, scaled)

        @block.tensor
        def _(pe):
            with pe.Fori(0, GROUPS) as g:
                pe.wait_ge(scaled_in, g + 1)
                turn_blocks(pe, m, 0, m.stage_a).then_inc(turned, 1)
                pe.wait_ge(copied, g + 1)
                feature_product(pe, m, 2, [(m.w["wo"][:, 0, :], m.stage_b)]).then_inc(out, 1)

        @block.scalar
        def _(act):
            with act.Fori(0, GROUPS) as g:
                act.wait_ge(turned, g + 1)
                act.activation(m.stage_b[:, :], m.ps[:, 0:GN], ACT.Copy).then_inc(copied, 1)
            act.wait_ge(degs, 1)
            act.activation(m.norm[:, :], deg, ACT.Sqrt).then_inc(rooted2, 1)
            batch_root(act, m, stats, rooted)


def feed_forward(nc, m):
    with Phase(nc, "ff0", "normed hidden relu0 relu1 out done stats rooted scaled") as (
            block, normed, hidden, relu0, relu1, out, done, stats, rooted, scaled):
        act0, act1 = m.stage_c[:, 0:GN], m.stage_c[:, GN:2 * GN]

        @block.scalar
        def _(act):
            act.sem_inc(done, 1)
            with act.Fori(0, GROUPS) as g:
                act.wait_ge(done, g + 1)
                act.activation(m.stage_a[:, :], m.feat[:, ds(g * GN, GN)], ACT.Identity,
                               bias=m.shift, scale=m.scale).then_inc(normed, 1)
                act.wait_ge(hidden, g * 2 + 1)
                act.activation(act0, m.ps[:, 0:GN], ACT.Relu, bias=m.column["b1"][:, 0:1]).then_inc(relu0, 1)
            batch_root(act, m, stats, rooted)

        @block.tensor
        def _(pe):
            with pe.Fori(0, GROUPS) as g:
                pe.wait_ge(normed, g + 1)
                for o in range(2):
                    feature_product(pe, m, 2 * o, [(m.w["w1"][:, 0, o * P:(o + 1) * P], m.stage_a)]).then_inc(hidden, 1)
                pe.wait_ge(relu0, g + 1)
                pe.wait_ge(relu1, g + 1)
                feature_product(pe, m, 4, [(m.w["w2"][:, 0, :], act0), (m.w["w2"][:, 1, :], act1)]).then_inc(out, 1)

        @block.vector
        def _(dve):
            with dve.Fori(0, GROUPS) as g:
                dve.wait_ge(hidden, g * 2 + 2)
                dve.tensor_scalar(act1, m.ps[:, 1024:1024 + GN], m.column["b1"][:, 1:2], 0.0, ALU.add, ALU.max).then_inc(relu1, 1)
                dve.wait_ge(out, g + 1)
                dve.scalar_tensor_tensor(m.feat[:, ds(g * GN, GN)], m.ps[:, 2048:2048 + GN], m.column["b2"],
                                         m.stage_a[:, :], ALU.add, ALU.add).then_inc(done, 1)
            dve.wait_ge(done, GROUPS + 1)
            batch_stats(dve, m, stats, m.column["n2w"], m.column["n2b"], rooted, scaled)


def project1(nc, m, t, keys, values):
    with Phase(nc, "pr1", "normed turned added stats summing rooted inverted lned turned2 copied2 xed projected "
               "evened evac stage_free done kept", m.pool_stored) as (
            block, normed, turned, added, stats, summing, rooted, inverted, lned, turned2, copied2, xed, projected,
            evened, evac, stage_free, done, kept, stored):
        before = m.stored_before
        m.stored_before += 32 * GROUPS
        root = m.small[:, 330:330 + GB]

        @block.scalar
        def _(act):
            act.sem_inc(done, 1)
            with act.Fori(0, GROUPS) as g:
                act.wait_ge(done, g + 1)
                act.activation(m.stage_a[:, :], m.feat[:, ds(g * GN, GN)], ACT.Identity,
                               bias=m.shift, scale=m.scale).then_inc(normed, 1)
                take_roots(act, m, root, stats, rooted, g)
                act.wait_ge(lned, g * GB + GB)
                act.activation(m.x[:, ds(g * GN, GN)], m.stage_b[:, :], ACT.Copy).then_inc(xed, 1)
                act.wait_ge(turned2, g + 1)
                act.activation(m.stage_a[:, :], m.ps[:, 1024:1024 + GN], ACT.Copy).then_inc(copied2, 1)
                act.wait_ge(xed, g + 1)
                act.wait_ge(evac, g * 3 * GB + 3 * GB)
                act.wait_ge(stage_free, g + 1)
                act.sem_inc(done, 1)

        @block.tensor
        def _(pe):
            pe.sem_inc(evened, 4)
            with pe.Fori(0, GROUPS) as g:
                pe.wait_ge(normed, g + 1)
                turn_blocks(pe, m, 0, m.stage_a).then_inc(turned, 1)
                pe.wait_ge(lned, g * GB + GB)
                turn_blocks(pe, m, 2, m.stage_b).then_inc(turned2, 1)
                pe.wait_ge(copied2, g + 1)
                for b in range(GB):
                    if b >= 4:
                        pe.wait_ge(evac, g * 3 * GB + 3 * (b - 3))
                    pe.matmul(m.bank(4 + b % 4), m.stage_a[:, b * P:(b + 1) * P], m.w["wqkvs"][:, 0, :],
                              start=True, stop=True).then_inc(projected, 1)

        @block.vector
        def _(dve):
            with dve.Fori(0, GROUPS) as g:
                dve.wait_ge(turned, g + 1)
                dve.tensor_tensor(m.stage_b[:, :], m.ps[:, 0:GN], m.x[:, ds(g * GN, GN)], ALU.add).then_inc(added, 1)
                dve.wait_ge(added, g + 1)
                normalize(dve, m, m.stage_b, m.stage_b, stats, summing, root, rooted, inverted, lned, g)
                bias = m.spread["bqkvs"]
                for b in range(GB):
                    dve.wait_ge(projected, g * GB + b + 1)
                    ps = m.bank(4 + b % 4)
                    at = (g * GB + b) * D
                    dve.tensor_tensor(m.q[:, ds(at, D)], ps[:, 0:D], bias[:, 0:D], ALU.add).then_inc(evac, 1)
                    dve.tensor_tensor(m.stage_c[:, b * 2 * D:(b + 1) * 2 * D], ps[:, D:3 * D], bias[:, D:3 * D],
                                      ALU.add).then_inc(evac, 1)
                    dve.tensor_tensor(m.feat[:, ds(at, D)], ps[:, 3 * D:4 * D], bias[:, 3 * D:4 * D], ALU.add).then_inc(evac, 1)

        @block.gpsimd
        def _(pool):
            kv = blocks(m.stage_c[:, :], 2 * D)
            with pool.Fori(0, GROUPS) as g:
                pool.wait_ge(evac, g * 3 * GB + 3 * GB)
                pool.dma_start(group_rows(keys, g), kv[:, :, 0:D]).then_inc(stored, 16)
                pool.dma_start(group_rows(values, g), kv[:, :, D:2 * D]).then_inc(stored, 16)
                pool.wait_ge(stored, before + g * 32 + 32)
                pool.sem_inc(stage_free, 1)


def skip_gate(nc, m, table):
    with Phase(nc, "sg1", "vec gate stats summing rooted inverted lned turned copied xed projected placed stored done") as (
            block, vec, gate, stats, summing, rooted, inverted, lned, turned, copied, xed, projected, placed, stored, done):
        root = m.small[:, 330:330 + GB]
        z = blocks(m.small[:, 200:200 + GB * H1], H1)
        logit, beta = m.small[:, 340:340 + GB], m.small[:, 350:350 + GB]
        wbeta = m.spread["wbeta"]
        steps = 11

        @block.vector
        def _(dve):
            dve.tensor_tensor(m.prod[:, 0:D], wbeta[:, 0:D], wbeta[:, 2 * D:3 * D], ALU.add).then_inc(vec, 1)
            dve.tensor_tensor(m.prod[:, D:2 * D], wbeta[:, D:2 * D], wbeta[:, 2 * D:3 * D], ALU.subtract).then_inc(vec, 1)
            dve.sem_inc(done, 1)
            with dve.Fori(0, GROUPS) as g:
                s = blocks(m.sums[:, ds(g * (GB * A1), GB * A1)], A1)
                skip = m.feat[:, ds(g * GN, GN)]
                a, b, c = m.stage_a[:, :], m.stage_b[:, :], m.stage_c[:, 0:GN]
                after = lambda n: dve.wait_ge(vec, g * steps + 2 + n)
                after(0)
                dve.wait_ge(done, g + 1)
                dve.tensor_scalar(z, s[:, :, D:A1], 1e-16, None, ALU.max).then_inc(vec, 1)
                after(1)
                dve.reciprocal(z, z).then_inc(vec, 1)
                after(2)
                dve.tensor_tensor(blocks(a).rearrange("p b (n c) -> p b n c", c=C1),
                                  s[:, :, 0:D].rearrange("p b (n c) -> p b n c", c=C1), copies(z, 3, C1), ALU.mult).then_inc(vec, 1)
                dve.tensor_tensor(blocks(b), blocks(skip), copies(m.prod[:, D:2 * D], 1, GB), ALU.mult).then_inc(vec, 1)
                after(4)
                dve.tensor_tensor(blocks(c), blocks(a), copies(m.prod[:, 0:D], 1, GB), ALU.mult).then_inc(vec, 1)
                after(5)
                dve.tensor_tensor(b, b, c, ALU.add).then_inc(vec, 1)
                after(6)
                dve.tensor_reduce(logit, blocks(b), AX.X, ALU.add).then_inc(vec, 1)
                dve.tensor_tensor(c, skip, a, ALU.subtract).then_inc(vec, 1)
                after(8)
                dve.tensor_tensor(a, a, m.x[:, ds(g * GN, GN)], ALU.add).then_inc(vec, 1)
                dve.wait_ge(gate, g + 1)
                dve.tensor_tensor(blocks(c), blocks(c), copies(beta, 2, P), ALU.mult).then_inc(vec, 1)
                after(10)
                dve.tensor_tensor(b, c, a, ALU.add).then_inc(vec, 1)
                after(11)
                normalize(dve, m, m.stage_b, m.stage_b, stats, summing, root, rooted, inverted, lned, g)
                dve.wait_ge(projected, g + 1)
                dve.tensor_tensor(blocks(m.sums[:, ds(g * GN, GN)])[:, :, 0:HID], blocks(m.ps[:, 1024:1024 + GN])[:, :, 0:HID],
                                  copies(m.norm[:, ds(g * GB, GB)], 2, HID), ALU.mult).then_inc(placed, 1)

        @block.scalar
        def _(act):
            with act.Fori(0, GROUPS) as g:
                act.wait_ge(vec, g * steps + 2 + 7)
                act.activation(beta, logit, ACT.Sigmoid).then_inc(gate, 1)
                take_roots(act, m, root, stats, rooted, g)
                act.wait_ge(lned, g * GB + GB)
                act.activation(m.x[:, ds(g * GN, GN)], m.stage_b[:, :], ACT.Copy).then_inc(xed, 1)
                act.wait_ge(turned, g + 1)
                act.activation(m.stage_d[:, 0:GN], m.ps[:, 0:GN], ACT.Copy).then_inc(copied, 1)

        @block.tensor
        def _(pe):
            with pe.Fori(0, GROUPS) as g:
                pe.wait_ge(lned, g * GB + GB)
                turn_blocks(pe, m, 0, m.stage_b).then_inc(turned, 1)
                pe.wait_ge(copied, g + 1)
                for b in range(GB):
                    mm = pe.matmul(m.ps[:, 1024 + b * P:1024 + b * P + HID], m.stage_d[:, b * P:(b + 1) * P],
                                   m.w["g1"][:, 0, :], start=True, stop=True)
                mm.then_inc(projected, 1)

        store_sums(block, m, table, HID, placed, xed, stored, done)


def plan_windows(nc, m, t, x_table):
    with Phase(nc, "pw", "rows_in made vec compared counted picked drawn kept") as (
            block, rows_in, made, vec, compared, counted, picked, drawn, kept):
        dst_i, src_i = m.rows_i[:, 0:COLS], m.rows_i[:, COLS:2 * COLS]
        dst_f, src_f = m.rows_f[:, 0:COLS], m.rows_f[:, COLS:2 * COLS]
        q = WCOLS // 4
        two = m.wwork[0:2]
        a, b, c = m.wwork
        rank, first_i, first_f = m.small[:, 0:ROWS], m.small[:, 8:8 + ROWS].bitcast(I32), m.small[:, 16:16 + ROWS]
        ps4 = lambda k: m.ps[:, 2048 * k:2048 * (k + 1)].rearrange("p (n q) -> p n q", n=4)[:, :, 0:q]
        by4 = lambda x: x.rearrange("p (n q) -> p n q", n=4)

        @block.sync
        def _(sp):
            for to, name in ((dst_i, "dst"), (src_i, "src")):
                sp.dma_start(to.rearrange("p (j e) -> p j e", e=P),
                             t[name].rearrange("(j p) e -> p j e", p=P)).then_inc(rows_in, 16)
            sp.dma_start(x_table.rearrange("(b p) f -> p b f", p=P), blocks(m.x[:, :])).then_inc(kept, 16)
            sp.wait_ge(rows_in, 32)
            sp.wait_ge(kept, 16)

        @block.gpsimd
        def _(pool):
            pool.iota(m.wint, [[1, WCOLS]], base=0, channel_multiplier=0).then_inc(made, 1)
            pool.memset(m.zeros, 0.0).then_inc(made, 1)
            pool.memset(m.slots, 0.0).then_inc(made, 1)

        @block.vector
        def _(dve):
            n = 0

            def then(op):
                nonlocal n
                n += 1
                op.then_inc(vec, 1)
                dve.wait_ge(vec, n)

            dve.wait_ge(made, 3)
            then(dve.tensor_copy(m.wramp, m.wint))
            dve.wait_ge(rows_in, 32)
            then(dve.tensor_copy(m.rows_f, m.rows_i))
            then(dve.tensor_scalar(first_i, dst_i[:, 0:COLS:P], WIN.bit_length() - 1, None, ALU.arith_shift_right))
            then(dve.tensor_copy(first_f, first_i))
            then(dve.tensor_tensor(rank, first_f, m.tile_id[:, :], ALU.add))
            then(dve.tensor_copy(m.count_to, m.wramp[:, 0:WIDE]))
            then(dve.tensor_copy(m.identb[:, :], m.ident[:, :]))
            for j in range(ROWS):
                if j >= 2:
                    dve.wait_ge(counted, 4 * (j - 1))
                dve.tensor_scalar(two[j % 2], m.wramp, rank[:, j:j + 1], None, ALU.is_ge).then_inc(compared, 1)
            dve.wait_ge(counted, 4 * ROWS)
            then(dve.tensor_scalar(by4(m.wtile), ps4(0), -1.0, 0.0, ALU.add, ALU.max))
            for j in range(ROWS):
                if j >= 2:
                    dve.wait_ge(drawn, j - 1)
                dve.tensor_scalar(two[j % 2], m.wtile, m.tile_id[:, j:j + 1], None, ALU.is_equal).then_inc(picked, 1)
            then(dve.tensor_tensor(m.window, m.wramp, m.wtile, ALU.subtract))
            dve.wait_ge(drawn, ROWS)
            then(dve.scalar_tensor_tensor(by4(a), by4(m.window), -float(WIN), ps4(0), ALU.mult, ALU.add))
            then(dve.tensor_copy(by4(m.wint), ps4(1)))
            then(dve.tensor_scalar(b, a, 0.0, None, ALU.is_ge))
            then(dve.scalar_tensor_tensor(b, a, float(WIN), b, ALU.is_lt, ALU.mult))
            then(dve.tensor_scalar(m.ring, m.wint, P - 1, None, ALU.bitwise_and))
            then(dve.tensor_copy(m.lo, m.ring))
            then(dve.tensor_scalar(m.ring, m.wint, P.bit_length() - 1, None, ALU.arith_shift_right))
            then(dve.tensor_copy(c, m.ring))
            then(dve.scalar_tensor_tensor(c, a, float(BLOCKS), c, ALU.mult, ALU.add))
            then(dve.scalar_tensor_tensor(c, c, 1.0, b, ALU.add, ALU.mult))
            then(dve.tensor_scalar(m.place, c, -1.0, None, ALU.add))
            then(dve.tensor_copy(m.wint, m.window))
            then(dve.tensor_scalar(m.ring, m.wint, SLOTS - 1, None, ALU.bitwise_and))
            then(dve.tensor_scalar(m.window, m.window, float(SLOTS // 2), None, ALU.add))
            then(dve.tensor_copy(m.out_slot, m.window))
            then(dve.tensor_scalar(m.clean, m.out_slot, SLOTS - 1, None, ALU.bitwise_and))
            then(dve.tensor_scalar(m.window, m.window, -float(SLOTS // 2), None, ALU.add))
            then(dve.memset(c, 0.0))
            then(dve.tensor_tensor(c[:, 0:WCOLS - 1], m.window[:, 1:WCOLS], m.window[:, 0:WCOLS - 1], ALU.subtract))

            def either(to, last, other):
                then(dve.tensor_tensor(a, last, other, ALU.subtract) if not isinstance(other, float)
                     else dve.tensor_scalar(a, last, -other, None, ALU.add))
                then(dve.tensor_tensor(a, a, c, ALU.mult))
                then(dve.tensor_tensor(to, a, other, ALU.add) if not isinstance(other, float)
                     else dve.tensor_scalar(to, a, other, None, ALU.add))

            slot_f, part_f = m.wtile, b
            then(dve.tensor_copy(slot_f, m.ring))
            either(m.out_slot, slot_f, float(SLOTS))
            then(dve.tensor_copy(m.out_block, m.wramp))
            then(dve.tensor_scalar(m.out_part, m.out_block, SLOTS - 1, None, ALU.bitwise_and))
            then(dve.tensor_copy(part_f, m.out_part))
            either(m.out_part, slot_f, part_f)
            then(dve.tensor_scalar(m.out_block, m.out_block, SLOTS.bit_length() - 1, None, ALU.arith_shift_right))
            then(dve.tensor_scalar(part_f, m.out_block, float(SPARE), None, ALU.add))
            then(dve.tensor_scalar(m.out_block, m.wint, SLOTS.bit_length() - 1, None, ALU.arith_shift_right))
            then(dve.tensor_copy(slot_f, m.out_block))
            either(m.out_block, slot_f, part_f)
            for table, size in ((m.ring, WIDE), (m.clean, WIDE // 2), (m.out_slot, WIDE), (m.out_part, WIDE), (m.out_block, P)):
                then(dve.tensor_scalar(table, table, float(size), None, ALU.mult))

        @block.tensor
        def _(pe):
            for j in range(ROWS):
                pe.wait_ge(compared, j + 1)
                for k in range(4):
                    pe.matmul(m.bank(k, q), m.ones[:, :], two[j % 2][:, k * q:(k + 1) * q],
                              start=(j == 0), stop=(j == ROWS - 1)).then_inc(counted, 1)
            for j in range(ROWS):
                pe.wait_ge(picked, j + 1)
                for k in range(8):
                    rows = (dst_f, src_f)[k // 4]
                    mm = pe.matmul(m.bank(k, q), rows[:, j * P:(j + 1) * P], two[j % 2][:, (k % 4) * q:(k % 4 + 1) * q],
                                   start=(j == 0), stop=(j == ROWS - 1))
                mm.then_inc(drawn, 1)


def load_steps(engine, regs, table, first, most):
    engine.load(regs, table[0:1, ds(first, len(regs))])
    return [engine.snap(r, min_val=0, max_val=most) for r in regs]


def count_edges(nc, m, adj):
    with Phase(nc, "ce", "hot product moved added cleaned stored0 stored1 stored2 stored3") as (
            block, hot, product, moved, added, cleaned, *stored):
        bank = lambda h, k: m.bank(h * HALF + k, WIDE)

        @block.vector
        def _(dve):
            regs = registers(nc, dve, "cedve", UNROLL)

            def one_hots(s, h, k):
                dve.tensor_scalar(m.by_lo[:, h, k, :], m.count_to[:, 0:P], m.lo[:, ds(s, 1)], None, ALU.is_equal)
                dve.tensor_scalar(m.by_place[:, h, k, :], m.count_to, m.place[:, ds(s, 1)], None,
                                  ALU.is_equal).then_inc(hot, 1)

            def half(j, h, at, first=False):
                if not first or j:
                    dve.wait_ge(product, j * HALF)
                for k in range(HALF):
                    s = j * HALF + k
                    one_hots(s + HALF, 1 - h, k)
                    if k % 2 == 0:
                        dve.wait_ge(moved, s + 2)
                    if k == 0 and not first:
                        dve.wait_ge(cleaned, (j - 1) * HALF)
                    if not first or s:
                        dve.wait_ge(added, s)
                    to = m.slots[:, ds(at[k], WIDE)]
                    dve.tensor_tensor(to, to, m.counted[:, h, k, :], ALU.add).then_inc(added, 1)

            for k in range(HALF):
                one_hots(k, 0, k)
            at = load_steps(dve, regs, m.ring, 0, (SLOTS - 1) * WIDE)
            half(0, 0, at, True)
            half(1, 1, at[HALF:], True)
            with dve.Fori(1, WTURNS) as i:
                at = load_steps(dve, regs, m.ring, i * UNROLL, (SLOTS - 1) * WIDE)
                half(2 * i, 0, at)
                half(2 * i + 1, 1, at[HALF:])

        @block.tensor
        def _(pe):
            def products(j, h, first=False):
                for k in range(HALF):
                    s = j * HALF + k
                    pe.wait_ge(hot, s + 1)
                    if not first:
                        pe.wait_ge(moved, s - UNROLL + 1)
                    pe.matmul(bank(h, k), m.by_lo[:, h, k, :], m.by_place[:, h, k, :], start=True, stop=True).then_inc(product, 1)

            products(0, 0, True)
            products(1, 1, True)
            with pe.Fori(1, WTURNS) as i:
                products(2 * i, 0)
                products(2 * i + 1, 1)

        @block.scalar
        def _(act):
            regs = registers(nc, act, "ceact", 4 * HALF)

            def half(j, h, at=None, whole=None, seen=None):
                if j is not None and not (isinstance(j, int) and j < 2):
                    act.wait_ge(added, (j - 1) * HALF)
                if whole is not None:
                    act.wait_ge(whole, seen)
                for k in range(HALF):
                    s = j * HALF + k
                    act.wait_ge(product, s + 1)
                    act.activation(m.counted[:, h, k, :], bank(h, k), ACT.Copy).then_inc(moved, 1)
                    if at is not None:
                        act.wait_ge(cleaned, s - HALF)
                        act.activation(m.slots_as_f32[:, ds(at[k], WIDE // 2)], m.zeros,
                                       ACT.Copy).then_inc(cleaned, 1)

            act.sem_inc(cleaned, HALF)
            half(0, 0)
            half(1, 1)
            at = load_steps(act, regs, m.clean, HALF, (SLOTS - 1) * WIDE // 2)
            half(2, 0, at)
            half(3, 1, at[HALF:], stored[0], 64)
            with act.Fori(1, WTURNS // 2) as i:
                at = load_steps(act, regs, m.clean, i * 4 * HALF - HALF, (SLOTS - 1) * WIDE // 2)
                for r in range(4):
                    half(4 * i + r, r % 2, at[r * HALF:], stored[(r + 1) % 4], 64 * (i + (r + 1) // 4))

        @block.sync
        def _(sp):
            regs = [sp.alloc_register(f"cesp{k}") for k in range(3 * HALF)]

            def half(j, r, first=False):
                sp.load(regs, m.stores[0:1, ds(j * 3 * HALF, 3 * HALF)])
                if not first:
                    sp.wait_ge(cleaned, (j - 2) * HALF + 1)
                for k in range(HALF):
                    slot, to_block, to_part = (sp.snap(v, min_val=0, max_val=most) for v, most in
                                               zip(regs[3 * k:3 * k + 3], (SLOTS * WIDE, (ADJ_BLOCKS - 1) * P, (SLOTS - 1) * WIDE)))
                    sp.wait_ge(added, j * HALF + k + 1)
                    sp.dma_start(adj[ds(to_block, P), ds(to_part, WIDE)],
                                 m.slots[:, ds(slot, WIDE)]).then_inc(stored[r], 16)

            for r in range(4):
                half(r, r, True)
            with sp.Fori(1, WTURNS // 2) as i:
                for r in range(4):
                    half(4 * i + r, r)
            for r in range(4):
                sp.wait_ge(stored[r], 64 * (WTURNS // 2))


def three_parts(then, dve, rows, rest, parts):
    then(dve.tensor_copy(parts[0], rows))
    then(dve.tensor_tensor(rest, rows, parts[0], ALU.subtract))
    then(dve.tensor_copy(parts[1], rest))
    then(dve.tensor_tensor(rest, rest, parts[1], ALU.subtract))
    then(dve.tensor_copy(parts[2], rest))


def first_parts(nc, m, table):
    with Phase(nc, "fp", "rows_in vec") as (block, rows_in, vec):
        rows = blocks(m.parts[1].bitcast(F32)[:, 0:BLOCKS * HID], HID)
        parts = m.parts[0][:, 0:BLOCKS * 3 * HID].rearrange("p (b t f) -> p b t f", t=3, f=HID)

        @block.sync
        def _(sp):
            sp.dma_start(rows, table.rearrange("(b p) f -> p b f", p=P)).then_inc(rows_in, 16)
            sp.wait_ge(rows_in, 16)

        @block.vector
        def _(dve):
            n = 0

            def then(op):
                nonlocal n
                n += 1
                op.then_inc(vec, 1)
                dve.wait_ge(vec, n)

            dve.wait_ge(rows_in, 16)
            three_parts(then, dve, rows, rows, [parts[:, :, t, :] for t in range(3)])


def dense(nc, m, tag, adj, kind, f, source, fn=None, target=None, weights=(), biases=(), check=False, out=None):
    halves = -(-f // D)
    fh = f // halves
    parts_in = m.parts[source]
    norm = kind in ("gcn", "gcn_end")
    end = kind in ("gcn_end", "gin_end")
    gin = kind in ("gin", "gin_end")
    turned_bank, hidden_bank, out_bank = m.bank(6, 2 * P), m.ps[:, 512 * 6 + 2 * P:512 * 7], m.bank(7, 2 * D)
    steps = {"gcn": 6, "gcn_end": 10, "gin": 7, "gin_end": 4}[kind]
    with Phase(nc, tag, "loaded0 loaded1 loaded2 multiplied checked summed scaled turned copied hidden relued projected vec "
               "aggregating aggregated rooted placed stored emptied peaked spotted flagged") as (
            block, loaded0, loaded1, loaded2, multiplied, checked, summed, scaled, turned, copied, hidden, relued, projected,
            vec, aggregating, aggregated, rooted, placed, stored, emptied, peaked, spotted, flagged):
        loaded = (loaded0, loaded1, loaded2)
        turns = BLOCKS // 3
        assert BLOCKS == 3 * turns + 1

        def every_block(engine, do):
            for k in range(3):
                do(k, k, 0)
            with engine.Fori(1, turns) as i:
                for k in range(3):
                    do(3 * i + k, k, i)
            do(BLOCKS - 1, 0, turns)

        @block.sync
        def _(sp):
            def load(b, k, i):
                wait(sp, multiplied, b - 2)
                if check:
                    wait(sp, checked, b - 2)
                rows = adj[b * P:(b + 1) * P, :] if isinstance(b, int) else adj[ds(b * P, P), :]
                sp.dma_start(m.adj[k], rows).then_inc(loaded[k], 16)
                if kind == "gin_end":
                    store(b - 3)

            def store(b):
                if isinstance(b, int) and b < 0:
                    return
                sp.wait_ge(placed, b + 1)
                if isinstance(b, int):
                    n = min(P, NODES - b * P)
                    sp.dma_start(out[b * P:b * P + n, :], m.x[0:n, b * P:(b + 1) * P]).then_inc(stored, 16)
                else:
                    sp.dma_start(out[ds(b * P, P), :], m.x[:, ds(b * P, P)]).then_inc(stored, 16)

            every_block(sp, load)
            if kind == "gin_end":
                for b in range(BLOCKS - 3, BLOCKS):
                    store(b)
                sp.wait_ge(stored, 16 * BLOCKS)

        @block.tensor
        def _(pe):
            def turn(b):
                pe.wait_ge(scaled if norm else summed, b + 1)
                for h in range(halves):
                    mm = pe.transpose(turned_bank[0:fh, h * P:(h + 1) * P], m.y[:, h * fh:(h + 1) * fh], m.ident[:, :])
                mm.then_inc(turned, 1)

            def hide(b):
                pe.wait_ge(copied, b + 1)
                for o in range(2):
                    for h in range(halves):
                        mm = pe.matmul(hidden_bank[:, o * P:(o + 1) * P], weights[0][:, h, o * P:(o + 1) * P],
                                       m.yT[:, h * P:(h + 1) * P], start=(h == 0), stop=(h == halves - 1))
                mm.then_inc(hidden, 1)

            def project(b):
                if gin:
                    pe.wait_ge(relued, 2 * b + 2)
                    for o in range(2):
                        mm = pe.matmul(out_bank[:, 0:fn], m.hid[:, o * P:(o + 1) * P], weights[1][:, o, :],
                                       start=(o == 0), stop=(o == 1))
                else:
                    pe.wait_ge(relued, b + 1)
                    mm = pe.matmul(out_bank[:, 0:fn], m.hid[0:f, 0:P], weights[0][0:f, 0, :], start=True, stop=True)
                mm.then_inc(projected, 1)

            own = {"gcn": {10: turn, 24: project}, "gcn_end": {}}.get(kind, {8: turn, 16: hide, 26: project})

            def multiply(b, k, i):
                pe.wait_ge(loaded[k], 16 * i + 16)
                wait(pe, summed, b - 2)
                for s in range(BLOCKS):
                    if s in own and not (isinstance(b, int) and b == 0):
                        own[s](b - 1)
                    here = m.adj[k][:, s:P * BLOCKS:BLOCKS]
                    for h in range(halves):
                        pe.matmul(m.bank(k * halves + h, 3 * fh), here,
                                  parts_in[:, s * 3 * f + h * 3 * fh:s * 3 * f + (h + 1) * 3 * fh], start=(s == 0), stop=False)
                for h in range(halves):
                    mm = pe.matmul(m.bank(k * halves + h, 3 * fh), m.identb[:, :],
                                   parts_in[:, ds(b * (3 * f) + h * 3 * fh, 3 * fh)], start=False, stop=True)
                mm.then_inc(multiplied, 1)

            every_block(pe, multiply)
            for s in own:
                own[s](BLOCKS - 1)
            if check:
                pe.wait_ge(peaked, 2)
                pe.matmul(m.bank(6, 1), m.ones[:, :], m.y[:, 0:1], start=True, stop=True).then_inc(spotted, 1)

        @block.scalar
        def _(act):
            def between(b, k, i):
                if kind == "gcn":
                    act.wait_ge(turned, b + 1)
                    act.activation(m.hid[0:f, 0:P], turned_bank[0:f, 0:P], ACT.Relu, bias=biases[0][0:f, :]).then_inc(relued, 1)
                if gin:
                    act.wait_ge(turned, b + 1)
                    act.activation(m.yT[:, 0:f], turned_bank[:, 0:f], ACT.Copy).then_inc(copied, 1)
                    act.wait_ge(hidden, b + 1)
                    for o in range(2):
                        act.activation(m.hid[:, o * P:(o + 1) * P], hidden_bank[:, o * P:(o + 1) * P], ACT.Relu,
                                       bias=biases[0][:, o:o + 1]).then_inc(relued, 1)
                if end:
                    act.wait_ge(aggregated, b + 1)
                    act.activation(m.root, m.mean_var[:, 1:2], ACT.Sqrt, bias=m.eps[:, 0:1]).then_inc(rooted, 1)

            every_block(act, between)

        @block.vector
        def _(dve):
            def finish(b, k, i):
                n = b * steps

                def then(op):
                    nonlocal n
                    n = n + 1
                    op.then_inc(vec, 1)
                    dve.wait_ge(vec, n)

                if check:
                    dve.wait_ge(loaded[k], 16 * i + 16)
                    wait(dve, checked, b)
                    dve.tensor_tensor(m.most, m.most, m.adj[k], ALU.max).then_inc(checked, 1)
                dve.wait_ge(multiplied, b + 1)
                if halves == 1:
                    y = m.bank(k, 3 * f).rearrange("p (t f) -> p f t", t=3)
                    dve.tensor_reduce(m.y[:, 0:f], y, AX.X, ALU.add).then_inc(summed, 1)
                else:
                    y = m.ps[:, 1024 * k:1024 * (k + 1)].rearrange("p (h q) -> p h q", h=2)[:, :, 0:3 * fh]
                    dve.tensor_reduce(m.y.rearrange("p (h f) -> p h f", h=2), y.rearrange("p h (t f) -> p h f t", t=3),
                                      AX.X, ALU.add).then_inc(summed, 1)
                here = m.norm[:, ds(b, 1)]
                x = m.x[:, ds(b * P, P)]
                if norm:
                    dve.wait_ge(summed, b + 1)
                    dve.tensor_scalar(m.y[:, 0:f], m.y[:, 0:f], here, None, ALU.mult).then_inc(scaled, 1)
                if kind == "gcn":
                    dve.wait_ge(projected, b + 1)
                    then(dve.tensor_scalar(m.h[:, 0:fn], out_bank[:, 0:fn], here, None, ALU.mult))
                    rows = m.h[:, 0:fn]
                if kind == "gcn_end":
                    dve.wait_ge(scaled, b + 1)
                    then(dve.tensor_tensor(m.h[:, 0:f], m.y[:, 0:f], biases[0], ALU.add))
                    then(dve.scalar_tensor_tensor(m.h[:, 0:f], m.h[:, 0:f], 0.0, x, ALU.max, ALU.add))
                if gin:
                    dve.wait_ge(projected, b + 1)
                    then(dve.tensor_tensor(m.h[:, 0:fn], out_bank[:, 0:fn], biases[1], ALU.add))
                    rows = m.h[:, 0:fn]
                    if kind == "gin":
                        then(dve.tensor_scalar(rows, rows, 0.0, None, ALU.max))
                    else:
                        then(dve.scalar_tensor_tensor(rows, rows, 0.0, x, ALU.max, ALU.add))
                if end:
                    then(dve.bn_stats(m.stats, m.h[:, 0:D]))
                    dve.sem_inc(aggregating, 1)
                    dve.bn_aggr(m.mean_var, m.stats).then_inc(aggregated, 1)
                    dve.wait_ge(rooted, b + 1)
                    then(dve.reciprocal(m.inverse, m.root))
                    last = dve.tensor_scalar(x, m.h[:, 0:D], m.mean_var[:, 0:1], m.inverse, ALU.subtract, ALU.mult)
                    if kind == "gin_end":
                        last.then_inc(placed, 1)
                        dve.wait_ge(placed, b + 1)
                    else:
                        then(last)
                    rows = x
                if target is not None:
                    fo = D if end else fn
                    ho = -(-fo // D)
                    to = m.parts[target][:, ds(b * (3 * fo), 3 * fo)].rearrange("p (h t f) -> p h t f", h=ho, t=3)
                    two = lambda a: a.rearrange("p (h f) -> p h f", h=ho)
                    three_parts(then, dve, two(rows), two(m.rest[:, 0:fo]), [to[:, :, t, :] for t in range(3)])

            if check:
                dve.memset(m.most, 0.0).then_inc(emptied, 1)
                dve.wait_ge(emptied, 1)
            every_block(dve, finish)
            if check:
                dve.wait_ge(checked, BLOCKS)
                dve.tensor_reduce(m.y[:, 0:1], m.most, AX.X, ALU.max).then_inc(peaked, 1)
                dve.wait_ge(peaked, 1)
                dve.tensor_scalar(m.y[:, 0:1], m.y[:, 0:1], float(EXACT), None, ALU.is_ge).then_inc(peaked, 1)
                dve.wait_ge(spotted, 1)
                dve.tensor_scalar(m.flag[:, :], m.bank(6, 1), 1.0, None, ALU.min).then_inc(flagged, 1)


def store_sums(block, m, table, f, placed, xed, stored, done):
    @block.sync
    def _(sp):
        with sp.Fori(0, GROUPS) as g:
            sp.wait_ge(placed, g + 1)
            if xed is not None:
                sp.wait_ge(xed, g + 1)
            sp.sem_inc(done, 1)
            sp.dma_start(group_rows(table, g), blocks(m.sums[:, ds(g * GN, GN)])[:, :, 0:f]).then_inc(stored, 16)
        sp.wait_ge(stored, 16 * GROUPS)


def gcn_step(nc, m, tag, weight, bias, f, table):
    with Phase(nc, tag, "scaled turned relued projected placed stored done") as (
            block, scaled, turned, relued, projected, placed, stored, done):

        @block.vector
        def _(dve):
            dve.sem_inc(done, 1)
            with dve.Fori(0, GROUPS) as g:
                s = blocks(m.sums[:, ds(g * GN, GN)])
                norm = m.norm[:, ds(g * GB, GB)]
                dve.wait_ge(done, g + 1)
                dve.tensor_tensor(blocks(m.stage_a[:, :])[:, :, 0:HID], s[:, :, 0:HID], copies(norm, 2, HID),
                                  ALU.mult).then_inc(scaled, 1)
                dve.wait_ge(projected, g + 1)
                dve.tensor_tensor(s[:, :, 0:f], blocks(m.ps[:, 1024:1024 + GN])[:, :, 0:f], copies(norm, 2, f),
                                  ALU.mult).then_inc(placed, 1)

        @block.tensor
        def _(pe):
            with pe.Fori(0, GROUPS) as g:
                pe.wait_ge(scaled, g + 1)
                turn_blocks(pe, m, 0, m.stage_a, HID).then_inc(turned, 1)
                pe.wait_ge(relued, g + 1)
                for b in range(GB):
                    mm = pe.matmul(m.ps[:, 1024 + b * P:1024 + b * P + f], m.stage_b[0:HID, b * P:(b + 1) * P],
                                   weight[0:HID, 0, :], start=True, stop=True)
                mm.then_inc(projected, 1)

        @block.scalar
        def _(act):
            with act.Fori(0, GROUPS) as g:
                act.wait_ge(turned, g + 1)
                act.activation(m.stage_b[0:HID, :], m.ps[0:HID, 0:GN], ACT.Relu, bias=bias[0:HID, :]).then_inc(relued, 1)

        store_sums(block, m, table, f, placed, None, stored, done)


def gcn_end(nc, m, table):
    with Phase(nc, "ge2", "vec stats summing rooted inverted lned xed placed stored done") as (
            block, vec, stats, summing, rooted, inverted, lned, xed, placed, stored, done):
        root = m.small[:, 330:330 + GB]
        steps = 3

        @block.vector
        def _(dve):
            dve.sem_inc(done, 1)
            with dve.Fori(0, GROUPS) as g:
                a, b = m.stage_a[:, :], m.stage_b[:, :]
                after = lambda n: dve.wait_ge(vec, g * steps + n)
                dve.wait_ge(done, g + 1)
                dve.tensor_tensor(blocks(a), blocks(m.sums[:, ds(g * GN, GN)]),
                                  copies(m.norm[:, ds(g * GB, GB)], 2, P), ALU.mult).then_inc(vec, 1)
                after(1)
                dve.tensor_tensor(blocks(a), blocks(a), copies(m.spread["c4"], 1, GB), ALU.add).then_inc(vec, 1)
                after(2)
                dve.scalar_tensor_tensor(b, a, 0.0, m.x[:, ds(g * GN, GN)], ALU.max, ALU.add).then_inc(vec, 1)
                after(3)
                normalize(dve, m, m.stage_b, m.stage_b, stats, summing, root, rooted, inverted, lned, g)
                dve.wait_ge(lned, g * GB + GB)
                dve.tensor_copy(m.gin_sums[:, ds(g * GN, GN)], b).then_inc(placed, 1)

        @block.scalar
        def _(act):
            with act.Fori(0, GROUPS) as g:
                take_roots(act, m, root, stats, rooted, g)
                act.wait_ge(lned, g * GB + GB)
                act.activation(m.x[:, ds(g * GN, GN)], m.stage_b[:, :], ACT.Copy).then_inc(xed, 1)

        @block.sync
        def _(sp):
            with sp.Fori(0, GROUPS) as g:
                sp.wait_ge(placed, g + 1)
                sp.wait_ge(xed, g + 1)
                sp.sem_inc(done, 1)
                sp.dma_start(group_rows(table, g), blocks(m.gin_sums[:, ds(g * GN, GN)])).then_inc(stored, 16)
            sp.wait_ge(stored, 16 * GROUPS)


def gin_step(nc, m, table):
    with Phase(nc, "gs3", "staged turned copied hidden relu0 relu1 projected biased placed stored done") as (
            block, staged, turned, copied, hidden, relu0, relu1, projected, biased, placed, stored, done):
        act0, act1 = m.stage_c[:, 0:GN], m.stage_c[:, GN:2 * GN]

        @block.scalar
        def _(act):
            act.sem_inc(done, 1)
            with act.Fori(0, GROUPS) as g:
                act.wait_ge(done, g + 1)
                act.activation(m.stage_a[:, :], m.gin_sums[:, ds(g * GN, GN)], ACT.Copy).then_inc(staged, 1)
                act.wait_ge(turned, g + 1)
                act.activation(m.stage_b[:, :], m.ps[:, 0:GN], ACT.Copy).then_inc(copied, 1)
                act.wait_ge(hidden, g * 2 + 1)
                act.activation(act0, m.ps[:, 1024:1024 + GN], ACT.Relu, bias=m.column["b1a"][:, 0:1]).then_inc(relu0, 1)

        @block.tensor
        def _(pe):
            pe.sem_inc(biased, 2)
            with pe.Fori(0, GROUPS) as g:
                pe.wait_ge(staged, g + 1)
                turn_blocks(pe, m, 0, m.stage_a).then_inc(turned, 1)
                pe.wait_ge(copied, g + 1)
                for o in range(2):
                    feature_product(pe, m, 2 + 2 * o, [(m.w["w1a"][:, 0, o * P:(o + 1) * P], m.stage_b)]).then_inc(hidden, 1)
                pe.wait_ge(relu0, g + 1)
                pe.wait_ge(relu1, g + 1)
                for b in range(GB):
                    out = gin_bank(m, b, 2 * D)
                    pe.wait_ge(biased, g * GB + b + 1)
                    pe.matmul(out, act0[:, b * P:(b + 1) * P], m.w["w1b"][:, 0, :], start=True, stop=False)
                    pe.matmul(out, act1[:, b * P:(b + 1) * P], m.w["w1b"][:, 1, :], start=False, stop=True).then_inc(projected, 1)

        @block.vector
        def _(dve):
            with dve.Fori(0, GROUPS) as g:
                s = m.sums[:, ds(g * 2 * GN, 2 * GN)]
                dve.wait_ge(hidden, g * 2 + 2)
                dve.tensor_scalar(act1, m.ps[:, 2048:2048 + GN], m.column["b1a"][:, 1:2], 0.0, ALU.add, ALU.max).then_inc(relu1, 1)
                for b in range(GB):
                    dve.wait_ge(projected, g * GB + b + 1)
                    dve.tensor_tensor(m.stage_d[:, b * 2 * D:(b + 1) * 2 * D], gin_bank(m, b, 2 * D), m.spread["b1b"],
                                      ALU.add).then_inc(biased, 1)
                dve.wait_ge(biased, g * GB + GB + 2)
                dve.tensor_scalar(s, m.stage_d, 0.0, None, ALU.max).then_inc(placed, 1)

        @block.sync
        def _(sp):
            with sp.Fori(0, GROUPS) as g:
                sp.wait_ge(placed, g + 1)
                sp.sem_inc(done, 1)
                sp.dma_start(group_rows(table, g), blocks(m.sums[:, ds(g * 2 * GN, 2 * GN)], 2 * D)).then_inc(stored, 16)
            sp.wait_ge(stored, 16 * GROUPS)


def gin_bank(m, b, n):
    return m.bank(6 + b % 2, n)


def gin_end(nc, m, out):
    with Phase(nc, "gf3", "staged turned copied0 copied1 hidden relu0 relu1 projected vec stats summing rooted inverted lned stored done") as (
            block, staged, turned, copied0, copied1, hidden, relu0, relu1, projected, vec, stats, summing, rooted, inverted,
            lned, stored, done):
        root = m.small[:, 330:330 + GB]
        steps = 2

        @block.scalar
        def _(act):
            act.sem_inc(done, 1)
            with act.Fori(0, GROUPS) as g:
                act.wait_ge(done, g + 1)
                act.activation(m.stage_c[:, :], m.sums[:, ds(g * 2 * GN, 2 * GN)], ACT.Copy).then_inc(staged, 1)
                act.wait_ge(turned, g * 2 + 1)
                act.activation(m.stage_d[:, 0:GN], m.ps[:, 0:GN], ACT.Copy).then_inc(copied0, 1)
                act.wait_ge(hidden, g * 2 + 1)
                act.activation(m.stage_a[:, :], m.ps[:, 2048:2048 + GN], ACT.Relu, bias=m.column["b2a"][:, 0:1]).then_inc(relu0, 1)
                take_roots(act, m, root, stats, rooted, g)

        @block.tensor
        def _(pe):
            with pe.Fori(0, GROUPS) as g:
                pe.wait_ge(staged, g + 1)
                for k in range(2):
                    for b in range(GB):
                        mm = pe.transpose(m.ps[:, 1024 * k + b * P:1024 * k + (b + 1) * P],
                                          m.stage_c[:, (2 * b + k) * P:(2 * b + k + 1) * P], m.ident[:, :])
                    mm.then_inc(turned, 1)
                pe.wait_ge(copied0, g + 1)
                pe.wait_ge(copied1, g + 1)
                for o in range(2):
                    feature_product(pe, m, 4 + 2 * o, [(m.w["w2a"][:, k, o * P:(o + 1) * P], m.stage_d[:, k * GN:(k + 1) * GN])
                                                       for k in range(2)]).then_inc(hidden, 1)
                pe.wait_ge(relu0, g + 1)
                pe.wait_ge(relu1, g + 1)
                for b in range(GB):
                    o = m.ps[:, b * P:(b + 1) * P]
                    pe.matmul(o, m.stage_a[:, b * P:(b + 1) * P], m.w["w2b"][:, 0, :], start=True, stop=False)
                    mm = pe.matmul(o, m.stage_b[:, b * P:(b + 1) * P], m.w["w2b"][:, 1, :], start=False, stop=True)
                mm.then_inc(projected, 1)

        @block.vector
        def _(dve):
            a, b = m.stage_a[:, :], m.stage_b[:, :]
            with dve.Fori(0, GROUPS) as g:
                dve.wait_ge(turned, g * 2 + 2)
                dve.tensor_copy(m.stage_d[:, GN:2 * GN], m.ps[:, 1024:1024 + GN]).then_inc(copied1, 1)
                dve.wait_ge(hidden, g * 2 + 2)
                dve.tensor_scalar(b, m.ps[:, 3072:3072 + GN], m.column["b2a"][:, 1:2], 0.0, ALU.add, ALU.max).then_inc(relu1, 1)
                dve.wait_ge(projected, g + 1)
                dve.tensor_tensor(blocks(a), blocks(m.ps[:, 0:GN]), copies(m.spread["b2b"], 1, GB), ALU.add).then_inc(vec, 1)
                dve.wait_ge(vec, g * steps + 1)
                dve.scalar_tensor_tensor(b, a, 0.0, m.x[:, ds(g * GN, GN)], ALU.max, ALU.add).then_inc(vec, 1)
                dve.wait_ge(vec, g * steps + 2)
                normalize(dve, m, m.stage_b, m.stage_c, stats, summing, root, rooted, inverted, lned, g)

        @block.sync
        def _(sp):
            with sp.Fori(0, GROUPS - 1) as g:
                sp.wait_ge(lned, g * GB + GB)
                sp.dma_start(group_rows(out, g), blocks(m.stage_c[:, 0:GN])).then_inc(stored, 16)
                sp.wait_ge(stored, g * 16 + 16)
                sp.sem_inc(done, 1)
            sp.wait_ge(lned, GROUPS * GB)
            first = (GROUPS - 1) * GN
            whole = (GB - 1) * P
            sp.dma_start(out[first:first + whole, :].rearrange("(b p) f -> p b f", p=P),
                         blocks(m.stage_c[:, 0:whole])).then_inc(stored, 16)
            sp.dma_start(out[first + whole:NODES, :], m.stage_c[0:LAST, whole:whole + P]).then_inc(stored, 16)
            sp.wait_ge(stored, 16 * (GROUPS + 1))


def restore(nc, m, x, sums):
    with Phase(nc, "re", "loaded") as (block, loaded):
        @block.sync
        def _(sp):
            sp.dma_start(blocks(m.x[:, :]), x.rearrange("(b p) f -> p b f", p=P)).then_inc(loaded, 16)
            sp.dma_start(blocks(m.sums[:, 0:BLOCKS * P])[:, :, 0:HID],
                         sums.rearrange("(b p) f -> p b f", p=P)).then_inc(loaded, 16)
            sp.wait_ge(loaded, 32)


def clear_sums(nc, m, n):
    with Phase(nc, "cs", "zeroed") as (block, zeroed):
        @block.vector
        def _(dve):
            dve.memset(m.sums[:, 0:n], 0.0).then_inc(zeroed, 1)


def program(nc, t, out):
    tables = {n: nc.dram_tensor(f"table_{n}", (BLOCKS * P, f), F32, kind="Internal").ap() for n, f in
              (("kv", 2 * D), ("k", D), ("v", D), ("h1", HID), ("h2", HID), ("h3", HID), ("h4", D), ("x", D), ("g", 2 * D), ("x1", D))}
    adj = nc.dram_tensor("adjacency", (ADJ_BLOCKS * P, SLOTS * WIDE), BF16, kind="Internal").ap()
    with ExitStack() as ctx:
        m = Memory(nc, ctx)
        plan(nc, m, t)
        project0(nc, m, t, tables["kv"])
        attend(nc, m, tables["kv"])
        attend_out(nc, m, t)
        feed_forward(nc, m)
        project1(nc, m, t, tables["k"], tables["v"])
        score(nc, m, tables["k"])
        softmax_rows(nc, m)
        softmax_weights(nc, m)
        clear_sums(nc, m, BLOCKS * A1)
        sum_values(nc, m, tables["v"])
        skip_gate(nc, m, tables["h1"])
        plan_windows(nc, m, t, tables["x1"])
        count_edges(nc, m, adj)
        first_parts(nc, m, tables["h1"])
        layer = lambda c, w: dict(fn=w.shape[2], weights=[w], biases=[c])
        dense(nc, m, "d1", adj, "gcn", HID, 0, target=1, **layer(m.column["c1"], m.w["g2"]))
        dense(nc, m, "d2", adj, "gcn", HID, 1, target=0, **layer(m.column["c2"], m.w["g3"]))
        dense(nc, m, "d3", adj, "gcn", HID, 0, target=1, **layer(m.column["c3"], m.w["g4"]))
        dense(nc, m, "d4", adj, "gcn_end", D, 1, target=0, biases=[m.spread["c4"]])
        dense(nc, m, "d5", adj, "gin", D, 0, fn=2 * D, target=1, weights=[m.w["w1a"], m.w["w1b"]],
              biases=[m.column["b1a"], m.spread["b1b"]])
        dense(nc, m, "d6", adj, "gin_end", 2 * D, 1, fn=D, weights=[m.w["w2a"], m.w["w2b"]],
              biases=[m.column["b2a"], m.spread["b2b"]], check=True, out=out)
        Phase.flag = m.flag
        plan(nc, m, t, again=True)
        restore(nc, m, tables["x1"], tables["h1"])
        sum_rows(nc, m, "s1", tables["h1"], HID, m.sums, D)
        gcn_step(nc, m, "n1", m.w["g2"], m.column["c1"], HID, tables["h2"])
        sum_rows(nc, m, "s2", tables["h2"], HID, m.sums, D)
        gcn_step(nc, m, "n2", m.w["g3"], m.column["c2"], HID, tables["h3"])
        sum_rows(nc, m, "s3", tables["h3"], HID, m.sums, D)
        gcn_step(nc, m, "n3", m.w["g4"], m.column["c3"], D, tables["h4"])
        sum_rows(nc, m, "s4", tables["h4"], D, m.sums, D)
        gcn_end(nc, m, tables["x"])
        sum_rows(nc, m, "s5", tables["x"], D, m.gin_sums, D)
        gin_step(nc, m, tables["g"])
        sum_rows(nc, m, "s6", tables["g"], 2 * D, m.sums, 2 * D)
        gin_end(nc, m, out)
        Phase.flag = None


def kernel(**inputs):
    import numpy as np
    from concourse import bacc
    from concourse.bass_utils import run_bass_kernel_spmd

    i = {k: np.asarray(v) for k, v in inputs.items()}

    def padded(a, rows, fill):
        out = np.full((rows, *a.shape[1:]), fill, a.dtype)
        out[:a.shape[0]] = a
        return out

    x = padded(i["x"], BLOCKS * P, 0)
    g0, g1, g2, g3 = ({k[7:]: v for k, v in i.items() if k.startswith(f"L{n}_gnn_")} for n in range(4))
    columns = {"bo": g0["bo"], "b1": g0["b1"], "b2": g0["b2"], "n1w": g0["bn1_w"], "n1b": g0["bn1_b"],
               "n2w": g0["bn2_w"], "n2b": g0["bn2_b"], "c1": g2["b1"], "c2": g2["b2"], "c3": g2["b3"],
               "b1a": g3["b1a"], "b2a": g3["b2a"]}
    spread = {"bqkvs": np.concatenate([g1["bq"], g1["bk"], g1["bv"], g1["bskip"]]),
              "wbeta": g1["Wbeta"].reshape(-1), "c4": g2["b4"], "b1b": g3["b1b"], "b2b": g3["b2b"]}
    arrays = {
        "x": x, "xT": x.T,
        "src": padded(i["src"], COLS * P, 0).reshape(COLS, P),
        "dst": padded(i["dst"], COLS * P, NO_DST).reshape(COLS, P),
        "wqkv0": np.concatenate([g0["Wq"].T, g0["Wk"].T, g0["Wv"].T], axis=1),
        "wo": g0["Wo"].T, "w1": g0["W1"].T, "w2": g0["W2"].T,
        "wqkvs": np.concatenate([g1["Wq"], g1["Wk"], g1["Wv"], g1["Wskip"]], axis=1),
        "g1": g2["W1"], "g2": g2["W2"], "g3": g2["W3"], "g4": g2["W4"],
        "w1a": g3["W1a"], "w1b": g3["W1b"], "w2a": g3["W2a"], "w2b": g3["W2b"],
        "columns": np.concatenate([padded(columns[n], k * P, 0).reshape(k, P) for n, k in COLUMNS]).T,
        "spread": np.concatenate([spread[n] for n, _ in SPREAD]).reshape(1, -1),
    }
    arrays = {k: np.ascontiguousarray(v) for k, v in arrays.items()}
    nc = bacc.Bacc("TRN2", target_bir_lowering=False, num_devices=1)
    tensors = {k: nc.dram_tensor(f"in_{k}", v.shape, mybir.dt.from_np(v.dtype), kind="ExternalInput").ap()
               for k, v in arrays.items()}
    out = nc.dram_tensor("out", (NODES, D), F32, kind="ExternalOutput").ap()
    program(nc, tensors, out)
    result = run_bass_kernel_spmd(nc, [{f"in_{k}": v for k, v in arrays.items()}], core_ids=[0])
    return result.results[0]["out"]
```

```python
from contextlib import ExitStack

import concourse.bass as bass
from concourse import mybir

P = 128
NODES, EDGES, D = 6250, 100000, 128
BLOCKS = -(-NODES // P)
LAST = NODES - (BLOCKS - 1) * P
TILES = -(-EDGES // P)
GB = 7
GROUPS = BLOCKS // GB
GN = GB * P
HALF = 4
UNROLL = 2 * HALF
TURNS = -(-(TILES + BLOCKS - 1) // UNROLL)
STEPS = TURNS * UNROLL
ROWS = -(-TILES // P)
COLS = ROWS * P
assert BLOCKS == GROUPS * GB and STEPS + HALF <= COLS
NO_DST = 16384
BIG = 1e30
H0, C0 = 8, D // 8
H1, C1 = 4, D // 4
HID = 100
A0 = D + H0 + 1
A1 = D + H1
SC = COLS * H1

F32 = mybir.dt.float32
I32 = mybir.dt.int32
BF16 = mybir.dt.bfloat16
F16 = mybir.dt.float16
ALU = mybir.AluOpType
ACT = mybir.ActivationFunctionType
AX = mybir.AxisListType
ds = bass.ds

WIN = 8
WINDOWS = BLOCKS * P // WIN
SLOTS = P // WIN
WIDE = BLOCKS * WIN
WTURNS = -(-(TILES + WINDOWS - 1) // UNROLL)
WSTEPS = WTURNS * UNROLL
assert WTURNS % 2 == 0
WCOLS = 1664
assert WSTEPS + 2 < WCOLS and WCOLS % 4 == 0 and WCOLS // 4 <= 512 and SLOTS % 2 == 0
RING = 32
SPARE = BLOCKS + 1
ADJ_BLOCKS = SPARE + -(-WSTEPS // SLOTS)
EXACT = 256
ARENA = 40200

WEIGHTS = [("wqkv0", 1, 3 * D), ("wo", 1, D), ("w1", 1, 2 * D), ("w2", 2, D), ("wqkvs", 1, 4 * D),
           ("g1", 1, HID), ("g2", 1, HID), ("g3", 1, HID), ("g4", 1, D),
           ("w1a", 1, 2 * D), ("w1b", 2, 2 * D), ("w2a", 2, 2 * D), ("w2b", 2, D)]
COLUMNS = [("bo", 1), ("b1", 2), ("b2", 1), ("n1w", 1), ("n1b", 1), ("n2w", 1), ("n2b", 1),
           ("c1", 1), ("c2", 1), ("c3", 1), ("b1a", 2), ("b2a", 2)]
SPREAD = [("bqkvs", 4 * D), ("wbeta", 3 * D), ("c3", HID), ("c4", D), ("b1b", 2 * D), ("b2b", D)]


class Memory:

    def __init__(self, nc, ctx):
        def sb(name, n, dt=F32):
            return ctx.enter_context(nc.sbuf_tensor(name, [P, n], dt))

        def split(t, *shape):
            names = " ".join("abc"[:len(shape)])
            return t.rearrange(f"p ({names}) -> p {names}", **dict(zip("abc", shape)))

        self.x = sb("x", BLOCKS * D)
        arena = sb("arena", ARENA)
        self.used = 0

        def take(n, dt=F32):
            size = n if dt in (F32, I32) else -(-n // 2)
            part = arena[:, self.used:self.used + size]
            self.used += size
            assert self.used <= ARENA, self.used
            return part if dt == F32 else part.bitcast(dt)

        big = take(BLOCKS * A0 + BLOCKS * D)
        self.sums = big
        self.gin_sums = big[:, BLOCKS * A0:]
        self.q = big[:, BLOCKS * A0:]
        self.score = big[:, 0:SC]
        self.srow = split(big[:, SC:2 * SC], ROWS, H1, P)
        self.fwd = split(big[:, 2 * SC:3 * SC], ROWS, H1, P)
        self.bwd = split(big[:, 0:SC], ROWS, H1, P)
        self.weight = big[:, 9000:9000 + SC]
        self.x_scratch = split(self.q[:, 5000:5000 + ROWS * (P + 1)], ROWS, P + 1)
        self.feat = take(BLOCKS * P)
        rows = take(UNROLL * 2 * D)
        self.rows = split(rows, UNROLL, 2 * D)
        self.hit = split(take(UNROLL * P), 2, HALF, P)
        self.hitT = split(take(UNROLL * P), 2, HALF, P)
        self.prod = take(HALF * D)
        self.msg = split(take(2 * HALF * A0), 2, HALF, A0)
        self.raw = take(2 * HALF * H0)
        self.stage_a = take(GN)
        self.stage_b = take(GN)
        self.stage_c = take(2 * GN)
        self.stage_d = rows[:, 0:2 * GN]
        self.local = take(COLS)
        self.src = take(COLS, I32)
        self.idx = take(UNROLL, I32)
        self.block = take(COLS, I32)
        self.pick0 = take(COLS)
        self.pick1 = take(COLS)
        self.dst_rows = take(COLS)
        self.ring4 = split(take(4 * HALF * 2 * D), 4 * HALF, 2 * D)
        self.idx4 = take(4 * HALF, I32)
        self.hit4 = split(take(4 * HALF * P), 4, HALF, P)

        self.used = 0
        self.rows_i = take(2 * COLS, I32)
        self.rows_f = take(2 * COLS)
        self.wramp = take(WCOLS)
        self.wtile = take(WCOLS)
        self.window = take(WCOLS)
        self.wwork = [take(WCOLS) for _ in range(3)]
        self.wint = take(WCOLS, I32)
        self.lo = take(WCOLS)
        self.place = take(WCOLS)
        self.ring = take(WCOLS, I32)
        self.clean = take(WCOLS, I32)
        self.stores = take(3 * WCOLS, I32)
        self.out_slot, self.out_block, self.out_part = (self.stores[:, k:3 * WCOLS:3] for k in range(3))
        self.count_to = take(WIDE, F16)
        self.by_lo = split(take(4 * HALF * P, BF16), 4, HALF, P)
        self.lo_now = split(take(4 * HALF), 4, HALF)
        self.by_place = split(take(2 * HALF * WIDE, BF16), 2, HALF, WIDE)
        self.counted = split(take(2 * HALF * WIDE, BF16), 2, HALF, WIDE)
        self.slots = take((RING + 2) * WIDE, BF16)
        self.slots_as_f32 = self.slots.bitcast(F32)
        self.zeros = take(WIDE // 2)

        self.used = 0
        self.adj = [take(SLOTS * WIDE, BF16) for _ in range(3)]
        parts0 = take(BLOCKS * 3 * D, BF16)
        parts1 = take(BLOCKS * 6 * D, BF16)
        self.parts = [parts0, parts1]
        self.most = parts0[:, 0:SLOTS * WIDE]
        self.y = take(2 * D)
        self.yT = take(2 * D)
        self.hid = take(2 * D)
        self.h = take(2 * D)
        self.rest = take(2 * D)
        self.stats = take(6)
        self.root, self.inverse = take(1), take(1)
        self.w, at = {}, 0
        w = sb("w", sum(k * n for _, k, n in WEIGHTS))
        for name, k, n in WEIGHTS:
            self.w[name] = split(w[:, at:at + k * n], k, n)
            at += k * n
        self.column, at = {}, 0
        self.columns = col = sb("columns", sum(n for _, n in COLUMNS))
        for name, n in COLUMNS:
            self.column[name] = col[:, at:at + n]
            at += n
        self.spread, at = {}, 0
        self.spreads = spread = sb("spread", sum(n for _, n in SPREAD))
        for name, n in SPREAD:
            self.spread[name] = spread[:, at:at + n]
            at += n
        self.ident = sb("ident", P)
        self.identb = sb("identb", P, BF16)
        self.flag = sb("flag", 1, I32)
        self.ones = sb("ones", P)
        self.number = sb("number", P)
        self.tile_id = sb("tile_id", ROWS)
        self.small = sb("small", 512)
        self.eps = sb("eps", 1)
        self.mean_var, self.scale, self.shift = self.small[:, 360:362], self.small[:, 362:363], self.small[:, 363:364]
        self.norm = sb("norm", BLOCKS)
        self.x_scratch = split(self.q[:, 5000:5000 + ROWS * (P + 1)], ROWS, P + 1)
        self.gathered = [ctx.enter_context(nc.semaphore(f"gathered{k}")) for k in range(UNROLL)]
        self.gathered_before = 0
        self.stored_before = 0
        self.gathered4 = [ctx.enter_context(nc.semaphore(f"gathered4_{r}")) for r in range(4)]
        self.gathered4_before = 0
        self.pool_stored = [ctx.enter_context(nc.semaphore("pool_stored"))]
        self.ps = ctx.enter_context(nc.psum_tensor("ps", [P, 8 * 512], F32))

    def bank(self, k, n=512):
        return self.ps[:, 512 * k:512 * k + n]


class Flagged:

    def __init__(self, block, flag):
        self.block, self.flag = block, flag

    def guarded(self, program):
        def run(engine):
            flag = engine.value_load(self.flag[0:1, 0:1], min_val=0, max_val=1)
            with engine.If(flag > 0):
                program(engine)
        return run

    def vector(self, program):
        self.block.vector(self.guarded(program))

    def scalar(self, program):
        self.block.scalar(self.guarded(program))

    def tensor(self, program):
        self.block.tensor(self.guarded(program))

    def gpsimd(self, program):
        self.block.gpsimd(self.guarded(program))

    def sync(self, program):
        self.block.sync(self.guarded(program))


class Phase:
    flag = None

    def __init__(self, nc, tag, names, lasting=()):
        self.nc, self.names, self.lasting = nc, [f"{tag}_{n}" for n in names.split()], list(lasting)

    def __enter__(self):
        self.ctx = ExitStack()
        nc = self.nc
        sems = [self.ctx.enter_context(nc.semaphore(n)) for n in self.names]
        with nc.Block() as clear:
            @clear.sync
            def _(sp):
                for s in sems:
                    sp.sem_clear(s)
        self.block = self.ctx.enter_context(nc.Block())
        if Phase.flag is not None:
            self.block = Flagged(self.block, Phase.flag)
        return (self.block, *sems, *self.lasting)

    def __exit__(self, *a):
        return self.ctx.__exit__(*a)


def copies(ap, axis, n):
    ap = ap.unsqueeze(axis)
    shape = list(ap.shape)
    shape[axis] = n
    return ap.broadcast_to(shape)


def group_rows(table, g):
    return table[ds(g * GN, GN), :].rearrange("(b p) f -> p b f", p=P)


def load_blocks(engine, regs, m, first):
    engine.load(regs, m.block[0:1, ds(first, HALF)])
    return [engine.snap(r, min_val=0, max_val=BLOCKS - 1) for r in regs]


def wait(engine, sem, n):
    if not (isinstance(n, int) and n <= 0):
        engine.wait_ge(sem, n)


def registers(nc, engine, name, n=HALF):
    return [engine.alloc_register(f"{name}{k}") for k in range(n)]


def plan(nc, m, t, again=False):
    with Phase(nc, "plan2" if again else "plan", "rows_in params_in made conv ranked compared counted stepped based "
               "picked drawn done") as (
            block, rows_in, params_in, made, conv, ranked, compared, counted, stepped, based,
            picked, drawn, done):
        dst_i = m.stage_a[:, :].bitcast(I32)
        src_i = m.stage_b[:, :].bitcast(I32)
        src_f = m.stage_c[:, 0:COLS]
        ramp = m.stage_c[:, COLS:2 * COLS]
        tile_of = m.feat[:, 0:COLS]
        block_of = m.feat[:, COLS:2 * COLS]
        reached = m.feat[:, 2 * COLS:4 * COLS]
        rank = m.small[:, 0:ROWS]
        blk_i = m.small[:, 8:8 + ROWS].bitcast(I32)
        blk_f = m.small[:, 16:16 + ROWS]
        ints = m.rows.rearrange("p a b -> p (a b)")[:, 0:COLS + P + 8].bitcast(I32)
        part = m.small[:, 24:25]

        @block.sync
        def _(sp):
            sp.dma_start(dst_i.rearrange("p (j e) -> p j e", e=P),
                         t["dst"].rearrange("(j p) e -> p j e", p=P)).then_inc(rows_in, 16)
            sp.dma_start(src_i.rearrange("p (j e) -> p j e", e=P),
                         t["src"].rearrange("(j p) e -> p j e", p=P)).then_inc(rows_in, 16)
            if again:
                sp.wait_ge(rows_in, 32)
                return
            for name, k, n in WEIGHTS:
                r = min(P, t[name].shape[0])
                sp.dma_start(m.w[name][0:r, :, :], t[name].rearrange("(k p) n -> p k n", p=r)).then_inc(params_in, 16)
            sp.dma_start(m.columns[:, :], t["columns"]).then_inc(params_in, 16)
            sp.dma_start(m.spreads[:, :], t["spread"].broadcast_to([P, t["spread"].shape[1]])).then_inc(params_in, 16)
            sp.dma_start(m.x[:, :].rearrange("p (b f) -> p b f", f=D),
                         t["x"].rearrange("(b p) f -> p b f", p=P)).then_inc(params_in, 16)
            sp.wait_ge(params_in, 16 * (len(WEIGHTS) + 3))

        @block.gpsimd
        def _(pool):
            pool.iota(ints[:, 0:COLS], [[1, COLS]], base=0, channel_multiplier=0).then_inc(made, 1)
            pool.iota(ints[:, COLS:COLS + ROWS], [[P, ROWS]], base=0, channel_multiplier=1).then_inc(made, 1)
            pool.memset(m.ones[:, :], 1.0).then_inc(made, 1)

        @block.vector
        def _(dve):
            dve.wait_ge(made, 3)
            dve.tensor_copy(ramp, ints[:, 0:COLS]).then_inc(conv, 1)
            dve.tensor_copy(m.tile_id[:, :], ints[:, COLS:COLS + ROWS]).then_inc(conv, 1)
            dve.wait_ge(rows_in, 32)
            dve.tensor_copy(m.dst_rows[:, :], dst_i).then_inc(conv, 1)
            dve.tensor_copy(src_f, src_i).then_inc(conv, 1)
            dve.tensor_scalar(blk_i, dst_i[:, 0:COLS:P], 7, None, ALU.arith_shift_right).then_inc(conv, 1)
            dve.wait_ge(conv, 5)
            dve.tensor_copy(m.number[:, :], ramp[:, 0:P]).then_inc(ranked, 1)
            dve.tensor_copy(blk_f, blk_i).then_inc(ranked, 1)
            dve.tensor_scalar(m.ident[:, :], ramp[:, 0:P], m.tile_id[:, 0:1], None, ALU.is_equal).then_inc(ranked, 1)
            dve.wait_ge(ranked, 3)
            dve.tensor_tensor(rank, blk_f, m.tile_id[:, :], ALU.add).then_inc(ranked, 1)
            dve.wait_ge(ranked, 4)
            for j in range(ROWS):
                if j >= 2:
                    dve.wait_ge(counted, 2 * (j - 1))
                dve.tensor_scalar(reached[:, (j % 2) * COLS:(j % 2 + 1) * COLS], ramp, rank[:, j:j + 1],
                                  None, ALU.is_ge).then_inc(compared, 1)
            dve.wait_ge(counted, 2 * ROWS)
            for k in range(2):
                c = slice(k * COLS // 2, (k + 1) * COLS // 2)
                dve.tensor_scalar(tile_of[:, c], m.bank(k, COLS // 2), -1.0, 0.0, ALU.add, ALU.max).then_inc(stepped, 1)
            dve.wait_ge(stepped, 2)
            dve.tensor_tensor(block_of, ramp, tile_of, ALU.subtract).then_inc(based, 1)
            for j in range(ROWS):
                c = slice(j * P, (j + 1) * P)
                dve.tensor_scalar(m.pick0[:, c], tile_of[:, c], m.tile_id[:, j:j + 1], None, ALU.is_equal).then_inc(picked, 1)
                before = max(j - 1, 0)
                dve.tensor_scalar(m.pick1[:, c], tile_of[:, c], m.tile_id[:, before:before + 1],
                                  None, ALU.is_equal).then_inc(picked, 1)
            dve.wait_ge(based, 1)
            dve.tensor_scalar(block_of, block_of, -float(P), None, ALU.mult).then_inc(based, 1)
            dve.tensor_tensor(m.rows.rearrange("p a b -> p (a b)")[:, 0:COLS], ramp, tile_of, ALU.subtract).then_inc(based, 1)
            dve.wait_ge(based, 3)
            dve.tensor_scalar(m.block[:, :], m.rows.rearrange("p a b -> p (a b)")[:, 0:COLS], float(BLOCKS - 1),
                              None, ALU.min).then_inc(done, 1)
            dve.wait_ge(drawn, 2 * ROWS)
            for j in range(ROWS):
                c = slice(j * P, (j + 1) * P)
                dve.tensor_tensor(m.local[:, c], m.ps[:, 1024 + j * P:1024 + (j + 1) * P], block_of[:, c], ALU.add).then_inc(done, 1)
                dve.tensor_copy(m.src[:, c], m.ps[:, 2048 + j * P:2048 + (j + 1) * P]).then_inc(done, 1)

        @block.tensor
        def _(pe):
            for j in range(ROWS):
                pe.wait_ge(compared, j + 1)
                for k in range(2):
                    pe.matmul(m.bank(k, COLS // 2), m.ones[:, :],
                              reached[:, (j % 2) * COLS + k * COLS // 2:(j % 2) * COLS + (k + 1) * COLS // 2],
                              start=(j == 0), stop=(j == ROWS - 1)).then_inc(counted, 1)
            for j in range(ROWS):
                pe.wait_ge(picked, 2 * (j + 1))
                c = slice(j * P, (j + 1) * P)
                for at, rows in ((1024, m.dst_rows[:, :]), (2048, src_f)):
                    out = m.ps[:, at + j * P:at + (j + 1) * P]
                    mm = pe.matmul(out, rows[:, c], m.pick0[:, c], start=True, stop=(j == 0))
                    if j:
                        mm = pe.matmul(out, rows[:, (j - 1) * P:j * P], m.pick1[:, c], start=False, stop=True)
                    mm.then_inc(drawn, 1)


def gathers(pool, m, table, f, idx_copied, issued, free, gathered):
    with pool.Fori(0, TURNS) as i:
        for h in range(2):
            pool.wait_ge(free, 2 * i + h + 1)
            pool.tensor_copy(m.idx[:, h * HALF:(h + 1) * HALF],
                             m.src[:, ds(i * UNROLL + h * HALF, HALF)]).then_inc(idx_copied, 1)
            pool.wait_ge(idx_copied, 2 * i + h + 1)
            pool.sem_inc(issued, 1)
            for k in range(h * HALF, (h + 1) * HALF):
                pool.indirect_dma_start(m.rows[:, k, 0:f], None, table,
                                        bass.IndirectOffsetOnAxis(m.idx[:, k:k + 1], 0)).then_inc(gathered[k], 16)


def gathers4(pool, m, table, f, idx_copied, issued, free, gathered):
    with pool.Fori(0, TURNS // 2) as i:
        for r in range(4):
            pool.wait_ge(free, 4 * i + r + 1)
            pool.wait_ge(idx_copied, 4 * i + r + 1)
            pool.sem_inc(issued, 1)
            for k in range(HALF):
                pool.indirect_dma_start(m.ring4[:, r * HALF + k, 0:f], None, table,
                                        bass.IndirectOffsetOnAxis(m.idx4[:, r * HALF + k:r * HALF + k + 1], 0)).then_inc(gathered[r], 16)


def copy_indices(act, m, j, r, issued, idx_copied):
    wait(act, issued, j - 2)
    act.activation(m.idx4[:, r * HALF:(r + 1) * HALF], m.src[:, ds(j * HALF, HALF)], ACT.Copy).then_inc(idx_copied, 1)


def hits4(dve, m, r, first):
    return dve.tensor_tensor(m.hit4[:, r], copies(m.number[:, :], 1, HALF),
                             copies(m.local[:, ds(first, HALF)], 2, P), ALU.is_equal)


def hits(dve, m, h, first):
    return dve.tensor_tensor(m.hit[:, h], copies(m.number[:, :], 1, HALF),
                             copies(m.local[:, ds(first, HALF)], 2, P), ALU.is_equal)


def sum_rows(nc, m, tag, table, f, sums, width):
    with Phase(nc, tag, "idx_copied issued free used added hit_ready", m.gathered) as (
            block, idx_copied, issued, free, used, added, hit_ready, *gathered):
        before = m.gathered_before
        m.gathered_before += 16 * TURNS

        @block.gpsimd
        def _(pool):
            gathers(pool, m, table, f, idx_copied, issued, free, gathered)

        @block.tensor
        def _(pe):
            pe.sem_inc(free, 2)
            with pe.Fori(0, TURNS) as i:
                for h in range(2):
                    pe.wait_ge(hit_ready, 2 * i + h + 1)
                    for k in range(HALF):
                        slot = h * HALF + k
                        pe.wait_ge(gathered[slot], before + 16 * i + 16)
                        pe.wait_ge(added, i * UNROLL + slot + 1)
                        pe.matmul(m.bank(slot, f), m.hit[:, h, k, :], m.rows[:, slot, 0:f],
                                  start=True, stop=True).then_inc(used, 1)
                    pe.wait_ge(used, i * UNROLL + (h + 1) * HALF)
                    pe.sem_inc(free, 1)

        @block.vector
        def _(dve):
            regs = registers(nc, dve, tag)
            dve.sem_inc(added, UNROLL)
            with dve.Fori(0, TURNS) as i:
                for h in range(2):
                    hits(dve, m, h, i * UNROLL + h * HALF).then_inc(hit_ready, 1)
                for h in range(2):
                    at = load_blocks(dve, regs, m, i * UNROLL + h * HALF)
                    for k in range(HALF):
                        slot = h * HALF + k
                        to = sums[:, ds(at[k] * width, f)]
                        dve.wait_ge(used, i * UNROLL + slot + 1)
                        dve.wait_ge(added, UNROLL + i * UNROLL + slot)
                        dve.tensor_tensor(to, to, m.bank(slot, f), ALU.add).then_inc(added, 1)


def attend(nc, m, table):
    with Phase(nc, "at0", "idx_copied issued free used added hit_ready turned copied q_ready multiplied "
               "reduced clipped weights_ready weighted ones_in", m.gathered4) as (
            block, idx_copied, issued, free, used, added, hit_ready, turned, copied, q_ready, multiplied,
            reduced, clipped, weights_ready, weighted, ones_in, *gathered):
        before = m.gathered4_before
        m.gathered4_before += 64 * (TURNS // 2)
        raw = m.raw[:, :].rearrange("p (a n) -> p a n", a=2)

        @block.gpsimd
        def _(pool):
            gathers4(pool, m, table, 2 * D, idx_copied, issued, free, gathered)

        @block.tensor
        def _(pe):
            regs = registers(nc, pe, "at0pe")
            pe.sem_inc(free, 4)

            def products(j, r):
                pe.wait_ge(weighted, j + 1)
                for k in range(HALF):
                    pe.wait_ge(added, j * HALF + k + 1)
                    mm = pe.matmul(m.bank(k, A0), m.hit4[:, r, k, :], m.msg[:, r % 2, k, :], start=True, stop=True)
                    mm.then_inc(used, 1)
                pe.wait_ge(used, (j + 2) * HALF)
                pe.sem_inc(free, 1)

            def turn(j, r):
                pe.wait_ge(hit_ready, j + 1)
                wait(pe, copied, j - 1)
                for k in range(HALF):
                    mm = pe.transpose(m.bank(4 + r % 2)[:, k * P:(k + 1) * P], m.hit4[:, r, k, :], m.ident[:, :])
                mm.then_inc(turned, 1)

            def queries(j, h):
                at = load_blocks(pe, regs, m, j * HALF)
                pe.wait_ge(copied, j + 1)
                wait(pe, multiplied, j - 1)
                for k in range(HALF):
                    mm = pe.matmul(m.bank(6 + h)[:, k * P:(k + 1) * P], m.hitT[:, h, k, :],
                                   m.q[:, ds(at[k] * D, D)], start=True, stop=True)
                mm.then_inc(q_ready, 1)

            def half(j, r):
                turn(j + 2, (r + 2) % 4)
                products(j, r)
                queries(j + 2, r % 2)

            pe.sem_inc(used, HALF)
            turn(0, 0)
            turn(1, 1)
            queries(0, 0)
            queries(1, 1)
            for j in range(4):
                half(j, j)
            with pe.Fori(1, TURNS // 2) as i:
                for r in range(4):
                    half(4 * i + r, r)

        @block.scalar
        def _(act):
            def copy(j, h):
                act.wait_ge(turned, j + 1)
                wait(act, q_ready, j - 1)
                act.activation(m.hitT[:, h], m.bank(4 + h).rearrange("p (k n) -> p k n", k=HALF), ACT.Copy).then_inc(copied, 1)

            def exps(j, h):
                act.wait_ge(clipped, j + 1)
                wait(act, used, j * HALF)
                act.activation(m.msg[:, h, :, D:D + H0], raw[:, h].rearrange("p (k n) -> p k n", k=HALF),
                               ACT.Exp, scale=float(C0) ** -0.5).then_inc(weights_ready, 1)

            copy_indices(act, m, 0, 0, issued, idx_copied)
            copy_indices(act, m, 1, 1, issued, idx_copied)
            copy_indices(act, m, 2, 2, issued, idx_copied)
            copy(0, 0)
            copy(1, 1)
            for j in range(4):
                exps(j, j % 2)
                copy(j + 2, j % 2)
                copy_indices(act, m, j + 3, (j + 3) % 4, issued, idx_copied)
            with act.Fori(1, TURNS // 2) as i:
                for r in range(4):
                    exps(4 * i + r, r % 2)
                    copy(4 * i + r + 2, r % 2)
                    copy_indices(act, m, 4 * i + r + 3, (r + 3) % 4, issued, idx_copied)

        @block.vector
        def _(dve):
            regs = registers(nc, dve, "at0dve")
            dve.memset(m.msg[:, :, :, D + H0:A0], 1.0).then_inc(ones_in, 1)
            dve.wait_ge(ones_in, 1)
            dve.sem_inc(added, HALF)

            def half(i, j, h, r, first=False):
                if not first:
                    at = load_blocks(dve, regs, m, (j - 1) * HALF)

                def add(k):
                    if first:
                        return
                    to = m.sums[:, ds(at[k] * A0, A0)]
                    dve.wait_ge(used, j * HALF + k + 1)
                    dve.wait_ge(added, j * HALF + k)
                    dve.tensor_tensor(to, to, m.bank(k, A0), ALU.add).then_inc(added, 1)

                rows = m.ring4[:, r * HALF:(r + 1) * HALF, :]
                dve.wait_ge(q_ready, j + 1)
                dve.wait_ge(gathered[r], before + 64 * i + 64)
                prod = m.prod[:, :].rearrange("p (k n) -> p k n", k=HALF)
                dve.tensor_tensor(prod, rows[:, :, 0:D],
                                  m.bank(6 + h).rearrange("p (k n) -> p k n", k=HALF), ALU.mult).then_inc(multiplied, 1)
                add(0)
                dve.wait_ge(multiplied, j + 1)
                dve.tensor_reduce(raw[:, h], m.prod[:, :].rearrange("p (n c) -> p n c", c=C0), AX.X, ALU.add).then_inc(reduced, 1)
                add(1)
                dve.wait_ge(reduced, j + 1)
                lim = 5.0 * float(C0) ** 0.5
                dve.tensor_scalar(raw[:, h], raw[:, h], lim, -lim, ALU.min, ALU.max).then_inc(clipped, 1)
                add(2)
                wait(dve, used, j * HALF)
                hits4(dve, m, (r + 2) % 4, (j + 2) * HALF).then_inc(hit_ready, 1)
                add(3)
                dve.wait_ge(weights_ready, j + 1)
                dve.tensor_tensor(m.msg[:, h, :, 0:D].rearrange("p k (n c) -> p k n c", c=C0),
                                  rows[:, :, D:2 * D].rearrange("p k (n c) -> p k n c", c=C0),
                                  copies(m.msg[:, h, :, D:D + H0], 3, C0), ALU.mult).then_inc(weighted, 1)

            hits4(dve, m, 0, 0).then_inc(hit_ready, 1)
            hits4(dve, m, 1, HALF).then_inc(hit_ready, 1)
            half(0, 0, 0, 0, True)
            for j in range(1, 4):
                half(0, j, j % 2, j)
            with dve.Fori(1, TURNS // 2) as i:
                for r in range(4):
                    half(i, 4 * i + r, r % 2, r)
            at = load_blocks(dve, regs, m, (2 * TURNS - 1) * HALF)
            for k in range(HALF):
                to = m.sums[:, ds(at[k] * A0, A0)]
                dve.wait_ge(used, 2 * TURNS * HALF + k + 1)
                dve.wait_ge(added, 2 * TURNS * HALF + k)
                dve.tensor_tensor(to, to, m.bank(k, A0), ALU.add).then_inc(added, 1)


def score(nc, m, table, edge_values):
    with Phase(nc, "sc1", "idx_copied issued free hit_ready turned copied q_ready multiplied reduced "
               "kept0 kept1 kept2 kept3", m.gathered4) as (
            block, idx_copied, issued, free, hit_ready, turned, copied, q_ready, multiplied, reduced,
            kept0, kept1, kept2, kept3, *gathered):
        before = m.gathered4_before
        m.gathered4_before += 64 * (TURNS // 2)
        kept = (kept0, kept1, kept2, kept3)

        @block.gpsimd
        def _(pool):
            gathers4(pool, m, table, 2 * D, idx_copied, issued, free, gathered)

        @block.sync
        def _(sp):
            def keep(j, r, i):
                sp.wait_ge(gathered[r], before + 64 * i + 64)
                sp.dma_start(edge_values[ds(j * P, P), :].rearrange("p (k f) -> p k f", k=HALF),
                             m.ring4[:, r * HALF:(r + 1) * HALF, D:2 * D]).then_inc(kept[r], 16)
                if not (isinstance(j, int) and j == 0):
                    sp.wait_ge(kept[r - 1], 16 * i + (16 if r else 0))
                    sp.wait_ge(multiplied, j)
                    sp.sem_inc(free, 1)

            sp.sem_inc(free, 4)
            for r in range(4):
                keep(r, r, 0)
            with sp.Fori(1, TURNS // 2) as i:
                for r in range(4):
                    keep(4 * i + r, r, i)
            sp.wait_ge(kept[3], 16 * (TURNS // 2))

        @block.tensor
        def _(pe):
            regs = registers(nc, pe, "sc1pe")

            def queries(j, h):
                pe.wait_ge(hit_ready, j + 1)
                wait(pe, copied, j - 1)
                for k in range(HALF):
                    mm = pe.transpose(m.bank(4 + h)[:, k * P:(k + 1) * P], m.hit[:, h, k, :], m.ident[:, :])
                mm.then_inc(turned, 1)
                at = load_blocks(pe, regs, m, j * HALF)
                pe.wait_ge(copied, j + 1)
                wait(pe, multiplied, j - 1)
                for k in range(HALF):
                    mm = pe.matmul(m.bank(6 + h)[:, k * P:(k + 1) * P], m.hitT[:, h, k, :],
                                   m.q[:, ds(at[k] * D, D)], start=True, stop=True)
                mm.then_inc(q_ready, 1)

            queries(0, 0)
            queries(1, 1)
            with pe.Fori(1, TURNS) as i:
                queries(2 * i, 0)
                queries(2 * i + 1, 1)

        @block.scalar
        def _(act):
            def half(j, r):
                act.wait_ge(turned, j + 1)
                wait(act, q_ready, j - 1)
                act.activation(m.hitT[:, r % 2], m.bank(4 + r % 2).rearrange("p (k n) -> p k n", k=HALF), ACT.Copy).then_inc(copied, 1)
                wait(act, reduced, j)
                copy_indices(act, m, j + 3, (r + 3) % 4, issued, idx_copied)

            for j in range(3):
                copy_indices(act, m, j, j, issued, idx_copied)
            for j in range(4):
                half(j, j)
            with act.Fori(1, TURNS // 2) as i:
                for r in range(4):
                    half(4 * i + r, r)

        @block.vector
        def _(dve):
            prod = m.prod[:, :].rearrange("p (k n) -> p k n", k=HALF)

            def half(i, j, r):
                wait(dve, turned, j)
                hits(dve, m, (r + 1) % 2, (j + 1) * HALF).then_inc(hit_ready, 1)
                dve.wait_ge(q_ready, j + 1)
                dve.wait_ge(gathered[r], before + 64 * i + 64)
                wait(dve, reduced, j)
                dve.tensor_tensor(prod, m.ring4[:, r * HALF:(r + 1) * HALF, 0:D],
                                  m.bank(6 + r % 2).rearrange("p (k n) -> p k n", k=HALF), ALU.mult).then_inc(multiplied, 1)
                dve.wait_ge(multiplied, j + 1)
                dve.tensor_reduce(m.score[:, ds(j * HALF * H1, HALF * H1)],
                                  m.prod[:, :].rearrange("p (n c) -> p n c", c=C1), AX.X, ALU.add).then_inc(reduced, 1)

            hits(dve, m, 0, 0).then_inc(hit_ready, 1)
            for r in range(4):
                half(0, r, r)
            with dve.Fori(1, TURNS // 2) as i:
                for r in range(4):
                    half(i, 4 * i + r, r)
            dve.memset(m.score[:, STEPS * H1:SC], 0.0).then_inc(reduced, 1)


def sum_values(nc, m, edge_values):
    with Phase(nc, "va1", "used added hit_ready weights_ready weighted read0 read1 read2 read3") as (
            block, used, added, hit_ready, weights_ready, weighted, read0, read1, read2, read3):
        read = (read0, read1, read2, read3)

        @block.sync
        def _(sp):
            def load(j, r):
                wait(sp, weighted, j - 3)
                sp.dma_start(m.ring4[:, r * HALF:(r + 1) * HALF, 0:D],
                             edge_values[ds(j * P, P), :].rearrange("p (k f) -> p k f", k=HALF)).then_inc(read[r], 16)

            for r in range(4):
                load(r, r)
            with sp.Fori(1, TURNS // 2) as i:
                for r in range(4):
                    load(4 * i + r, r)

        @block.tensor
        def _(pe):
            with pe.Fori(0, TURNS) as i:
                for h in range(2):
                    j = 2 * i + h
                    pe.wait_ge(hit_ready, j + 1)
                    pe.wait_ge(weighted, j + 1)
                    pe.wait_ge(weights_ready, j + 1)
                    pe.wait_ge(added, j * HALF + HALF)
                    for k in range(HALF):
                        pe.matmul(m.bank(h * HALF + k, A1), m.hit[:, h, k, :], m.msg[:, h, k, 0:A1],
                                  start=True, stop=True).then_inc(used, 1)

        @block.scalar
        def _(act):
            with act.Fori(0, TURNS) as i:
                for h in range(2):
                    act.wait_ge(added, i * UNROLL + (h + 1) * HALF)
                    act.activation(m.msg[:, h, :, D:A1],
                                   m.weight[:, ds((i * UNROLL + h * HALF) * H1, HALF * H1)].rearrange("p (k n) -> p k n", n=H1),
                                   ACT.Copy).then_inc(weights_ready, 1)

        @block.vector
        def _(dve):
            regs = registers(nc, dve, "va1", 4 * HALF)
            dve.sem_inc(added, UNROLL)

            def half(i, j, r, at):
                h = r % 2
                first = isinstance(j, int) and j < 2
                for k in range(HALF):
                    if not first:
                        to = m.sums[:, ds(at[k] * A1, A1)]
                        if k == 0:
                            dve.wait_ge(used, (j - 1) * HALF)
                        dve.wait_ge(added, j * HALF + k)
                        dve.tensor_tensor(to, to, m.bank(h * HALF + k, A1), ALU.add).then_inc(added, 1)
                    part = slice(k % 2 * 2, k % 2 * 2 + 2)
                    first_step = j * HALF + k % 2 * 2
                    if k < 2:
                        op = dve.tensor_tensor(m.hit[:, h, part], copies(m.number[:, :], 1, 2),
                                               copies(m.local[:, ds(first_step, 2)], 2, P), ALU.is_equal)
                        if k == 1:
                            op.then_inc(hit_ready, 1)
                    else:
                        if k == 2:
                            dve.wait_ge(read[r], 16 * i + 16)
                        op = dve.tensor_tensor(
                            m.msg[:, h, part, 0:D].rearrange("p k (n c) -> p k n c", c=C1),
                            m.ring4[:, r * HALF + part.start:r * HALF + part.stop, 0:D].rearrange("p k (n c) -> p k n c", c=C1),
                            copies(m.weight[:, ds(first_step * H1, 2 * H1)].rearrange("p (k n) -> p k n", n=H1), 3, C1), ALU.mult)
                        if k == 3:
                            op.then_inc(weighted, 1)

            at = load_steps(dve, regs, m.block, 0, BLOCKS - 1)
            for j in range(4):
                half(0, j, j, at[(j - 2) * HALF:] if j >= 2 else None)
            with dve.Fori(1, TURNS // 2) as i:
                at = load_steps(dve, regs, m.block, i * 4 * HALF - 2 * HALF, BLOCKS - 1)
                for r in range(4):
                    half(i, 4 * i + r, r, at[r * HALF:])
            last = load_steps(dve, regs, m.block, (2 * TURNS - 2) * HALF, BLOCKS - 1)
            for j in (2 * TURNS - 2, 2 * TURNS - 1):
                at = last[(j - 2 * TURNS + 2) * HALF:]
                for k in range(HALF):
                    to = m.sums[:, ds(at[k] * A1, A1)]
                    dve.wait_ge(used, j * HALF + k + 1)
                    dve.wait_ge(added, UNROLL + j * HALF + k)
                    dve.tensor_tensor(to, to, m.bank(j % 2 * HALF + k, A1), ALU.add).then_inc(added, 1)


def softmax_rows(nc, m):
    with Phase(nc, "sr1", "turned copied placed taken") as (block, turned, copied, placed, taken):
        by_step = m.score.rearrange("p (s h) -> p h s", h=H1)
        turned_scores = m.stage_c[:, 0:H1 * P]
        turned_picks = m.stage_a[:, 0:2 * P]

        @block.tensor
        def _(pe):
            for j in range(ROWS):
                c = slice(j * P, (j + 1) * P)
                if j:
                    pe.wait_ge(copied, 2 * j)
                for h in range(H1):
                    pe.transpose(m.bank(0)[:, h * P:(h + 1) * P], by_step[:, h, c], m.ident[:, :])
                pe.transpose(m.bank(1)[:, 0:P], m.pick0[:, c], m.ident[:, :])
                pe.transpose(m.bank(1)[:, P:2 * P], m.pick1[:, c], m.ident[:, :]).then_inc(turned, 1)
                pe.wait_ge(copied, 2 * (j + 1))
                if j >= 2:
                    pe.wait_ge(taken, j - 1)
                pe.matmul(m.bank(2 + j % 2), turned_picks[:, 0:P], turned_scores, start=True,
                          stop=(j == ROWS - 1)).then_inc(placed, 1)
                if j:
                    pe.matmul(m.bank(2 + (j - 1) % 2), turned_picks[:, P:2 * P], turned_scores,
                              start=False, stop=True).then_inc(placed, 1)

        @block.scalar
        def _(act):
            for j in range(ROWS):
                act.wait_ge(turned, j + 1)
                if j:
                    act.wait_ge(placed, 2 * j - 1)
                act.activation(turned_scores, m.bank(0), ACT.Copy).then_inc(copied, 1)
                act.activation(turned_picks, m.bank(1, 2 * P), ACT.Copy).then_inc(copied, 1)

        @block.vector
        def _(dve):
            for j in range(ROWS):
                dve.wait_ge(placed, min(2 * (j + 2) - 1, 2 * ROWS - 1))
                dve.tensor_copy(m.srow[:, j], m.bank(2 + j % 2).rearrange("p (h e) -> p h e", h=H1)).then_inc(taken, 1)


def softmax_weights(nc, m):
    with Phase(nc, "sw1", "linked first ends turned rowed seven chained back backed second maxed exped drawn stored") as (
            block, linked, first, ends, turned, rowed, seven, chained, back, backed, second, maxed, exped, drawn, stored):
        links = m.x_scratch
        dst = m.dst_rows[:, :].rearrange("p (j e) -> p j e", e=P)
        ends_of = m.small[:, 0:ROWS * 4 * H1].rearrange("p (j q h) -> p j q h", q=4, h=H1)
        carried = m.small[:, 128:128 + ROWS * 2 * H1].rearrange("p (j q h) -> p j q h", q=2, h=H1)
        row = lambda t, a=0: t[0:H1, a:a + COLS]
        last_max, first_max = row(m.stage_a), row(m.stage_b)
        first_dst, last_dst = row(m.stage_c), row(m.stage_c, COLS)
        flat = m.hit.rearrange("p a k n -> p (a k n)")
        flat_t = m.hitT.rearrange("p a k n -> p (a k n)")
        flat_m = m.msg.rearrange("p a k n -> p (a k n)")
        cont, single = row(m.stage_d), row(m.stage_d, COLS)
        onward, backward, penalty = row(flat), row(flat_t), row(flat_m)

        def run(dve, starts, sem):
            for j in range(ROWS):
                for h in range(H1):
                    for to, q in ((m.fwd, 0), (m.bwd, 1)):
                        start = -BIG if starts is None else starts[:, j, q, h:h + 1]
                        if q == 0:
                            dve.tensor_tensor_scan(to[:, j, h, :], links[:, j, 0:P], m.srow[:, j, h, :], start,
                                                   ALU.add, ALU.max).then_inc(sem, 1)
                        else:
                            dve.tensor_tensor_scan(to[:, j, h, ::-1], links[:, j, P:0:-1], m.srow[:, j, h, ::-1], start,
                                                   ALU.add, ALU.max).then_inc(sem, 1)

        @block.vector
        def _(dve):
            dve.memset(links[:, :, 0:1], 0.0).then_inc(linked, 1)
            dve.memset(links[:, :, P:P + 1], 0.0).then_inc(linked, 1)
            dve.tensor_tensor(links[:, :, 1:P], dst[:, :, 1:P], dst[:, :, 0:P - 1], ALU.is_equal).then_inc(linked, 1)
            dve.wait_ge(linked, 3)
            dve.tensor_scalar(links[:, :, 1:P], links[:, :, 1:P], -1.0, BIG, ALU.add, ALU.mult).then_inc(linked, 1)
            dve.wait_ge(linked, 4)
            run(dve, None, first)
            dve.wait_ge(first, 2 * ROWS * H1)
            dve.tensor_copy(ends_of[:, :, 0, :], m.fwd[:, :, :, P - 1]).then_inc(ends, 1)
            dve.tensor_copy(ends_of[:, :, 1, :], m.bwd[:, :, :, 0]).then_inc(ends, 1)
            dve.tensor_copy(ends_of[:, :, 2, :], copies(dst[:, :, 0], 2, H1)).then_inc(ends, 1)
            dve.tensor_copy(ends_of[:, :, 3, :], copies(dst[:, :, P - 1], 2, H1)).then_inc(ends, 1)
            for q, to in enumerate((last_max, first_max, first_dst, last_dst)):
                dve.wait_ge(turned, q + 1)
                dve.tensor_copy(to, m.ps[0:H1, 1024 * q:1024 * q + COLS]).then_inc(rowed, 1)
            dve.wait_ge(rowed, 4)
            dve.memset(cont[:, 0:1], 0.0).then_inc(seven, 1)
            dve.tensor_tensor(cont[:, 1:COLS], first_dst[:, 1:COLS], last_dst[:, 0:COLS - 1], ALU.is_equal).then_inc(seven, 1)
            dve.tensor_tensor(single, first_dst, last_dst, ALU.is_equal).then_inc(seven, 1)
            dve.memset(backward[:, COLS - 1:COLS], 0.0).then_inc(seven, 1)
            dve.wait_ge(seven, 4)
            dve.tensor_tensor(onward, cont, single, ALU.mult).then_inc(seven, 1)
            dve.tensor_tensor(backward[:, 0:COLS - 1], cont[:, 1:COLS], single[:, 0:COLS - 1], ALU.mult).then_inc(seven, 1)
            dve.wait_ge(seven, 6)
            for t_, f_ in ((onward, onward), (backward, backward), (penalty, cont)):
                dve.tensor_scalar(t_, f_, -1.0, BIG, ALU.add, ALU.mult).then_inc(seven, 1)
            dve.wait_ge(seven, 9)
            dve.tensor_tensor_scan(onward, onward, last_max, -BIG, ALU.add, ALU.max).then_inc(chained, 1)
            dve.tensor_tensor_scan(backward[:, ::-1], backward[:, ::-1], first_max[:, ::-1], -BIG, ALU.add, ALU.max).then_inc(chained, 1)
            dve.wait_ge(chained, 2)
            dve.memset(last_max[:, 0:1], -BIG).then_inc(chained, 1)
            dve.memset(first_max[:, COLS - 1:COLS], -BIG).then_inc(chained, 1)
            dve.tensor_tensor(last_max[:, 1:COLS], onward[:, 0:COLS - 1], penalty[:, 1:COLS], ALU.add).then_inc(chained, 1)
            dve.tensor_tensor(first_max[:, 0:COLS - 1], backward[:, 1:COLS], penalty[:, 1:COLS], ALU.add).then_inc(chained, 1)
            dve.wait_ge(back, 1)
            dve.tensor_copy(m.small[:, 128:128 + ROWS * 2 * H1], m.ps[:, 0:ROWS * 2 * H1]).then_inc(backed, 1)
            dve.wait_ge(backed, 1)
            run(dve, carried, second)
            dve.wait_ge(second, 2 * ROWS * H1)
            for j in range(ROWS):
                dve.tensor_tensor(m.fwd[:, j], m.fwd[:, j], m.bwd[:, j], ALU.max).then_inc(maxed, 1)
            for j in range(ROWS):
                dve.wait_ge(maxed, j + 1)
                dve.tensor_tensor(m.srow[:, j], m.srow[:, j], m.fwd[:, j], ALU.subtract).then_inc(maxed, 1)
            for j in range(ROWS):
                dve.wait_ge(drawn, j + 1)
                dve.wait_ge(maxed, 2 * ROWS)
                dve.tensor_copy(m.weight[:, j * P * H1:(j + 1) * P * H1].rearrange("p (s h) -> p h s", h=H1),
                                m.bank(1 + j % 2).rearrange("p (h s) -> p h s", h=H1)).then_inc(stored, 1)

        @block.scalar
        def _(act):
            for j in range(ROWS):
                act.wait_ge(maxed, ROWS + j + 1)
                act.activation(m.srow[:, j], m.srow[:, j], ACT.Exp, scale=float(C1) ** -0.5).then_inc(exped, 1)

        @block.tensor
        def _(pe):
            pe.wait_ge(ends, 4)
            for q in range(4):
                for j in range(ROWS):
                    mm = pe.transpose(m.ps[0:H1, 1024 * q + j * P:1024 * q + (j + 1) * P], ends_of[:, j, q, :], m.ident[:, :])
                mm.then_inc(turned, 1)
            pe.wait_ge(chained, 6)
            pe.wait_ge(rowed, 4)
            for j in range(ROWS):
                for q, of in enumerate((last_max, first_max)):
                    mm = pe.transpose(m.ps[:, (2 * j + q) * H1:(2 * j + q + 1) * H1], of[:, j * P:(j + 1) * P], m.ident[0:H1, 0:H1])
            mm.then_inc(back, 1)
            for j in range(ROWS):
                pe.wait_ge(exped, j + 1)
                if j >= 2:
                    pe.wait_ge(stored, j - 1)
                for h in range(H1):
                    out = m.bank(1 + j % 2)[:, h * P:(h + 1) * P]
                    mm = pe.matmul(out, m.srow[:, j, h, :], m.pick0[:, j * P:(j + 1) * P], start=True, stop=(j == 0))
                    if j:
                        mm = pe.matmul(out, m.srow[:, j - 1, h, :], m.pick1[:, j * P:(j + 1) * P], start=False, stop=True)
                mm.then_inc(drawn, 1)


CHUNKS = ((0, 512), (512, GN))


def blocks(ap, n=P):
    return ap.rearrange("p (b n) -> p b n", n=n)


def turn_blocks(pe, m, bank, of, rows=P):
    for b in range(GB):
        out = m.ps[0:rows, 512 * bank + b * P:512 * bank + (b + 1) * P]
        mm = pe.transpose(out, of[:, b * P:b * P + rows], m.ident[:, :])
    return mm


def feature_product(pe, m, bank, pairs):
    for a, b in CHUNKS:
        for n, (w, x) in enumerate(pairs):
            mm = pe.matmul(m.ps[:, 512 * bank + a:512 * bank + b], w, x[:, a:b], start=(n == 0), stop=(n == len(pairs) - 1))
    return mm


def normalize(dve, m, at, to, stats, summing, root, rooted, inverted, step, g):
    six = m.small[:, 256:256 + 6 * GB].rearrange("p (b n) -> p b n", n=6)
    two = m.small[:, 304:304 + 2 * GB].rearrange("p (b n) -> p b n", n=2)
    std = m.small[:, 320:320 + GB]
    base = g * (2 * GB)
    for b in range(GB):
        dve.bn_stats(six[:, b, :], at[:, b * P:(b + 1) * P]).then_inc(stats, 1)
    dve.wait_ge(stats, base + GB)
    dve.sem_inc(summing, 1)
    for b in range(GB):
        dve.bn_aggr(two[:, b, :], six[:, b, :]).then_inc(stats, 1)
    dve.wait_ge(rooted, g + 1)
    dve.reciprocal(std, root).then_inc(inverted, 1)
    dve.wait_ge(inverted, g + 1)
    for b in range(GB):
        dve.tensor_scalar(to[:, b * P:(b + 1) * P], at[:, b * P:(b + 1) * P], two[:, b, 0:1], std[:, b:b + 1],
                          ALU.subtract, ALU.mult).then_inc(step, 1)


def take_roots(act, m, root, stats, rooted, g):
    two = m.small[:, 304:304 + 2 * GB].rearrange("p (b n) -> p b n", n=2)
    act.wait_ge(stats, g * (2 * GB) + 2 * GB)
    act.activation(root, two[:, :, 1], ACT.Sqrt, bias=m.eps[:, 0:1]).then_inc(rooted, 1)


def project0(nc, m, t, table):
    with Phase(nc, "pr0", "loaded projected dve_out act_out stage_free zeroed", m.pool_stored) as (
            block, loaded, projected, dve_out, act_out, stage_free, zeroed, stored):
        before = m.stored_before
        m.stored_before += 16 * GROUPS
        share = {0: (GB + 1) // 2, 1: GB // 2}

        @block.sync
        def _(sp):
            with sp.Fori(0, GROUPS) as g:
                sp.wait_ge(projected, g * GB + GB)
                sp.dma_start(m.stage_a[:, :], t["xT"][:, ds(g * GN, GN)]).then_inc(loaded, 16)

        @block.tensor
        def _(pe):
            pe.sem_inc(projected, GB)
            with pe.Fori(0, GROUPS) as g:
                pe.wait_ge(loaded, g * 16 + 16)
                for b in range(GB):
                    pe.wait_ge((dve_out, act_out)[b % 2], g * share[b % 2] + b // 2 + 1)
                    pe.matmul(m.bank(b, 3 * D), m.stage_a[:, b * P:(b + 1) * P], m.w["wqkv0"][:, 0, :],
                              start=True, stop=True).then_inc(projected, 1)

        @block.vector
        def _(dve):
            dve.sem_inc(dve_out, share[0])
            dve.memset(m.sums[:, 0:BLOCKS * A0], 0.0).then_inc(zeroed, 1)
            dve.memset(m.eps[:, :], 1e-5).then_inc(zeroed, 1)
            with dve.Fori(0, GROUPS) as g:
                dve.wait_ge(stage_free, g + 1)
                for b in range(0, GB, 2):
                    dve.wait_ge(projected, g * GB + GB + b + 1)
                    dve.tensor_copy(m.q[:, ds((g * GB + b) * D, D)], m.bank(b)[:, 0:D])
                    dve.tensor_copy(m.stage_c[:, b * 2 * D:(b + 1) * 2 * D], m.bank(b)[:, D:3 * D]).then_inc(dve_out, 1)

        @block.scalar
        def _(act):
            act.sem_inc(act_out, share[1])
            with act.Fori(0, GROUPS) as g:
                act.wait_ge(stage_free, g + 1)
                for b in range(1, GB, 2):
                    act.wait_ge(projected, g * GB + GB + b + 1)
                    act.activation(m.q[:, ds((g * GB + b) * D, D)], m.bank(b)[:, 0:D], ACT.Copy)
                    act.activation(m.stage_c[:, b * 2 * D:(b + 1) * 2 * D], m.bank(b)[:, D:3 * D], ACT.Copy).then_inc(act_out, 1)

        @block.gpsimd
        def _(pool):
            pool.sem_inc(stage_free, 1)
            with pool.Fori(0, GROUPS) as g:
                pool.wait_ge(dve_out, (g + 2) * share[0])
                pool.wait_ge(act_out, (g + 2) * share[1])
                pool.dma_start(group_rows(table, g), blocks(m.stage_c[:, :], 2 * D)).then_inc(stored, 16)
                pool.wait_ge(stored, before + g * 16 + 16)
                pool.sem_inc(stage_free, 1)


def batch_stats(dve, m, stats, weight, bias, rooted, scaled):
    n, parts = 250, NODES // 250
    six = m.small[:, 0:6 * parts].rearrange("p (b n) -> p b n", n=6)
    for b in range(parts):
        dve.bn_stats(six[:, b, :], m.feat[:, b * n:(b + 1) * n]).then_inc(stats, 1)
    dve.wait_ge(stats, parts)
    dve.bn_aggr(m.mean_var, m.small[:, 0:6 * parts]).then_inc(stats, 1)
    dve.wait_ge(rooted, 1)
    dve.reciprocal(m.scale, m.scale).then_inc(scaled, 1)
    dve.wait_ge(scaled, 1)
    dve.tensor_tensor(m.scale, m.scale, weight, ALU.mult).then_inc(scaled, 1)
    dve.wait_ge(scaled, 2)
    dve.tensor_tensor(m.shift, m.mean_var[:, 0:1], m.scale, ALU.mult).then_inc(scaled, 1)
    dve.wait_ge(scaled, 3)
    dve.tensor_tensor(m.shift, bias, m.shift, ALU.subtract).then_inc(scaled, 1)


def batch_root(act, m, stats, rooted):
    act.wait_ge(stats, NODES // 250 + 1)
    act.activation(m.scale, m.mean_var[:, 1:2], ACT.Sqrt, bias=m.eps[:, 0:1]).then_inc(rooted, 1)


def attend_out(nc, m, t):
    with Phase(nc, "ao0", "loaded inv scaled_in turned copied out done degs rooted2 stats rooted scaled") as (
            block, loaded, inv, scaled_in, turned, copied, out, done, degs, rooted2, stats, rooted, scaled):
        z = blocks(m.small[:, 200:200 + GB * H0], H0)
        deg = m.small[:, 400:400 + BLOCKS]

        @block.sync
        def _(sp):
            with sp.Fori(0, GROUPS) as g:
                sp.wait_ge(done, g + 1)
                sp.dma_start(m.stage_c[:, 0:GN], t["xT"][:, ds(g * GN, GN)]).then_inc(loaded, 16)

        @block.vector
        def _(dve):
            dve.sem_inc(done, 1)
            with dve.Fori(0, GROUPS) as g:
                s = blocks(m.sums[:, ds(g * (GB * A0), GB * A0)], A0)
                dve.tensor_scalar(z, s[:, :, D:D + H0], 1e-6, None, ALU.add).then_inc(inv, 1)
                dve.wait_ge(inv, g * 2 + 1)
                dve.reciprocal(z, z).then_inc(inv, 1)
                dve.wait_ge(inv, g * 2 + 2)
                dve.tensor_tensor(blocks(m.stage_a[:, :]).rearrange("p b (n c) -> p b n c", c=C0),
                                  s[:, :, 0:D].rearrange("p b (n c) -> p b n c", c=C0), copies(z, 3, C0),
                                  ALU.mult).then_inc(scaled_in, 1)
                dve.wait_ge(out, g + 1)
                dve.wait_ge(loaded, g * 16 + 16)
                dve.scalar_tensor_tensor(m.feat[:, ds(g * GN, GN)], m.ps[:, 1024:1024 + GN], m.column["bo"],
                                         m.stage_c[:, 0:GN], ALU.add, ALU.add).then_inc(done, 1)
            dve.tensor_scalar(deg, blocks(m.sums[:, 0:BLOCKS * A0], A0)[:, :, A0 - 1], 1.0, None, ALU.add).then_inc(degs, 1)
            dve.wait_ge(rooted2, 1)
            dve.reciprocal(m.norm[:, :], m.norm[:, :]).then_inc(degs, 1)
            dve.wait_ge(done, GROUPS + 1)
            batch_stats(dve, m, stats, m.column["n1w"], m.column["n1b"], rooted, scaled)

        @block.tensor
        def _(pe):
            with pe.Fori(0, GROUPS) as g:
                pe.wait_ge(scaled_in, g + 1)
                turn_blocks(pe, m, 0, m.stage_a).then_inc(turned, 1)
                pe.wait_ge(copied, g + 1)
                feature_product(pe, m, 2, [(m.w["wo"][:, 0, :], m.stage_b)]).then_inc(out, 1)

        @block.scalar
        def _(act):
            with act.Fori(0, GROUPS) as g:
                act.wait_ge(turned, g + 1)
                act.activation(m.stage_b[:, :], m.ps[:, 0:GN], ACT.Copy).then_inc(copied, 1)
            act.wait_ge(degs, 1)
            act.activation(m.norm[:, :], deg, ACT.Sqrt).then_inc(rooted2, 1)
            batch_root(act, m, stats, rooted)


def feed_forward(nc, m):
    with Phase(nc, "ff0", "normed hidden relu0 relu1 out done stats rooted scaled") as (
            block, normed, hidden, relu0, relu1, out, done, stats, rooted, scaled):
        act0, act1 = m.stage_c[:, 0:GN], m.stage_c[:, GN:2 * GN]

        @block.scalar
        def _(act):
            act.sem_inc(done, 1)
            with act.Fori(0, GROUPS) as g:
                act.wait_ge(done, g + 1)
                act.activation(m.stage_a[:, :], m.feat[:, ds(g * GN, GN)], ACT.Identity,
                               bias=m.shift, scale=m.scale).then_inc(normed, 1)
                act.wait_ge(hidden, g * 2 + 1)
                act.activation(act0, m.ps[:, 0:GN], ACT.Relu, bias=m.column["b1"][:, 0:1]).then_inc(relu0, 1)
            batch_root(act, m, stats, rooted)

        @block.tensor
        def _(pe):
            with pe.Fori(0, GROUPS) as g:
                pe.wait_ge(normed, g + 1)
                for o in range(2):
                    feature_product(pe, m, 2 * o, [(m.w["w1"][:, 0, o * P:(o + 1) * P], m.stage_a)]).then_inc(hidden, 1)
                pe.wait_ge(relu0, g + 1)
                pe.wait_ge(relu1, g + 1)
                feature_product(pe, m, 4, [(m.w["w2"][:, 0, :], act0), (m.w["w2"][:, 1, :], act1)]).then_inc(out, 1)

        @block.vector
        def _(dve):
            with dve.Fori(0, GROUPS) as g:
                dve.wait_ge(hidden, g * 2 + 2)
                dve.tensor_scalar(act1, m.ps[:, 1024:1024 + GN], m.column["b1"][:, 1:2], 0.0, ALU.add, ALU.max).then_inc(relu1, 1)
                dve.wait_ge(out, g + 1)
                dve.scalar_tensor_tensor(m.feat[:, ds(g * GN, GN)], m.ps[:, 2048:2048 + GN], m.column["b2"],
                                         m.stage_a[:, :], ALU.add, ALU.add).then_inc(done, 1)
            dve.wait_ge(done, GROUPS + 1)
            batch_stats(dve, m, stats, m.column["n2w"], m.column["n2b"], rooted, scaled)


def project1(nc, m, t, table):
    with Phase(nc, "pr1", "normed turned added stats summing rooted inverted lned turned2 copied2 projected "
               "evened evac stage_free done kept", m.pool_stored) as (
            block, normed, turned, added, stats, summing, rooted, inverted, lned, turned2, copied2, projected,
            evened, evac, stage_free, done, kept, stored):
        before = m.stored_before
        m.stored_before += 16 * GROUPS
        root = m.small[:, 330:330 + GB]

        @block.scalar
        def _(act):
            act.sem_inc(done, 1)
            with act.Fori(0, GROUPS) as g:
                act.wait_ge(done, g + 1)
                act.activation(m.stage_d[:, 0:GN], m.feat[:, ds(g * GN, GN)], ACT.Identity,
                               bias=m.shift, scale=m.scale).then_inc(normed, 1)
                take_roots(act, m, root, stats, rooted, g)
                act.wait_ge(lned, g * GB + GB)
                act.activation(m.x[:, ds(g * GN, GN)], m.stage_b[:, :], ACT.Copy).then_inc(kept, 1)
                act.wait_ge(turned2, g + 1)
                act.activation(m.stage_a[:, :], m.ps[:, 1024:1024 + GN], ACT.Copy).then_inc(copied2, 1)
                act.wait_ge(turned, g + 1)
                act.sem_inc(done, 1)

        @block.tensor
        def _(pe):
            pe.sem_inc(evened, 4)
            with pe.Fori(0, GROUPS) as g:
                pe.wait_ge(normed, g + 1)
                turn_blocks(pe, m, 0, m.stage_d).then_inc(turned, 1)
                pe.wait_ge(lned, g * GB + GB)
                turn_blocks(pe, m, 2, m.stage_b).then_inc(turned2, 1)
                pe.wait_ge(copied2, g + 1)
                for b in range(GB):
                    if b >= 4:
                        pe.wait_ge(evac, g * 3 * GB + 3 * (b - 3))
                    pe.matmul(m.bank(4 + b % 4), m.stage_a[:, b * P:(b + 1) * P], m.w["wqkvs"][:, 0, :],
                              start=True, stop=True).then_inc(projected, 1)

        @block.vector
        def _(dve):
            dve.sem_inc(kept, 1)
            with dve.Fori(0, GROUPS) as g:
                dve.wait_ge(turned, g + 1)
                dve.wait_ge(kept, g + 1)
                dve.tensor_tensor(m.stage_b[:, :], m.ps[:, 0:GN], m.x[:, ds(g * GN, GN)], ALU.add).then_inc(added, 1)
                dve.wait_ge(added, g + 1)
                normalize(dve, m, m.stage_b, m.stage_b, stats, summing, root, rooted, inverted, lned, g)
                bias = m.spread["bqkvs"]
                dve.wait_ge(stage_free, g + 1)
                for b in range(GB):
                    dve.wait_ge(projected, g * GB + b + 1)
                    ps = m.bank(4 + b % 4)
                    at = (g * GB + b) * D
                    dve.tensor_tensor(m.q[:, ds(at, D)], ps[:, 0:D], bias[:, 0:D], ALU.add).then_inc(evac, 1)
                    dve.tensor_tensor(m.stage_c[:, b * 2 * D:(b + 1) * 2 * D], ps[:, D:3 * D], bias[:, D:3 * D],
                                      ALU.add).then_inc(evac, 1)
                    dve.tensor_tensor(m.feat[:, ds(at, D)], ps[:, 3 * D:4 * D], bias[:, 3 * D:4 * D], ALU.add).then_inc(evac, 1)

        @block.gpsimd
        def _(pool):
            kv = blocks(m.stage_c[:, :], 2 * D)
            pool.sem_inc(stage_free, 1)
            with pool.Fori(0, GROUPS) as g:
                pool.wait_ge(evac, g * 3 * GB + 3 * GB)
                pool.dma_start(group_rows(table, g), kv).then_inc(stored, 16)
                pool.wait_ge(stored, before + g * 16 + 16)
                pool.sem_inc(stage_free, 1)


def skip_gate(nc, m, table):
    with Phase(nc, "sg1", "vec gate stats summing rooted inverted lned turned copied xed projected placed stored done") as (
            block, vec, gate, stats, summing, rooted, inverted, lned, turned, copied, xed, projected, placed, stored, done):
        root = m.small[:, 330:330 + GB]
        z = blocks(m.small[:, 200:200 + GB * H1], H1)
        logit, beta = m.small[:, 340:340 + GB], m.small[:, 350:350 + GB]
        wbeta = m.spread["wbeta"]
        steps = 11

        @block.vector
        def _(dve):
            dve.tensor_tensor(m.prod[:, 0:D], wbeta[:, 0:D], wbeta[:, 2 * D:3 * D], ALU.add).then_inc(vec, 1)
            dve.tensor_tensor(m.prod[:, D:2 * D], wbeta[:, D:2 * D], wbeta[:, 2 * D:3 * D], ALU.subtract).then_inc(vec, 1)

            def place(g):
                dve.wait_ge(projected, g + 1)
                dve.tensor_tensor(blocks(m.sums[:, ds(g * GN, GN)])[:, :, 0:HID], blocks(m.ps[:, 1024:1024 + GN])[:, :, 0:HID],
                                  copies(m.norm[:, ds(g * GB, GB)], 2, HID), ALU.mult).then_inc(placed, 1)

            def group(g):
                s = blocks(m.sums[:, ds(g * (GB * A1), GB * A1)], A1)
                skip = m.feat[:, ds(g * GN, GN)]
                a, b, c = m.stage_a[:, :], m.stage_b[:, :], m.stage_c[:, 0:GN]
                after = lambda n: dve.wait_ge(vec, g * steps + 2 + n)
                after(0)
                wait(dve, xed, g)
                dve.tensor_scalar(z, s[:, :, D:A1], 1e-16, None, ALU.max).then_inc(vec, 1)
                after(1)
                dve.reciprocal(z, z).then_inc(vec, 1)
                after(2)
                dve.tensor_tensor(blocks(a).rearrange("p b (n c) -> p b n c", c=C1),
                                  s[:, :, 0:D].rearrange("p b (n c) -> p b n c", c=C1), copies(z, 3, C1), ALU.mult).then_inc(vec, 1)
                dve.tensor_tensor(blocks(b), blocks(skip), copies(m.prod[:, D:2 * D], 1, GB), ALU.mult).then_inc(vec, 1)
                after(4)
                dve.tensor_tensor(blocks(c), blocks(a), copies(m.prod[:, 0:D], 1, GB), ALU.mult).then_inc(vec, 1)
                after(5)
                dve.tensor_tensor(b, b, c, ALU.add).then_inc(vec, 1)
                if not (isinstance(g, int) and g == 0):
                    place(g - 1)
                after(6)
                dve.tensor_reduce(logit, blocks(b), AX.X, ALU.add).then_inc(vec, 1)
                dve.tensor_tensor(c, skip, a, ALU.subtract).then_inc(vec, 1)
                after(8)
                dve.tensor_tensor(a, a, m.x[:, ds(g * GN, GN)], ALU.add).then_inc(vec, 1)
                dve.wait_ge(gate, g + 1)
                dve.tensor_tensor(blocks(c), blocks(c), copies(beta, 2, P), ALU.mult).then_inc(vec, 1)
                after(10)
                dve.tensor_tensor(b, c, a, ALU.add).then_inc(vec, 1)
                after(11)
                normalize(dve, m, m.stage_b, m.stage_b, stats, summing, root, rooted, inverted, lned, g)

            group(0)
            with dve.Fori(1, GROUPS) as g:
                group(g)
            place(GROUPS - 1)

        @block.scalar
        def _(act):
            with act.Fori(0, GROUPS) as g:
                act.wait_ge(vec, g * steps + 2 + 7)
                act.activation(beta, logit, ACT.Sigmoid).then_inc(gate, 1)
                take_roots(act, m, root, stats, rooted, g)
                act.wait_ge(turned, g + 1)
                act.activation(m.stage_d[:, 0:GN], m.ps[:, 0:GN], ACT.Copy).then_inc(copied, 1)
                act.activation(m.x[:, ds(g * GN, GN)], m.stage_b[:, :], ACT.Copy).then_inc(xed, 1)

        @block.tensor
        def _(pe):
            def group(g):
                pe.wait_ge(lned, g * GB + GB)
                turn_blocks(pe, m, 0, m.stage_b).then_inc(turned, 1)
                pe.wait_ge(copied, g + 1)
                wait(pe, placed, g)
                for b in range(GB):
                    mm = pe.matmul(m.ps[:, 1024 + b * P:1024 + b * P + HID], m.stage_d[:, b * P:(b + 1) * P],
                                   m.w["g1"][:, 0, :], start=True, stop=True)
                mm.then_inc(projected, 1)

            group(0)
            with pe.Fori(1, GROUPS) as g:
                group(g)

        store_sums(block, m, table, HID, placed, xed, stored, done)


def plan_windows(nc, m, t, x_table):
    with Phase(nc, "pw", "rows_in made vec compared counted picked drawn kept") as (
            block, rows_in, made, vec, compared, counted, picked, drawn, kept):
        dst_i, src_i = m.rows_i[:, 0:COLS], m.rows_i[:, COLS:2 * COLS]
        dst_f, src_f = m.rows_f[:, 0:COLS], m.rows_f[:, COLS:2 * COLS]
        q = WCOLS // 4
        two = m.wwork[0:2]
        a, b, c = m.wwork
        rank, first_i, first_f = m.small[:, 0:ROWS], m.small[:, 8:8 + ROWS].bitcast(I32), m.small[:, 16:16 + ROWS]
        ps4 = lambda k: m.ps[:, 2048 * k:2048 * (k + 1)].rearrange("p (n q) -> p n q", n=4)[:, :, 0:q]
        by4 = lambda x: x.rearrange("p (n q) -> p n q", n=4)

        @block.sync
        def _(sp):
            for to, name in ((dst_i, "dst"), (src_i, "src")):
                sp.dma_start(to.rearrange("p (j e) -> p j e", e=P),
                             t[name].rearrange("(j p) e -> p j e", p=P)).then_inc(rows_in, 16)
            sp.dma_start(x_table.rearrange("(b p) f -> p b f", p=P), blocks(m.x[:, :])).then_inc(kept, 16)
            sp.wait_ge(rows_in, 32)
            sp.wait_ge(kept, 16)

        @block.gpsimd
        def _(pool):
            pool.iota(m.wint, [[1, WCOLS]], base=0, channel_multiplier=0).then_inc(made, 1)
            pool.memset(m.zeros, 0.0).then_inc(made, 1)
            pool.memset(m.slots, 0.0).then_inc(made, 1)

        @block.vector
        def _(dve):
            n = 0

            def then(op):
                nonlocal n
                n += 1
                op.then_inc(vec, 1)
                dve.wait_ge(vec, n)

            dve.wait_ge(made, 3)
            then(dve.tensor_copy(m.wramp, m.wint))
            dve.wait_ge(rows_in, 32)
            then(dve.tensor_copy(m.rows_f, m.rows_i))
            then(dve.tensor_scalar(first_i, dst_i[:, 0:COLS:P], WIN.bit_length() - 1, None, ALU.arith_shift_right))
            then(dve.tensor_copy(first_f, first_i))
            then(dve.tensor_tensor(rank, first_f, m.tile_id[:, :], ALU.add))
            then(dve.tensor_copy(m.count_to, m.wramp[:, 0:WIDE]))
            then(dve.tensor_copy(m.identb[:, :], m.ident[:, :]))
            for j in range(ROWS):
                if j >= 2:
                    dve.wait_ge(counted, 4 * (j - 1))
                dve.tensor_scalar(two[j % 2], m.wramp, rank[:, j:j + 1], None, ALU.is_ge).then_inc(compared, 1)
            dve.wait_ge(counted, 4 * ROWS)
            then(dve.tensor_scalar(by4(m.wtile), ps4(0), -1.0, 0.0, ALU.add, ALU.max))
            for j in range(ROWS):
                if j >= 2:
                    dve.wait_ge(drawn, j - 1)
                dve.tensor_scalar(two[j % 2], m.wtile, m.tile_id[:, j:j + 1], None, ALU.is_equal).then_inc(picked, 1)
            then(dve.tensor_tensor(m.window, m.wramp, m.wtile, ALU.subtract))
            dve.wait_ge(drawn, ROWS)
            then(dve.scalar_tensor_tensor(by4(a), by4(m.window), -float(WIN), ps4(0), ALU.mult, ALU.add))
            then(dve.tensor_copy(by4(m.wint), ps4(1)))
            then(dve.tensor_scalar(b, a, 0.0, None, ALU.is_ge))
            then(dve.scalar_tensor_tensor(b, a, float(WIN), b, ALU.is_lt, ALU.mult))
            then(dve.tensor_scalar(m.ring, m.wint, P - 1, None, ALU.bitwise_and))
            then(dve.tensor_copy(m.lo, m.ring))
            then(dve.tensor_scalar(m.ring, m.wint, P.bit_length() - 1, None, ALU.arith_shift_right))
            then(dve.tensor_copy(c, m.ring))
            then(dve.scalar_tensor_tensor(c, a, float(BLOCKS), c, ALU.mult, ALU.add))
            then(dve.scalar_tensor_tensor(c, c, 1.0, b, ALU.add, ALU.mult))
            then(dve.tensor_scalar(m.place, c, -1.0, None, ALU.add))
            for table, ahead, size in ((m.ring, 0, WIDE), (m.clean, RING // 2, WIDE // 2)):
                then(dve.tensor_scalar(table, m.window, float(ahead), None, ALU.add))
                then(dve.tensor_scalar(table, table, RING - 1, None, ALU.bitwise_and))
                then(dve.tensor_scalar(table, table, float(size), None, ALU.mult))
            even, real = m.wtile, b
            then(dve.tensor_copy(m.wint, m.window))
            then(dve.tensor_scalar(m.wint, m.wint, 1, None, ALU.arith_shift_right))
            then(dve.tensor_copy(even, m.wint))
            then(dve.memset(c, 0.0))
            then(dve.tensor_tensor(c[:, 0:WCOLS - 2], even[:, 2:WCOLS], even[:, 0:WCOLS - 2], ALU.subtract))
            then(dve.tensor_scalar(even, even, 2.0, None, ALU.mult))
            then(dve.tensor_copy(m.wint, even))

            def either(table, spare, size):
                then(dve.tensor_tensor(a, real, spare, ALU.subtract))
                then(dve.tensor_tensor(a, a, c, ALU.mult))
                then(dve.tensor_tensor(a, a, spare, ALU.add))
                then(dve.tensor_scalar(table, a, float(size), None, ALU.mult))

            then(dve.tensor_scalar(m.out_slot, m.wint, RING - 1, None, ALU.bitwise_and))
            then(dve.tensor_scalar(real, m.out_slot, -float(RING), None, ALU.add))
            then(dve.tensor_tensor(a, real, c, ALU.mult))
            then(dve.tensor_scalar(m.out_slot, a, float(RING), float(WIDE), ALU.add, ALU.mult))
            spare = even
            for table, op, by, size in ((m.out_block, ALU.arith_shift_right, SLOTS.bit_length() - 1, P),
                                        (m.out_part, ALU.bitwise_and, SLOTS - 1, WIDE)):
                then(dve.tensor_scalar(table, m.wint, by, None, op))
                then(dve.tensor_copy(real, table))
                then(dve.tensor_copy(table, m.wramp))
                then(dve.tensor_scalar(table, table, by, None, op))
                then(dve.tensor_scalar(spare, table, float(SPARE if size == P else 0), None, ALU.add))
                either(table, spare, size)

        @block.tensor
        def _(pe):
            for j in range(ROWS):
                pe.wait_ge(compared, j + 1)
                for k in range(4):
                    pe.matmul(m.bank(k, q), m.ones[:, :], two[j % 2][:, k * q:(k + 1) * q],
                              start=(j == 0), stop=(j == ROWS - 1)).then_inc(counted, 1)
            for j in range(ROWS):
                pe.wait_ge(picked, j + 1)
                for k in range(8):
                    rows = (dst_f, src_f)[k // 4]
                    mm = pe.matmul(m.bank(k, q), rows[:, j * P:(j + 1) * P], two[j % 2][:, (k % 4) * q:(k % 4 + 1) * q],
                                   start=(j == 0), stop=(j == ROWS - 1))
                mm.then_inc(drawn, 1)


def load_steps(engine, regs, table, first, most):
    engine.load(regs, table[0:1, ds(first, len(regs))])
    return [engine.snap(r, min_val=0, max_val=most) for r in regs]


def count_edges(nc, m, adj):
    with Phase(nc, "ce", "hot fetched begun lo_hot product moved added cleaned stored0 stored1 stored2 stored3") as (
            block, hot, fetched, begun, lo_hot, product, moved, added, cleaned, *stored):
        bank = lambda h, k: m.bank(h * HALF + k, WIDE)

        @block.gpsimd
        def _(pool):
            def fetch(j, r):
                pool.tensor_copy(m.lo_now[:, r, :], m.lo[:, ds(j * HALF, HALF)]).then_inc(fetched, 1)

            def half(j, r):
                wait(pool, lo_hot, (j - 2) * HALF)
                fetch(j + 1, (r + 1) % 4)
                pool.wait_ge(fetched, j + 1)
                wait(pool, product, (j - 3) * HALF)
                pool.sem_inc(begun, 1)
                for k in range(HALF):
                    pool.tensor_scalar(m.by_lo[:, r, k, :], m.count_to[:, 0:P], m.lo_now[:, r, k:k + 1], None,
                                       ALU.is_equal).then_inc(lo_hot, 1)

            fetch(0, 0)
            for r in range(4):
                half(r, r)
            with pool.Fori(1, WTURNS // 2) as i:
                for r in range(4):
                    half(4 * i + r, r)

        @block.vector
        def _(dve):
            regs = registers(nc, dve, "cedve", 4 * HALF)

            def one_hot(s, h, k):
                dve.tensor_scalar(m.by_place[:, h, k, :], m.count_to, m.place[:, ds(s, 1)], None,
                                  ALU.is_equal).then_inc(hot, 1)

            def half(j, h, at):
                wait(dve, product, j * HALF)
                for k in range(HALF):
                    s = j * HALF + k
                    one_hot(s + HALF, 1 - h, k)
                    if k % 2 == 0:
                        dve.wait_ge(moved, s + 2)
                    if k == 0:
                        wait(dve, cleaned, (j - 1) * HALF)
                    wait(dve, added, s)
                    to = m.slots[:, ds(at[k], WIDE)]
                    dve.tensor_tensor(to, to, m.counted[:, h, k, :], ALU.add).then_inc(added, 1)

            for k in range(HALF):
                one_hot(k, 0, k)
            at = load_steps(dve, regs, m.ring, 0, (RING - 1) * WIDE)
            for r in range(4):
                half(r, r % 2, at[r * HALF:])
            with dve.Fori(1, WTURNS // 2) as i:
                at = load_steps(dve, regs, m.ring, i * 4 * HALF, (RING - 1) * WIDE)
                for r in range(4):
                    half(4 * i + r, r % 2, at[r * HALF:])

        @block.tensor
        def _(pe):
            def half(j, r):
                for k in range(HALF):
                    s = j * HALF + k
                    pe.wait_ge(lo_hot, s + 1)
                    pe.wait_ge(hot, s + 1)
                    wait(pe, moved, s - UNROLL + 1)
                    pe.matmul(bank(r % 2, k), m.by_lo[:, r, k, :], m.by_place[:, r % 2, k, :], start=True, stop=True).then_inc(product, 1)

            for r in range(4):
                half(r, r)
            with pe.Fori(1, WTURNS // 2) as i:
                for r in range(4):
                    half(4 * i + r, r)

        @block.scalar
        def _(act):
            regs = registers(nc, act, "ceact", 4 * HALF)

            def half(j, h, at=None, whole=None, seen=None):
                if j is not None and not (isinstance(j, int) and j < 2):
                    act.wait_ge(added, (j - 1) * HALF)
                if whole is not None:
                    act.wait_ge(whole, seen)
                for k in range(HALF):
                    s = j * HALF + k
                    act.wait_ge(product, s + 1)
                    act.activation(m.counted[:, h, k, :], bank(h, k), ACT.Copy).then_inc(moved, 1)
                    if at is not None:
                        act.wait_ge(cleaned, s - HALF)
                        act.activation(m.slots_as_f32[:, ds(at[k], WIDE // 2)], m.zeros,
                                       ACT.Copy).then_inc(cleaned, 1)

            act.sem_inc(cleaned, HALF)
            half(0, 0)
            half(1, 1)
            at = load_steps(act, regs, m.clean, HALF, (RING - 1) * WIDE // 2)
            half(2, 0, at)
            half(3, 1, at[HALF:], stored[0], 32)
            with act.Fori(1, WTURNS // 2) as i:
                at = load_steps(act, regs, m.clean, i * 4 * HALF - HALF, (RING - 1) * WIDE // 2)
                for r in range(4):
                    half(4 * i + r, r % 2, at[r * HALF:], stored[(r + 1) % 4], 32 * (i + (r + 1) // 4))

        @block.sync
        def _(sp):
            regs = [sp.alloc_register(f"cesp{k}") for k in range(3 * HALF)]

            def half(j, r, first=False):
                sp.load(regs, m.stores[0:1, ds(j * 3 * HALF, 3 * HALF)])
                if not first:
                    sp.wait_ge(cleaned, (j - 2) * HALF + 1)
                for k in range(0, HALF, 2):
                    slot, to_block, to_part = (sp.snap(v, min_val=0, max_val=most) for v, most in
                                               zip(regs[3 * k:3 * k + 3], (RING * WIDE, (ADJ_BLOCKS - 1) * P, (SLOTS - 2) * WIDE)))
                    sp.wait_ge(added, j * HALF + k + 2)
                    sp.dma_start(adj[ds(to_block, P), ds(to_part, 2 * WIDE)],
                                 m.slots[:, ds(slot, 2 * WIDE)]).then_inc(stored[r], 16)

            for r in range(4):
                half(r, r, True)
            with sp.Fori(1, WTURNS // 2) as i:
                for r in range(4):
                    half(4 * i + r, r)
            for r in range(4):
                sp.wait_ge(stored[r], 32 * (WTURNS // 2))


def three_parts(then, dve, rows, rest, parts):
    then(dve.tensor_copy(parts[0], rows))
    then(dve.tensor_tensor(rest, rows, parts[0], ALU.subtract))
    then(dve.tensor_copy(parts[1], rest))
    then(dve.tensor_tensor(rest, rest, parts[1], ALU.subtract))
    then(dve.tensor_copy(parts[2], rest))


def first_parts(nc, m, table):
    with Phase(nc, "fp", "rows_in vec") as (block, rows_in, vec):
        rows = blocks(m.parts[1].bitcast(F32)[:, 0:BLOCKS * HID], HID)
        parts = m.parts[0][:, 0:BLOCKS * 3 * HID].rearrange("p (b t f) -> p b t f", t=3, f=HID)

        @block.sync
        def _(sp):
            sp.dma_start(rows, table.rearrange("(b p) f -> p b f", p=P)).then_inc(rows_in, 16)
            sp.wait_ge(rows_in, 16)

        @block.vector
        def _(dve):
            n = 0

            def then(op):
                nonlocal n
                n += 1
                op.then_inc(vec, 1)
                dve.wait_ge(vec, n)

            dve.wait_ge(rows_in, 16)
            three_parts(then, dve, rows, rows, [parts[:, :, t, :] for t in range(3)])


def dense(nc, m, tag, adj, kind, f, source, fn=None, target=None, weights=(), biases=(), check=False, out=None):
    halves = -(-f // D)
    fh = f // halves
    parts_in = m.parts[source]
    norm = kind in ("gcn", "gcn_rows", "gcn_end")
    end = kind in ("gcn_end", "gin_end")
    gin = kind in ("gin", "gin_end")
    turned_bank, hidden_bank, out_bank = m.bank(6, 2 * P), m.ps[:, 512 * 6 + 2 * P:512 * 7], m.bank(7, 2 * D)
    steps = {"gcn": 6, "gcn_rows": 7, "gcn_end": 10, "gin": 7, "gin_end": 4}[kind]
    with Phase(nc, tag, "loaded0 loaded1 loaded2 multiplied checked summed scaled turned copied hidden relued projected vec "
               "aggregating aggregated rooted placed stored emptied peaked spotted flagged") as (
            block, loaded0, loaded1, loaded2, multiplied, checked, summed, scaled, turned, copied, hidden, relued, projected,
            vec, aggregating, aggregated, rooted, placed, stored, emptied, peaked, spotted, flagged):
        loaded = (loaded0, loaded1, loaded2)
        turns = BLOCKS // 3
        assert BLOCKS == 3 * turns + 1

        def every_block(engine, do):
            for k in range(3):
                do(k, k, 0)
            with engine.Fori(1, turns) as i:
                for k in range(3):
                    do(3 * i + k, k, i)
            do(BLOCKS - 1, 0, turns)

        @block.sync
        def _(sp):
            def load(b, k, i):
                wait(sp, multiplied, b - 2)
                if check:
                    wait(sp, checked, b - 2)
                rows = adj[b * P:(b + 1) * P, :] if isinstance(b, int) else adj[ds(b * P, P), :]
                sp.dma_start(m.adj[k], rows).then_inc(loaded[k], 16)
                if kind == "gin_end":
                    store(b - 3)

            def store(b):
                if isinstance(b, int) and b < 0:
                    return
                sp.wait_ge(placed, b + 1)
                if isinstance(b, int):
                    n = min(P, NODES - b * P)
                    sp.dma_start(out[b * P:b * P + n, :], m.x[0:n, b * P:(b + 1) * P]).then_inc(stored, 16)
                else:
                    sp.dma_start(out[ds(b * P, P), :], m.x[:, ds(b * P, P)]).then_inc(stored, 16)

            every_block(sp, load)
            if kind == "gin_end":
                for b in range(BLOCKS - 3, BLOCKS):
                    store(b)
                sp.wait_ge(stored, 16 * BLOCKS)

        @block.tensor
        def _(pe):
            def turn(b):
                pe.wait_ge(scaled if norm else summed, b + 1)
                for h in range(halves):
                    mm = pe.transpose(turned_bank[0:fh, h * P:(h + 1) * P], m.y[:, h * fh:(h + 1) * fh], m.ident[:, :])
                mm.then_inc(turned, 1)

            def hide(b):
                pe.wait_ge(copied, b + 1)
                for o in range(2):
                    for h in range(halves):
                        mm = pe.matmul(hidden_bank[:, o * P:(o + 1) * P], weights[0][:, h, o * P:(o + 1) * P],
                                       m.yT[:, h * P:(h + 1) * P], start=(h == 0), stop=(h == halves - 1))
                mm.then_inc(hidden, 1)

            def project(b):
                if gin:
                    pe.wait_ge(relued, 2 * b + 2)
                    for o in range(2):
                        mm = pe.matmul(out_bank[:, 0:fn], m.hid[:, o * P:(o + 1) * P], weights[1][:, o, :],
                                       start=(o == 0), stop=(o == 1))
                else:
                    pe.wait_ge(relued, b + 1)
                    mm = pe.matmul(out_bank[:, 0:fn], m.hid[0:f, 0:P], weights[0][0:f, 0, :], start=True, stop=True)
                mm.then_inc(projected, 1)

            own = {8: turn, 16: hide, 26: project} if gin else {} if kind == "gcn_rows" else {10: turn, 24: project}

            def multiply(b, k, i):
                pe.wait_ge(loaded[k], 16 * i + 16)
                wait(pe, summed, b - 2)
                for s in range(BLOCKS):
                    if s in own and not (isinstance(b, int) and b == 0):
                        own[s](b - 1)
                    here = m.adj[k][:, s:P * BLOCKS:BLOCKS]
                    for h in range(halves):
                        pe.matmul(m.bank(k * halves + h, 3 * fh), here,
                                  parts_in[:, s * 3 * f + h * 3 * fh:s * 3 * f + (h + 1) * 3 * fh], start=(s == 0), stop=False)
                for h in range(halves):
                    mm = pe.matmul(m.bank(k * halves + h, 3 * fh), m.identb[:, :],
                                   parts_in[:, ds(b * (3 * f) + h * 3 * fh, 3 * fh)], start=False, stop=True)
                mm.then_inc(multiplied, 1)

            every_block(pe, multiply)
            for s in own:
                own[s](BLOCKS - 1)
            if check:
                pe.wait_ge(peaked, 2)
                pe.matmul(m.bank(6, 1), m.ones[:, :], m.y[:, 0:1], start=True, stop=True).then_inc(spotted, 1)

        @block.scalar
        def _(act):
            def between(b, k, i):
                if kind == "gcn":
                    act.wait_ge(turned, b + 1)
                    act.activation(m.hid[0:f, 0:P], turned_bank[0:f, 0:P], ACT.Relu, bias=biases[0][0:f, :]).then_inc(relued, 1)
                if kind == "gcn_end":
                    act.wait_ge(turned, b + 1)
                    act.activation(m.hid[0:f, 0:P], turned_bank[0:f, 0:P], ACT.Copy).then_inc(relued, 1)
                if gin:
                    act.wait_ge(turned, b + 1)
                    act.activation(m.yT[:, 0:f], turned_bank[:, 0:f], ACT.Copy).then_inc(copied, 1)
                    act.wait_ge(hidden, b + 1)
                    for o in range(2):
                        act.activation(m.hid[:, o * P:(o + 1) * P], hidden_bank[:, o * P:(o + 1) * P], ACT.Relu,
                                       bias=biases[0][:, o:o + 1]).then_inc(relued, 1)
                if end:
                    act.wait_ge(aggregated, b + 1)
                    act.activation(m.root, m.mean_var[:, 1:2], ACT.Sqrt, bias=m.eps[:, 0:1]).then_inc(rooted, 1)

            every_block(act, between)

        @block.vector
        def _(dve):
            def finish(b, k, i):
                n = b * steps

                def then(op):
                    nonlocal n
                    n = n + 1
                    op.then_inc(vec, 1)
                    dve.wait_ge(vec, n)

                if check:
                    dve.wait_ge(loaded[k], 16 * i + 16)
                    wait(dve, checked, b)
                    dve.tensor_tensor(m.most, m.most, m.adj[k], ALU.max).then_inc(checked, 1)
                dve.wait_ge(multiplied, b + 1)
                if halves == 1:
                    y = m.bank(k, 3 * f).rearrange("p (t f) -> p f t", t=3)
                    dve.tensor_reduce(m.y[:, 0:f], y, AX.X, ALU.add).then_inc(summed, 1)
                else:
                    y = m.ps[:, 1024 * k:1024 * (k + 1)].rearrange("p (h q) -> p h q", h=2)[:, :, 0:3 * fh]
                    dve.tensor_reduce(m.y.rearrange("p (h f) -> p h f", h=2), y.rearrange("p h (t f) -> p h f t", t=3),
                                      AX.X, ALU.add).then_inc(summed, 1)
                here = m.norm[:, ds(b, 1)]
                x = m.x[:, ds(b * P, P)]
                if norm:
                    dve.wait_ge(summed, b + 1)
                    dve.tensor_scalar(m.y[:, 0:f], m.y[:, 0:f], here, None, ALU.mult).then_inc(scaled, 1)
                if kind == "gcn":
                    dve.wait_ge(projected, b + 1)
                    then(dve.tensor_scalar(m.h[:, 0:fn], out_bank[:, 0:fn], here, None, ALU.mult))
                    rows = m.h[:, 0:fn]
                if kind == "gcn_rows":
                    dve.wait_ge(scaled, b + 1)
                    rows = m.h[:, 0:f]
                    then(dve.tensor_tensor(rows, m.y[:, 0:f], biases[0], ALU.add))
                    then(dve.tensor_scalar(rows, rows, 0.0, here, ALU.max, ALU.mult))
                if kind == "gcn_end":
                    dve.wait_ge(projected, b + 1)
                    then(dve.tensor_tensor(m.h[:, 0:D], out_bank[:, 0:D], biases[0], ALU.add))
                    then(dve.scalar_tensor_tensor(m.h[:, 0:D], m.h[:, 0:D], 0.0, x, ALU.max, ALU.add))
                if gin:
                    dve.wait_ge(projected, b + 1)
                    then(dve.tensor_tensor(m.h[:, 0:fn], out_bank[:, 0:fn], biases[1], ALU.add))
                    rows = m.h[:, 0:fn]
                    if kind == "gin":
                        then(dve.tensor_scalar(rows, rows, 0.0, None, ALU.max))
                    else:
                        then(dve.scalar_tensor_tensor(rows, rows, 0.0, x, ALU.max, ALU.add))
                if end:
                    then(dve.bn_stats(m.stats, m.h[:, 0:D]))
                    dve.sem_inc(aggregating, 1)
                    dve.bn_aggr(m.mean_var, m.stats).then_inc(aggregated, 1)
                    dve.wait_ge(rooted, b + 1)
                    then(dve.reciprocal(m.inverse, m.root))
                    last = dve.tensor_scalar(x, m.h[:, 0:D], m.mean_var[:, 0:1], m.inverse, ALU.subtract, ALU.mult)
                    if kind == "gin_end":
                        last.then_inc(placed, 1)
                        dve.wait_ge(placed, b + 1)
                    else:
                        then(last)
                    rows = x
                if target is not None:
                    fo = D if end else fn
                    ho = -(-fo // D)
                    to = m.parts[target][:, ds(b * (3 * fo), 3 * fo)].rearrange("p (h t f) -> p h t f", h=ho, t=3)
                    two = lambda a: a.rearrange("p (h f) -> p h f", h=ho)
                    three_parts(then, dve, two(rows), two(m.rest[:, 0:fo]), [to[:, :, t, :] for t in range(3)])

            if check:
                dve.memset(m.most, 0.0).then_inc(emptied, 1)
                dve.wait_ge(emptied, 1)
            every_block(dve, finish)
            if check:
                dve.wait_ge(checked, BLOCKS)
                dve.tensor_reduce(m.y[:, 0:1], m.most, AX.X, ALU.max).then_inc(peaked, 1)
                dve.wait_ge(peaked, 1)
                dve.tensor_scalar(m.y[:, 0:1], m.y[:, 0:1], float(EXACT), None, ALU.is_ge).then_inc(peaked, 1)
                dve.wait_ge(spotted, 1)
                dve.tensor_scalar(m.flag[:, :], m.bank(6, 1), 1.0, None, ALU.min).then_inc(flagged, 1)


def store_sums(block, m, table, f, placed, xed, stored, done):
    @block.sync
    def _(sp):
        with sp.Fori(0, GROUPS) as g:
            sp.wait_ge(placed, g + 1)
            if xed is not None:
                sp.wait_ge(xed, g + 1)
            sp.sem_inc(done, 1)
            sp.dma_start(group_rows(table, g), blocks(m.sums[:, ds(g * GN, GN)])[:, :, 0:f]).then_inc(stored, 16)
        sp.wait_ge(stored, 16 * GROUPS)


def gcn_step(nc, m, tag, weight, bias, f, table):
    with Phase(nc, tag, "scaled turned relued projected placed stored done") as (
            block, scaled, turned, relued, projected, placed, stored, done):

        @block.vector
        def _(dve):
            dve.sem_inc(done, 1)
            with dve.Fori(0, GROUPS) as g:
                s = blocks(m.sums[:, ds(g * GN, GN)])
                norm = m.norm[:, ds(g * GB, GB)]
                dve.wait_ge(done, g + 1)
                dve.tensor_tensor(blocks(m.stage_a[:, :])[:, :, 0:HID], s[:, :, 0:HID], copies(norm, 2, HID),
                                  ALU.mult).then_inc(scaled, 1)
                dve.wait_ge(projected, g + 1)
                dve.tensor_tensor(s[:, :, 0:f], blocks(m.ps[:, 1024:1024 + GN])[:, :, 0:f], copies(norm, 2, f),
                                  ALU.mult).then_inc(placed, 1)

        @block.tensor
        def _(pe):
            with pe.Fori(0, GROUPS) as g:
                pe.wait_ge(scaled, g + 1)
                turn_blocks(pe, m, 0, m.stage_a, HID).then_inc(turned, 1)
                pe.wait_ge(relued, g + 1)
                for b in range(GB):
                    mm = pe.matmul(m.ps[:, 1024 + b * P:1024 + b * P + f], m.stage_b[0:HID, b * P:(b + 1) * P],
                                   weight[0:HID, 0, :], start=True, stop=True)
                mm.then_inc(projected, 1)

        @block.scalar
        def _(act):
            with act.Fori(0, GROUPS) as g:
                act.wait_ge(turned, g + 1)
                act.activation(m.stage_b[0:HID, :], m.ps[0:HID, 0:GN], ACT.Relu, bias=bias[0:HID, :]).then_inc(relued, 1)

        store_sums(block, m, table, f, placed, None, stored, done)


def gcn_end(nc, m, table):
    with Phase(nc, "ge2", "vec stats summing rooted inverted lned xed placed stored done") as (
            block, vec, stats, summing, rooted, inverted, lned, xed, placed, stored, done):
        root = m.small[:, 330:330 + GB]
        steps = 3

        @block.vector
        def _(dve):
            dve.sem_inc(done, 1)
            with dve.Fori(0, GROUPS) as g:
                a, b = m.stage_a[:, :], m.stage_b[:, :]
                after = lambda n: dve.wait_ge(vec, g * steps + n)
                dve.wait_ge(done, g + 1)
                dve.tensor_tensor(blocks(a), blocks(m.sums[:, ds(g * GN, GN)]),
                                  copies(m.norm[:, ds(g * GB, GB)], 2, P), ALU.mult).then_inc(vec, 1)
                after(1)
                dve.tensor_tensor(blocks(a), blocks(a), copies(m.spread["c4"], 1, GB), ALU.add).then_inc(vec, 1)
                after(2)
                dve.scalar_tensor_tensor(b, a, 0.0, m.x[:, ds(g * GN, GN)], ALU.max, ALU.add).then_inc(vec, 1)
                after(3)
                normalize(dve, m, m.stage_b, m.stage_b, stats, summing, root, rooted, inverted, lned, g)
                dve.wait_ge(lned, g * GB + GB)
                dve.tensor_copy(m.gin_sums[:, ds(g * GN, GN)], b).then_inc(placed, 1)

        @block.scalar
        def _(act):
            with act.Fori(0, GROUPS) as g:
                take_roots(act, m, root, stats, rooted, g)
                act.wait_ge(lned, g * GB + GB)
                act.activation(m.x[:, ds(g * GN, GN)], m.stage_b[:, :], ACT.Copy).then_inc(xed, 1)

        @block.sync
        def _(sp):
            with sp.Fori(0, GROUPS) as g:
                sp.wait_ge(placed, g + 1)
                sp.wait_ge(xed, g + 1)
                sp.sem_inc(done, 1)
                sp.dma_start(group_rows(table, g), blocks(m.gin_sums[:, ds(g * GN, GN)])).then_inc(stored, 16)
            sp.wait_ge(stored, 16 * GROUPS)


def gin_step(nc, m, table):
    with Phase(nc, "gs3", "staged turned copied hidden relu0 relu1 projected biased placed stored done") as (
            block, staged, turned, copied, hidden, relu0, relu1, projected, biased, placed, stored, done):
        act0, act1 = m.stage_c[:, 0:GN], m.stage_c[:, GN:2 * GN]

        @block.scalar
        def _(act):
            act.sem_inc(done, 1)
            with act.Fori(0, GROUPS) as g:
                act.wait_ge(done, g + 1)
                act.activation(m.stage_a[:, :], m.gin_sums[:, ds(g * GN, GN)], ACT.Copy).then_inc(staged, 1)
                act.wait_ge(turned, g + 1)
                act.activation(m.stage_b[:, :], m.ps[:, 0:GN], ACT.Copy).then_inc(copied, 1)
                act.wait_ge(hidden, g * 2 + 1)
                act.activation(act0, m.ps[:, 1024:1024 + GN], ACT.Relu, bias=m.column["b1a"][:, 0:1]).then_inc(relu0, 1)

        @block.tensor
        def _(pe):
            pe.sem_inc(biased, 2)
            with pe.Fori(0, GROUPS) as g:
                pe.wait_ge(staged, g + 1)
                turn_blocks(pe, m, 0, m.stage_a).then_inc(turned, 1)
                pe.wait_ge(copied, g + 1)
                for o in range(2):
                    feature_product(pe, m, 2 + 2 * o, [(m.w["w1a"][:, 0, o * P:(o + 1) * P], m.stage_b)]).then_inc(hidden, 1)
                pe.wait_ge(relu0, g + 1)
                pe.wait_ge(relu1, g + 1)
                for b in range(GB):
                    out = gin_bank(m, b, 2 * D)
                    pe.wait_ge(biased, g * GB + b + 1)
                    pe.matmul(out, act0[:, b * P:(b + 1) * P], m.w["w1b"][:, 0, :], start=True, stop=False)
                    pe.matmul(out, act1[:, b * P:(b + 1) * P], m.w["w1b"][:, 1, :], start=False, stop=True).then_inc(projected, 1)

        @block.vector
        def _(dve):
            with dve.Fori(0, GROUPS) as g:
                s = m.sums[:, ds(g * 2 * GN, 2 * GN)]
                dve.wait_ge(hidden, g * 2 + 2)
                dve.tensor_scalar(act1, m.ps[:, 2048:2048 + GN], m.column["b1a"][:, 1:2], 0.0, ALU.add, ALU.max).then_inc(relu1, 1)
                for b in range(GB):
                    dve.wait_ge(projected, g * GB + b + 1)
                    dve.tensor_tensor(m.stage_d[:, b * 2 * D:(b + 1) * 2 * D], gin_bank(m, b, 2 * D), m.spread["b1b"],
                                      ALU.add).then_inc(biased, 1)
                dve.wait_ge(biased, g * GB + GB + 2)
                dve.tensor_scalar(s, m.stage_d, 0.0, None, ALU.max).then_inc(placed, 1)

        @block.sync
        def _(sp):
            with sp.Fori(0, GROUPS) as g:
                sp.wait_ge(placed, g + 1)
                sp.sem_inc(done, 1)
                sp.dma_start(group_rows(table, g), blocks(m.sums[:, ds(g * 2 * GN, 2 * GN)], 2 * D)).then_inc(stored, 16)
            sp.wait_ge(stored, 16 * GROUPS)


def gin_bank(m, b, n):
    return m.bank(6 + b % 2, n)


def gin_end(nc, m, out):
    with Phase(nc, "gf3", "staged turned copied0 copied1 hidden relu0 relu1 projected vec stats summing rooted inverted lned stored done") as (
            block, staged, turned, copied0, copied1, hidden, relu0, relu1, projected, vec, stats, summing, rooted, inverted,
            lned, stored, done):
        root = m.small[:, 330:330 + GB]
        steps = 2

        @block.scalar
        def _(act):
            act.sem_inc(done, 1)
            with act.Fori(0, GROUPS) as g:
                act.wait_ge(done, g + 1)
                act.activation(m.stage_c[:, :], m.sums[:, ds(g * 2 * GN, 2 * GN)], ACT.Copy).then_inc(staged, 1)
                act.wait_ge(turned, g * 2 + 1)
                act.activation(m.stage_d[:, 0:GN], m.ps[:, 0:GN], ACT.Copy).then_inc(copied0, 1)
                act.wait_ge(hidden, g * 2 + 1)
                act.activation(m.stage_a[:, :], m.ps[:, 2048:2048 + GN], ACT.Relu, bias=m.column["b2a"][:, 0:1]).then_inc(relu0, 1)
                take_roots(act, m, root, stats, rooted, g)

        @block.tensor
        def _(pe):
            with pe.Fori(0, GROUPS) as g:
                pe.wait_ge(staged, g + 1)
                for k in range(2):
                    for b in range(GB):
                        mm = pe.transpose(m.ps[:, 1024 * k + b * P:1024 * k + (b + 1) * P],
                                          m.stage_c[:, (2 * b + k) * P:(2 * b + k + 1) * P], m.ident[:, :])
                    mm.then_inc(turned, 1)
                pe.wait_ge(copied0, g + 1)
                pe.wait_ge(copied1, g + 1)
                for o in range(2):
                    feature_product(pe, m, 4 + 2 * o, [(m.w["w2a"][:, k, o * P:(o + 1) * P], m.stage_d[:, k * GN:(k + 1) * GN])
                                                       for k in range(2)]).then_inc(hidden, 1)
                pe.wait_ge(relu0, g + 1)
                pe.wait_ge(relu1, g + 1)
                for b in range(GB):
                    o = m.ps[:, b * P:(b + 1) * P]
                    pe.matmul(o, m.stage_a[:, b * P:(b + 1) * P], m.w["w2b"][:, 0, :], start=True, stop=False)
                    mm = pe.matmul(o, m.stage_b[:, b * P:(b + 1) * P], m.w["w2b"][:, 1, :], start=False, stop=True)
                mm.then_inc(projected, 1)

        @block.vector
        def _(dve):
            a, b = m.stage_a[:, :], m.stage_b[:, :]
            with dve.Fori(0, GROUPS) as g:
                dve.wait_ge(turned, g * 2 + 2)
                dve.tensor_copy(m.stage_d[:, GN:2 * GN], m.ps[:, 1024:1024 + GN]).then_inc(copied1, 1)
                dve.wait_ge(hidden, g * 2 + 2)
                dve.tensor_scalar(b, m.ps[:, 3072:3072 + GN], m.column["b2a"][:, 1:2], 0.0, ALU.add, ALU.max).then_inc(relu1, 1)
                dve.wait_ge(projected, g + 1)
                dve.tensor_tensor(blocks(a), blocks(m.ps[:, 0:GN]), copies(m.spread["b2b"], 1, GB), ALU.add).then_inc(vec, 1)
                dve.wait_ge(vec, g * steps + 1)
                dve.scalar_tensor_tensor(b, a, 0.0, m.x[:, ds(g * GN, GN)], ALU.max, ALU.add).then_inc(vec, 1)
                dve.wait_ge(vec, g * steps + 2)
                normalize(dve, m, m.stage_b, m.stage_c, stats, summing, root, rooted, inverted, lned, g)

        @block.sync
        def _(sp):
            with sp.Fori(0, GROUPS - 1) as g:
                sp.wait_ge(lned, g * GB + GB)
                sp.dma_start(group_rows(out, g), blocks(m.stage_c[:, 0:GN])).then_inc(stored, 16)
                sp.wait_ge(stored, g * 16 + 16)
                sp.sem_inc(done, 1)
            sp.wait_ge(lned, GROUPS * GB)
            first = (GROUPS - 1) * GN
            whole = (GB - 1) * P
            sp.dma_start(out[first:first + whole, :].rearrange("(b p) f -> p b f", p=P),
                         blocks(m.stage_c[:, 0:whole])).then_inc(stored, 16)
            sp.dma_start(out[first + whole:NODES, :], m.stage_c[0:LAST, whole:whole + P]).then_inc(stored, 16)
            sp.wait_ge(stored, 16 * (GROUPS + 1))


def restore(nc, m, x, sums):
    with Phase(nc, "re", "loaded") as (block, loaded):
        @block.sync
        def _(sp):
            sp.dma_start(blocks(m.x[:, :]), x.rearrange("(b p) f -> p b f", p=P)).then_inc(loaded, 16)
            sp.dma_start(blocks(m.sums[:, 0:BLOCKS * P])[:, :, 0:HID],
                         sums.rearrange("(b p) f -> p b f", p=P)).then_inc(loaded, 16)
            sp.wait_ge(loaded, 32)


def clear_sums(nc, m, n):
    with Phase(nc, "cs", "zeroed") as (block, zeroed):
        @block.vector
        def _(dve):
            dve.memset(m.sums[:, 0:n], 0.0).then_inc(zeroed, 1)


def program(nc, t, out):
    tables = {n: nc.dram_tensor(f"table_{n}", (BLOCKS * P, f), F32, kind="Internal").ap() for n, f in
              (("kv", 2 * D), ("kv1", 2 * D), ("h1", HID), ("h2", HID), ("h3", HID), ("h4", D), ("x", D), ("g", 2 * D), ("x1", D))}
    edge_values = nc.dram_tensor("edge_values", (2 * TURNS * P, HALF * D), F32, kind="Internal").ap()
    adj = nc.dram_tensor("adjacency", (ADJ_BLOCKS * P, SLOTS * WIDE), BF16, kind="Internal").ap()
    with ExitStack() as ctx:
        m = Memory(nc, ctx)
        plan(nc, m, t)
        project0(nc, m, t, tables["kv"])
        attend(nc, m, tables["kv"])
        attend_out(nc, m, t)
        feed_forward(nc, m)
        project1(nc, m, t, tables["kv1"])
        score(nc, m, tables["kv1"], edge_values)
        softmax_rows(nc, m)
        softmax_weights(nc, m)
        clear_sums(nc, m, BLOCKS * A1)
        sum_values(nc, m, edge_values)
        skip_gate(nc, m, tables["h1"])
        plan_windows(nc, m, t, tables["x1"])
        count_edges(nc, m, adj)
        first_parts(nc, m, tables["h1"])
        layer = lambda c, w: dict(fn=w.shape[2], weights=[w], biases=[c])
        dense(nc, m, "d1", adj, "gcn", HID, 0, target=1, **layer(m.column["c1"], m.w["g2"]))
        dense(nc, m, "d2", adj, "gcn", HID, 1, target=0, **layer(m.column["c2"], m.w["g3"]))
        dense(nc, m, "d3", adj, "gcn_rows", HID, 0, fn=HID, target=1, biases=[m.spread["c3"]])
        dense(nc, m, "d4", adj, "gcn_end", HID, 1, target=0, **layer(m.spread["c4"], m.w["g4"]))
        dense(nc, m, "d5", adj, "gin", D, 0, fn=2 * D, target=1, weights=[m.w["w1a"], m.w["w1b"]],
              biases=[m.column["b1a"], m.spread["b1b"]])
        dense(nc, m, "d6", adj, "gin_end", 2 * D, 1, fn=D, weights=[m.w["w2a"], m.w["w2b"]],
              biases=[m.column["b2a"], m.spread["b2b"]], check=True, out=out)
        Phase.flag = m.flag
        plan(nc, m, t, again=True)
        restore(nc, m, tables["x1"], tables["h1"])
        sum_rows(nc, m, "s1", tables["h1"], HID, m.sums, D)
        gcn_step(nc, m, "n1", m.w["g2"], m.column["c1"], HID, tables["h2"])
        sum_rows(nc, m, "s2", tables["h2"], HID, m.sums, D)
        gcn_step(nc, m, "n2", m.w["g3"], m.column["c2"], HID, tables["h3"])
        sum_rows(nc, m, "s3", tables["h3"], HID, m.sums, D)
        gcn_step(nc, m, "n3", m.w["g4"], m.column["c3"], D, tables["h4"])
        sum_rows(nc, m, "s4", tables["h4"], D, m.sums, D)
        gcn_end(nc, m, tables["x"])
        sum_rows(nc, m, "s5", tables["x"], D, m.gin_sums, D)
        gin_step(nc, m, tables["g"])
        sum_rows(nc, m, "s6", tables["g"], 2 * D, m.sums, 2 * D)
        gin_end(nc, m, out)
        Phase.flag = None


def kernel(**inputs):
    import numpy as np
    from concourse import bacc
    from concourse.bass_utils import run_bass_kernel_spmd

    i = {k: np.asarray(v) for k, v in inputs.items()}

    def padded(a, rows, fill):
        out = np.full((rows, *a.shape[1:]), fill, a.dtype)
        out[:a.shape[0]] = a
        return out

    x = padded(i["x"], BLOCKS * P, 0)
    g0, g1, g2, g3 = ({k[7:]: v for k, v in i.items() if k.startswith(f"L{n}_gnn_")} for n in range(4))
    columns = {"bo": g0["bo"], "b1": g0["b1"], "b2": g0["b2"], "n1w": g0["bn1_w"], "n1b": g0["bn1_b"],
               "n2w": g0["bn2_w"], "n2b": g0["bn2_b"], "c1": g2["b1"], "c2": g2["b2"], "c3": g2["b3"],
               "b1a": g3["b1a"], "b2a": g3["b2a"]}
    spread = {"bqkvs": np.concatenate([g1["bq"], g1["bk"], g1["bv"], g1["bskip"]]),
              "wbeta": g1["Wbeta"].reshape(-1), "c3": g2["b3"], "c4": g2["b4"], "b1b": g3["b1b"], "b2b": g3["b2b"]}
    arrays = {
        "x": x, "xT": x.T,
        "src": padded(i["src"], COLS * P, 0).reshape(COLS, P),
        "dst": padded(i["dst"], COLS * P, NO_DST).reshape(COLS, P),
        "wqkv0": np.concatenate([g0["Wq"].T, g0["Wk"].T, g0["Wv"].T], axis=1),
        "wo": g0["Wo"].T, "w1": g0["W1"].T, "w2": g0["W2"].T,
        "wqkvs": np.concatenate([g1["Wq"], g1["Wk"], g1["Wv"], g1["Wskip"]], axis=1),
        "g1": g2["W1"], "g2": g2["W2"], "g3": g2["W3"], "g4": g2["W4"],
        "w1a": g3["W1a"], "w1b": g3["W1b"], "w2a": g3["W2a"], "w2b": g3["W2b"],
        "columns": np.concatenate([padded(columns[n], k * P, 0).reshape(k, P) for n, k in COLUMNS]).T,
        "spread": np.concatenate([spread[n] for n, _ in SPREAD]).reshape(1, -1),
    }
    arrays = {k: np.ascontiguousarray(v) for k, v in arrays.items()}
    nc = bacc.Bacc("TRN2", target_bir_lowering=False, num_devices=1)
    tensors = {k: nc.dram_tensor(f"in_{k}", v.shape, mybir.dt.from_np(v.dtype), kind="ExternalInput").ap()
               for k, v in arrays.items()}
    out = nc.dram_tensor("out", (NODES, D), F32, kind="ExternalOutput").ap()
    program(nc, tensors, out)
    result = run_bass_kernel_spmd(nc, [{f"in_{k}": v for k, v in arrays.items()}], core_ids=[0])
    return result.results[0]["out"]
```
